# Optimizing a Trainium2 kernel written in Bass

```python
import numpy as np
import jax
import jax.numpy as jnp

def _softmax(x, axis=-1):
    return jax.nn.softmax(x, axis=axis)

def _gelu(x):
    return jax.nn.gelu(x, approximate=True)

def _silu(x):
    return jax.nn.silu(x)

def _sigmoid(x):
    return jax.nn.sigmoid(x)

def _layernorm(x, axis=-1, eps=1e-05):
    m = jnp.mean(x, axis=axis, keepdims=True)
    v = jnp.var(x, axis=axis, keepdims=True)
    return (x - m) / jnp.sqrt(v + eps)

def _scatter_add(tgt, idx, src, axis=0):
    return tgt.at[idx].add(src)

def _segment_sum(src, seg, n):
    return jax.ops.segment_sum(src, seg, n)
kernel_name = 'mk_decoder_postln_d2_seqx_r8_b56c59'

def setup_inputs(seed: int=0):
    np.random.seed(seed)
    _w = jnp.asarray

    def _rec_inputs():
        import jax
        import jax.numpy as jnp
        _rk = jax.random.key(seed)
        x = 7.22e-05 + 1 * jax.random.normal(jax.random.fold_in(_rk, 1), (16, 64, 128), jnp.float32)
        _lenS = 64 - jax.random.randint(jax.random.fold_in(_rk, 7), (16,), 0, max(1, 64 // 4) + 1, jnp.int32)
        _lenS2 = 64 - jax.random.randint(jax.random.fold_in(_rk, 8), (16,), 0, max(1, 64 // 4) + 1, jnp.int32)
        _ctx_1024P = jax.random.normal(jax.random.fold_in(_rk, 11), (16, 16, 128), jnp.float32)
        _ctx_1024c = jax.random.dirichlet(jax.random.fold_in(_rk, 511), 0.3 * jnp.ones((16,), jnp.float32), (16, 64))
        _ctx_1024t = jnp.einsum('bsk,bkd->bsd', _ctx_1024c, _ctx_1024P)
        _ctx_1024t = _ctx_1024t * jax.lax.rsqrt(jnp.mean(jnp.square(_ctx_1024t)) + 1e-12) * 0.953939
        ctx_1024 = 4.13588e-05 + 0.999923 * (_ctx_1024t + 0.3 * jax.random.normal(jax.random.fold_in(_rk, 611), (16, 64, 128), jnp.float32))
        _validS = jnp.arange(64)[None, :] < _lenS[:, None]
        _validS2 = jnp.arange(64)[None, :] < _lenS2[:, None]
        _causal = jnp.tril(jnp.ones((64, 64), dtype=bool))
        mask_Bx1x1xS2_ik0 = jnp.where(jnp.broadcast_to(_validS2[:, None, None, :], (16, 1, 1, 64)), 0, 1).astype(jnp.int32)
        return (x, ctx_1024, mask_Bx1x1xS2_ik0)
    x, ctx_1024, mask_Bx1x1xS2_ik0 = _rec_inputs()

    def _L0_attn_setup():
        import jax, jax.numpy as jnp
        import numpy as np
        import math
        N_HEAD = 16

        def _rope_cos_sin(T, head_dim):
            j = jnp.arange(head_dim // 2, dtype=jnp.float32)
            theta = jnp.power(10000.0, -2.0 * j / head_dim)
            t = jnp.arange(T, dtype=jnp.float32)
            ang = t[:, None] * theta[None, :]
            return (jnp.cos(ang), jnp.sin(ang))

        def _apply_rope(u, cos, sin):
            B, H, T, d = u.shape
            u = u.reshape(B, H, T, d // 2, 2)
            u0, u1 = (u[..., 0], u[..., 1])
            r0 = u0 * cos - u1 * sin
            r1 = u0 * sin + u1 * cos
            return jnp.stack([r0, r1], axis=-1).reshape(B, H, T, d)
        key = jax.random.key(seed)
        ks = jax.random.split(key, 9)
        C = 128
        s = 1.0 / math.sqrt(C)
        return {'x': jax.random.normal(ks[0], (4, 256, C), dtype=jnp.float32), 'wq': jax.random.normal(ks[1], (C, C), dtype=jnp.float32) * s, 'bq': jax.random.normal(ks[2], (C,), dtype=jnp.float32) * s, 'wk': jax.random.normal(ks[3], (C, C), dtype=jnp.float32) * s, 'bk': jax.random.normal(ks[4], (C,), dtype=jnp.float32) * s, 'wv': jax.random.normal(ks[5], (C, C), dtype=jnp.float32) * s, 'bv': jax.random.normal(ks[6], (C,), dtype=jnp.float32) * s, 'wp': jax.random.normal(ks[7], (C, C), dtype=jnp.float32) * s, 'bp': jax.random.normal(ks[8], (C,), dtype=jnp.float32) * s}
    _L0_attn_all = _L0_attn_setup()
    _L0_attn_in = {k: v for k, v in _L0_attn_all.items() if k in ('wq', 'bq', 'wk', 'bk', 'wv', 'bv', 'wp', 'bp')}
    del _L0_attn_all

    def _L0_xattn_setup():
        import jax, jax.numpy as jnp
        import numpy as np
        BS, SEQ, D_MODEL, N_HEADS = (4, 256, 128, 16)
        D_HEAD = D_MODEL // N_HEADS

        def _split_heads(x):
            b, s, _ = x.shape
            return x.reshape(b, s, N_HEADS, D_HEAD).transpose(0, 2, 1, 3)
        key = jax.random.key(seed)
        ks = jax.random.split(key, 12)
        s = 1.0 / np.sqrt(D_MODEL)
        return {'Q': jax.random.normal(ks[0], (BS, SEQ, D_MODEL), jnp.float32), 'K': jax.random.normal(ks[1], (BS, SEQ, D_MODEL), jnp.float32), 'V': jax.random.normal(ks[2], (BS, SEQ, D_MODEL), jnp.float32), 'mask': jax.random.randint(ks[3], (BS, 1, 1, SEQ), 0, 2, jnp.int32), 'Wq': jax.random.normal(ks[4], (D_MODEL, D_MODEL), jnp.float32) * s, 'bq': jnp.zeros((D_MODEL,), jnp.float32), 'Wk': jax.random.normal(ks[5], (D_MODEL, D_MODEL), jnp.float32) * s, 'bk': jnp.zeros((D_MODEL,), jnp.float32), 'Wv': jax.random.normal(ks[6], (D_MODEL, D_MODEL), jnp.float32) * s, 'bv': jnp.zeros((D_MODEL,), jnp.float32), 'Wo': jax.random.normal(ks[7], (D_MODEL, D_MODEL), jnp.float32) * s, 'bo': jnp.zeros((D_MODEL,), jnp.float32)}
    _L0_xattn_all = _L0_xattn_setup()
    _L0_xattn_in = {k: v for k, v in _L0_xattn_all.items() if k in ('Wq', 'bq', 'Wk', 'bk', 'Wv', 'bv', 'Wo', 'bo')}
    del _L0_xattn_all

    def _L0_ffn_setup():
        import jax, jax.numpy as jnp
        import numpy as np
        B, S, H = (2, 256, 128)
        E, I, K = (8, 512, 2)

        def _moe_forward(x, gate_w, wg, wu, wd):
            b, s, h = x.shape
            x_flat = x.reshape(-1, h)
            logits = x_flat @ gate_w.T
            top_v, top_i = jax.lax.top_k(logits, K)
            probs = jax.nn.softmax(top_v.astype(jnp.float32), axis=-1).astype(logits.dtype)
            one_hot = jax.nn.one_hot(top_i, E, dtype=probs.dtype)
            combine = jnp.einsum('tk,tke->et', probs, one_hot)

            def body(acc, ws):
                wge, wue, wde, we = ws
                hidden = jax.nn.silu(x_flat @ wge.T) * (x_flat @ wue.T)
                return (acc + we[:, None] * (hidden @ wde.T), None)
            out, _ = jax.lax.scan(body, jnp.zeros_like(x_flat), (wg, wu, wd, combine))
            return out.reshape(b, s, h)
        key = jax.random.key(seed)
        ks = jax.random.split(key, 5)
        scale_h = 1.0 / np.sqrt(H)
        scale_i = 1.0 / np.sqrt(I)
        x = jax.random.normal(ks[0], (B, S, H), dtype=jnp.float32)
        gate_w = jax.random.normal(ks[1], (E, H), dtype=jnp.float32) * scale_h
        wg = jax.random.normal(ks[2], (E, I, H), dtype=jnp.float32) * scale_h
        wu = jax.random.normal(ks[3], (E, I, H), dtype=jnp.float32) * scale_h
        wd = jax.random.normal(ks[4], (E, H, I), dtype=jnp.float32) * scale_i
        return {'x': x, 'gate_w': gate_w, 'wg': wg, 'wu': wu, 'wd': wd}
    _L0_ffn_all = _L0_ffn_setup()
    _L0_ffn_in = {k: v for k, v in _L0_ffn_all.items() if k in ('gate_w', 'wg', 'wu', 'wd')}
    del _L0_ffn_all

    def _L1_attn_setup():
        import jax, jax.numpy as jnp
        import numpy as np
        D_MODEL, D_QKV, N_HEADS = (128, 64, 16)
        key = jax.random.key(seed)
        k_x, k_qkv, k_out = jax.random.split(key, 3)
        X = jax.random.normal(k_x, (2, 256, D_MODEL), dtype=jnp.float32)
        W_qkv = jax.random.normal(k_qkv, (D_MODEL, 3 * D_QKV * N_HEADS), dtype=jnp.float32) * D_MODEL ** (-0.5)
        W_out = jax.random.normal(k_out, (D_QKV * N_HEADS, D_MODEL), dtype=jnp.float32) * (D_QKV * N_HEADS) ** (-0.5)
        return {'X': X, 'W_qkv': W_qkv, 'W_out': W_out}
    _L1_attn_all = _L1_attn_setup()
    _L1_attn_in = {k: v for k, v in _L1_attn_all.items() if k in ('W_qkv', 'W_out')}
    del _L1_attn_all

    def _L1_xattn_setup():
        import jax, jax.numpy as jnp
        import numpy as np
        D_MODEL = 128
        NHEADS = 16
        D_K = D_MODEL // NHEADS
        B, S = (4, 256)
        NEG = -1000000000000.0
        key = jax.random.key(seed)
        ks = jax.random.split(key, 8)
        scale = 1.0 / np.sqrt(D_MODEL)
        return {'query': jax.random.normal(ks[0], (B, S, D_MODEL), jnp.float32), 'key': jax.random.normal(ks[1], (B, S, D_MODEL), jnp.float32), 'value': jax.random.normal(ks[2], (B, S, D_MODEL), jnp.float32), 'mask': jax.random.randint(ks[3], (B, 1, 1, S), 0, 2, jnp.int32), 'Wq': jax.random.normal(ks[4], (D_MODEL, D_MODEL), jnp.float32) * scale, 'Wk': jax.random.normal(ks[5], (D_MODEL, D_MODEL), jnp.float32) * scale, 'Wv': jax.random.normal(ks[6], (D_MODEL, D_MODEL), jnp.float32) * scale, 'Wo': jax.random.normal(ks[7], (D_MODEL, D_MODEL), jnp.float32) * scale}
    _L1_xattn_all = _L1_xattn_setup()
    _L1_xattn_in = {k: v for k, v in _L1_xattn_all.items() if k in ('Wq', 'Wk', 'Wv', 'Wo')}
    del _L1_xattn_all

    def _L1_ffn_setup():
        import jax, jax.numpy as jnp
        import numpy as np
        EPS = 1e-06
        LN_EPS = 1e-05

        def _absmean_core(W):
            gamma = jnp.mean(jnp.abs(W)) + EPS
            Ws = W / gamma
            Wq = jnp.sign(Ws) * jnp.minimum(jnp.round(jnp.abs(Ws)), 1.0)
            return (Wq, gamma)

        @jax.custom_vjp
        def absmean(W):
            return _absmean_core(W)[0]

        def _absmean_fwd(W):
            Wq, gamma = _absmean_core(W)
            return (Wq, gamma)

        def _absmean_bwd(gamma, g):
            return (g / gamma,)
        absmean.defvjp(_absmean_fwd, _absmean_bwd)

        def layernorm(x, w, b, eps=LN_EPS):
            mu = jnp.mean(x, axis=-1, keepdims=True)
            var = jnp.mean((x - mu) ** 2, axis=-1, keepdims=True)
            return (x - mu) * jax.lax.rsqrt(var + eps) * w + b
        key = jax.random.key(seed)
        k1, k2, k3 = jax.random.split(key, 3)
        d, h = (128, 512)
        B, T = (8, 256)
        return {'x': jax.random.normal(k1, (B, T, d), jnp.float32), 'W_fc': jax.random.normal(k2, (h, d), jnp.float32), 'ln_w': jnp.ones((h,), jnp.float32), 'ln_b': jnp.zeros((h,), jnp.float32), 'W_proj': jax.random.normal(k3, (d, h), jnp.float32)}
    _L1_ffn_all = _L1_ffn_setup()
    _L1_ffn_in = {k: v for k, v in _L1_ffn_all.items() if k in ('W_fc', 'ln_w', 'ln_b', 'W_proj')}
    del _L1_ffn_all
    return {'x': x, 'ctx_1024': ctx_1024, 'mask_Bx1x1xS2_ik0': mask_Bx1x1xS2_ik0, 'L0_attn_wq': _L0_attn_in['wq'], 'L0_attn_bq': _L0_attn_in['bq'], 'L0_attn_wk': _L0_attn_in['wk'], 'L0_attn_bk': _L0_attn_in['bk'], 'L0_attn_wv': _L0_attn_in['wv'], 'L0_attn_bv': _L0_attn_in['bv'], 'L0_attn_wp': _L0_attn_in['wp'], 'L0_attn_bp': _L0_attn_in['bp'], 'L0_xattn_Wq': _L0_xattn_in['Wq'], 'L0_xattn_bq': _L0_xattn_in['bq'], 'L0_xattn_Wk': _L0_xattn_in['Wk'], 'L0_xattn_bk': _L0_xattn_in['bk'], 'L0_xattn_Wv': _L0_xattn_in['Wv'], 'L0_xattn_bv': _L0_xattn_in['bv'], 'L0_xattn_Wo': _L0_xattn_in['Wo'], 'L0_xattn_bo': _L0_xattn_in['bo'], 'L0_ffn_gate_w': _L0_ffn_in['gate_w'], 'L0_ffn_wg': _L0_ffn_in['wg'], 'L0_ffn_wu': _L0_ffn_in['wu'], 'L0_ffn_wd': _L0_ffn_in['wd'], 'L1_attn_W_qkv': _L1_attn_in['W_qkv'], 'L1_attn_W_out': _L1_attn_in['W_out'], 'L1_xattn_Wq': _L1_xattn_in['Wq'], 'L1_xattn_Wk': _L1_xattn_in['Wk'], 'L1_xattn_Wv': _L1_xattn_in['Wv'], 'L1_xattn_Wo': _L1_xattn_in['Wo'], 'L1_ffn_W_fc': _L1_ffn_in['W_fc'], 'L1_ffn_ln_w': _L1_ffn_in['ln_w'], 'L1_ffn_ln_b': _L1_ffn_in['ln_b'], 'L1_ffn_W_proj': _L1_ffn_in['W_proj']}

def reference(x, ctx_1024, mask_Bx1x1xS2_ik0, L0_attn_wq, L0_attn_bq, L0_attn_wk, L0_attn_bk, L0_attn_wv, L0_attn_bv, L0_attn_wp, L0_attn_bp, L0_xattn_Wq, L0_xattn_bq, L0_xattn_Wk, L0_xattn_bk, L0_xattn_Wv, L0_xattn_bv, L0_xattn_Wo, L0_xattn_bo, L0_ffn_gate_w, L0_ffn_wg, L0_ffn_wu, L0_ffn_wd, L1_attn_W_qkv, L1_attn_W_out, L1_xattn_Wq, L1_xattn_Wk, L1_xattn_Wv, L1_xattn_Wo, L1_ffn_W_fc, L1_ffn_ln_w, L1_ffn_ln_b, L1_ffn_W_proj):
    import jax
    import jax.numpy as jnp

    def _L0_attn_ref(x, wq, bq, wk, bk, wv, bv, wp, bp):
        import jax, jax.numpy as jnp
        import numpy as np
        import math
        N_HEAD = 16

        def _rope_cos_sin(T, head_dim):
            j = jnp.arange(head_dim // 2, dtype=jnp.float32)
            theta = jnp.power(10000.0, -2.0 * j / head_dim)
            t = jnp.arange(T, dtype=jnp.float32)
            ang = t[:, None] * theta[None, :]
            return (jnp.cos(ang), jnp.sin(ang))

        def _apply_rope(u, cos, sin):
            B, H, T, d = u.shape
            u = u.reshape(B, H, T, d // 2, 2)
            u0, u1 = (u[..., 0], u[..., 1])
            r0 = u0 * cos - u1 * sin
            r1 = u0 * sin + u1 * cos
            return jnp.stack([r0, r1], axis=-1).reshape(B, H, T, d)
        B, T, C = x.shape
        H = N_HEAD
        d = C // H

        def proj(w, b):
            return (jnp.einsum('btc,oc->bto', x, w) + b).reshape(B, T, H, d).transpose(0, 2, 1, 3)
        q, k, v = (proj(wq, bq), proj(wk, bk), proj(wv, bv))
        cos, sin = _rope_cos_sin(T, d)
        q = _apply_rope(q, cos, sin)
        k = _apply_rope(k, cos, sin)
        att = jnp.einsum('bhqd,bhkd->bhqk', q, k) * (1.0 / math.sqrt(d))
        causal = jnp.tril(jnp.ones((T, T), dtype=bool))
        att = jnp.where(causal, att, jnp.finfo(att.dtype).min)
        att = jax.nn.softmax(att, axis=-1)
        y = jnp.einsum('bhqk,bhkd->bhqd', att, v)
        y = y.transpose(0, 2, 1, 3).reshape(B, T, C)
        return jnp.einsum('btc,oc->bto', y, wp) + bp

    def _L0_xattn_ref(Q, K, V, mask, Wq, bq, Wk, bk, Wv, bv, Wo, bo):
        import jax, jax.numpy as jnp
        import numpy as np
        BS, SEQ, D_MODEL, N_HEADS = (4, 256, 128, 16)
        D_HEAD = D_MODEL // N_HEADS

        def _split_heads(x):
            b, s, _ = x.shape
            return x.reshape(b, s, N_HEADS, D_HEAD).transpose(0, 2, 1, 3)
        q = _split_heads(Q @ Wq.T + bq)
        k = _split_heads(K @ Wk.T + bk)
        v = _split_heads(V @ Wv.T + bv)
        scores = jnp.einsum('bhqd,bhkd->bhqk', q, k) / np.sqrt(D_HEAD).astype(np.float32)
        scores = jnp.where(mask == 0, jnp.float32(-1000000000.0), scores)
        attn = jax.nn.softmax(scores, axis=-1)
        ctx = jnp.einsum('bhqk,bhkd->bhqd', attn, v)
        b, h, s, d = ctx.shape
        ctx = ctx.transpose(0, 2, 1, 3).reshape(b, s, h * d)
        return ctx @ Wo.T + bo

    def _L0_ffn_ref(x, gate_w, wg, wu, wd):
        import jax, jax.numpy as jnp
        import numpy as np
        B, S, H = (2, 256, 128)
        E, I, K = (8, 512, 2)

        def _moe_forward(x, gate_w, wg, wu, wd):
            b, s, h = x.shape
            x_flat = x.reshape(-1, h)
            logits = x_flat @ gate_w.T
            top_v, top_i = jax.lax.top_k(logits, K)
            probs = jax.nn.softmax(top_v.astype(jnp.float32), axis=-1).astype(logits.dtype)
            one_hot = jax.nn.one_hot(top_i, E, dtype=probs.dtype)
            combine = jnp.einsum('tk,tke->et', probs, one_hot)

            def body(acc, ws):
                wge, wue, wde, we = ws
                hidden = jax.nn.silu(x_flat @ wge.T) * (x_flat @ wue.T)
                return (acc + we[:, None] * (hidden @ wde.T), None)
            out, _ = jax.lax.scan(body, jnp.zeros_like(x_flat), (wg, wu, wd, combine))
            return out.reshape(b, s, h)
        return _moe_forward(x, gate_w, wg, wu, wd)

    def _L1_attn_ref(X, W_qkv, W_out):
        import jax, jax.numpy as jnp
        import numpy as np
        D_MODEL, D_QKV, N_HEADS = (128, 64, 16)
        b, s, _ = X.shape
        h, d = (N_HEADS, D_QKV)
        scale = d ** 0.5
        qkv = X @ W_qkv
        qkv = qkv.reshape(b, s, h, d, 3)
        q, k, v = (qkv[..., 0], qkv[..., 1], qkv[..., 2])
        scores = jnp.einsum('bqhd,bkhd->bhqk', q, k) / scale
        weights = jax.nn.softmax(scores, axis=-1)
        attn = jnp.einsum('bhqk,bkhd->bqhd', weights, v)
        return attn.reshape(b, s, h * d) @ W_out

    def _L1_xattn_ref(query, key, value, mask, Wq, Wk, Wv, Wo):
        import jax, jax.numpy as jnp
        import numpy as np
        D_MODEL = 128
        NHEADS = 16
        D_K = D_MODEL // NHEADS
        B, S = (4, 256)
        NEG = -1000000000000.0
        b = query.shape[0]

        def split_heads(x, W):
            y = jnp.einsum('bsd,ed->bse', x, W)
            return y.reshape(b, -1, NHEADS, D_K).transpose(0, 2, 1, 3)
        q = split_heads(query, Wq)
        k = split_heads(key, Wk)
        v = split_heads(value, Wv)
        scores = jnp.einsum('bhqd,bhkd->bhqk', q, k) / jnp.sqrt(jnp.float32(D_K))
        scores = jnp.where(mask == 0, jnp.float32(NEG), scores)
        weights = jax.nn.softmax(scores, axis=-1)
        out = jnp.einsum('bhqk,bhkd->bhqd', weights, v)
        out = out.transpose(0, 2, 1, 3).reshape(b, -1, D_MODEL)
        out = jnp.einsum('bsd,ed->bse', out, Wo)
        return out

    def _L1_ffn_ref(x, W_fc, ln_w, ln_b, W_proj):
        import jax, jax.numpy as jnp
        import numpy as np
        EPS = 1e-06
        LN_EPS = 1e-05

        def _absmean_core(W):
            gamma = jnp.mean(jnp.abs(W)) + EPS
            Ws = W / gamma
            Wq = jnp.sign(Ws) * jnp.minimum(jnp.round(jnp.abs(Ws)), 1.0)
            return (Wq, gamma)

        @jax.custom_vjp
        def absmean(W):
            return _absmean_core(W)[0]

        def _absmean_fwd(W):
            Wq, gamma = _absmean_core(W)
            return (Wq, gamma)

        def _absmean_bwd(gamma, g):
            return (g / gamma,)
        absmean.defvjp(_absmean_fwd, _absmean_bwd)

        def layernorm(x, w, b, eps=LN_EPS):
            mu = jnp.mean(x, axis=-1, keepdims=True)
            var = jnp.mean((x - mu) ** 2, axis=-1, keepdims=True)
            return (x - mu) * jax.lax.rsqrt(var + eps) * w + b
        h = jnp.einsum('btd,hd->bth', x, absmean(W_fc))
        h = jax.nn.gelu(h, approximate=False)
        h = layernorm(h, ln_w, ln_b)
        return jnp.einsum('bth,dh->btd', h, absmean(W_proj))
    x = _layernorm(x + _L0_attn_ref(x, L0_attn_wq, L0_attn_bq, L0_attn_wk, L0_attn_bk, L0_attn_wv, L0_attn_bv, L0_attn_wp, L0_attn_bp), axis=-1)
    x = _layernorm(x + _L0_xattn_ref(x, ctx_1024, ctx_1024, mask_Bx1x1xS2_ik0, L0_xattn_Wq, L0_xattn_bq, L0_xattn_Wk, L0_xattn_bk, L0_xattn_Wv, L0_xattn_bv, L0_xattn_Wo, L0_xattn_bo), axis=-1)
    x = _layernorm(x + _L0_ffn_ref(x, L0_ffn_gate_w, L0_ffn_wg, L0_ffn_wu, L0_ffn_wd), axis=-1)
    x = _layernorm(x + _L1_attn_ref(x, L1_attn_W_qkv, L1_attn_W_out), axis=-1)
    x = _layernorm(x + _L1_xattn_ref(x, ctx_1024, ctx_1024, mask_Bx1x1xS2_ik0, L1_xattn_Wq, L1_xattn_Wk, L1_xattn_Wv, L1_xattn_Wo), axis=-1)
    x = _layernorm(x + _L1_ffn_ref(x, L1_ffn_W_fc, L1_ffn_ln_w, L1_ffn_ln_b, L1_ffn_W_proj), axis=-1)
    return x

_drawn_inputs = setup_inputs


def setup_inputs(seed=0):
    import zlib

    import numpy as np

    out = dict(_drawn_inputs(seed))
    spreads = {'L0_xattn_bq': (0.0, 0.1),
     'L0_xattn_bk': (0.0, 0.1),
     'L0_xattn_bv': (0.0, 0.1),
     'L0_xattn_bo': (0.0, 0.1),
     'L1_ffn_ln_w': (1.0, 0.2),
     'L1_ffn_ln_b': (0.0, 0.1)}
    factors = {}
    for name, (base, spread) in spreads.items():
        noise = np.random.default_rng([zlib.crc32(name.encode()), seed]).standard_normal(out[name].shape)
        drawn = base * np.exp(spread * noise) if base else spread * noise
        out[name] = jnp.asarray(drawn.astype(out[name].dtype))
    for name, factor in factors.items():
        out[name] = (out[name] * factor).astype(out[name].dtype)
    return out
```

```python
from contextlib import ExitStack

import numpy as np

import concourse.bass as bass
from concourse import mybir

F32 = mybir.dt.float32
BF16 = mybir.dt.bfloat16
I32 = mybir.dt.int32
U32 = mybir.dt.uint32
ALU = mybir.AluOpType
ACT = mybir.ActivationFunctionType
AX = mybir.AxisListType

P = 128
BATCH, SEQ = 16, 64
NT = BATCH * SEQ // P
HEADS = 16
DH = 8
DW = 64
PAIRS = HEADS // 2
EXPERTS, INNER = 8, 512
CH = INNER // P
BANK = 512
LN_EPS = 1e-5

C_ID, C_COS, C_SIN, C_HEAD, C_CAUSAL, C_IOTA, C_FILL0, C_FILL1, C_ONES, C_HALF, C_END = (
    0, 128, 192, 256, 264, 328, 336, 464, 592, 720, 722)
CAUSAL_FILL = -(2.0 ** 100)


def bf16_parts(value):
    parts, rest = [], np.float32(value)
    for _ in range(3):
        bits = np.array(rest, np.float32).view(np.uint32)
        part = np.array(bits & np.uint32(0xFFFF0000), np.uint32).view(np.float32)
        parts.append(float(part))
        rest = np.float32(rest - part)
    assert float(rest) == 0.0
    return parts


def constants():
    c = np.zeros((P, C_END), np.float32)
    c[:, C_ID:C_ID + P] = np.eye(P)
    d = np.arange(P) % DH
    theta = np.power(np.float32(10000.0), (np.float32(-2.0) * (d // 2).astype(np.float32) / np.float32(DH)).astype(np.float32))
    angle = theta[:, None].astype(np.float32) * np.arange(SEQ, dtype=np.float32)[None, :]
    c[:, C_COS:C_COS + SEQ] = np.cos(angle)
    c[:, C_SIN:C_SIN + SEQ] = np.sin(angle) * np.where(d % 2 == 0, -1.0, 1.0)[:, None]
    c[:, C_HEAD:C_HEAD + 8] = (np.arange(P)[:, None] % 64) // DH == np.arange(8)[None, :]
    c[:, C_CAUSAL:C_CAUSAL + SEQ] = np.where(np.arange(SEQ)[None, :] > np.arange(P)[:, None] % SEQ, CAUSAL_FILL, 0.0)
    c[:, C_IOTA:C_IOTA + 8] = np.arange(8)[None, :]
    for col, fill in ((C_FILL0, -1e9), (C_FILL1, -1e12)):
        for j, part in enumerate(bf16_parts(fill * np.sqrt(DH))):
            for b in range(2):
                c[2 * j + b, col + SEQ * b:col + SEQ * (b + 1)] = part
    c[:, C_ONES:C_ONES + P] = 1.0
    c[:, C_HALF:C_HALF + 2] = np.arange(P)[:, None] // 64 == np.arange(2)[None, :]
    return c


def decoder_kernel(nc, A, out):
    with ExitStack() as ctx:
        def sb(name, shape, dt=F32):
            return ctx.enter_context(nc.sbuf_tensor(name, shape, dt))

        def sem(name):
            return ctx.enter_context(nc.semaphore(name))

        running = {}

        class Mark:

            def __init__(self, name, total):
                if name not in running:
                    running[name] = [sem(name), 0]
                self.sem, self.base = running[name]
                running[name][1] += total

            def at(self, n):
                return self.sem, self.base + n

        def bc(ap, axis, n):
            shape = list(ap.shape)
            shape.insert(axis, n)
            return ap.unsqueeze(axis).to_broadcast(shape)

        table = nc.inline_tensor(constants(), "shape_constants").ap()
        PS = ctx.enter_context(nc.psum_tensor("banks", [P, 8, BANK], F32))
        cst = sb("cst", [P, C_END])
        X = sb("X", [P, NT, P])
        XR = sb("XR", [P, NT, P])
        XT = sb("XT", [P, NT * P])
        CT = sb("CT", [P, NT * P])
        WT = sb("WT", [P, 12, P])
        PR = sb("PR", [P, 3, HEADS * SEQ])
        PT = sb("PT", [P, 2, PAIRS, P])
        WQKV = sb("WQKV", [P, 3 * HEADS * DW])
        WOUT = sb("WOUT", [P, PAIRS, P])
        FCW = sb("FCW", [P, 2, CH, P])
        lnwb = sb("lnwb", [P, 2, CH])
        gw = sb("gw", [8, P])
        gwT = sb("gwT", [P, 8])
        qkb = sb("qkb", [P, 2, 2, 2])
        rowb = sb("rowb", [P, 4, P])
        mk = sb("mk", [P, NT, SEQ])
        mrb = sb("mrb", [6, NT, SEQ], BF16)
        idb = sb("idb", [P, P], BF16)
        caus = sb("caus", [P, SEQ], BF16)
        fills = sb("fills", [6, 2, P], BF16)
        mx = sb("mx", [P, 2, HEADS])
        rs = sb("rs", [P, 2, HEADS])
        ysb = sb("ysb", [P, 2, P])
        yT = sb("yT", [P, 2, P])
        R = sb("R", [P, 2, P])
        stats = sb("stats", [P, 2, 6])
        mv = sb("mv", [P, 2, 2])
        ve = sb("ve", [P, 2, 1])
        rstd = sb("rstd", [P, 2, 1])
        half = sb("half", [P, 1])
        lg = sb("lg", [P, NT, 8])
        top = sb("top", [P, NT, 8])
        topi = sb("topi", [P, NT, 8], U32)
        topf = sb("topf", [P, NT, 2])
        pk = sb("pk", [P, 4, NT])
        comb = sb("comb", [P, 2, NT, EXPERTS])
        gam = sb("gam", [P, 8])
        U = sb("U", [P, 32768])
        ident = cst[:, C_ID:C_ID + P]

        def region(start, size, pattern=None, **k):
            v = U[:, start:start + size]
            return v.rearrange(pattern, **k) if pattern else v

        WG = region(0, 4096, "p (e i) -> p e i", e=EXPERTS)
        WU = region(4096, 4096, "p (e i) -> p e i", e=EXPERTS)
        WD = region(8192, 4096, "p (e c h) -> p e c h", e=EXPERTS, c=CH)
        WGR = region(12288, 4096, "p (e c h) -> p e c h", e=EXPERTS, c=CH)
        WUR = region(16384, 4096, "p (e c h) -> p e c h", e=EXPERTS, c=CH)
        WDR = region(20480, 4096, "p (e i) -> p e i", e=EXPERTS)
        HID = region(12288, 4096, "p (k c t) -> p k c t", k=2, c=CH)
        SG = region(16384, 1024, "p (k t) -> p k t", k=2)
        QS = region(24576, 2048, "p (g t q) -> p g t q", g=2, t=NT)
        KT = region(26624, 1024, "p (g t k) -> p g t k", g=2, t=NT)
        KB = region(27648, 2048, "p (n g h k) -> p n g h k", n=2, g=2, h=8)
        VB = region(29696, 2304, "p (b r a e) -> p b r a e", b=BATCH, r=PAIRS, a=2)
        TMP = region(0, 2048, "p (n t k) -> p n t k", n=4, t=NT)
        TC = region(2048, 2048, "p (n t k) -> p n t k", n=4, t=NT)
        TS = region(4096, 2048, "p (n t k) -> p n t k", n=4, t=NT)
        RAWW = region(8192, 1536, "p (w f) -> p w f", w=12)
        CTXR = region(9728, 1024, "p (t f) -> p t f", t=NT)
        mki = region(10752, 512).bitcast(I32).rearrange("p (t k) -> p t k", t=NT)
        mri = U[0:6, 11264:11776].bitcast(I32).rearrange("p (t k) -> p t k", t=NT)
        QW = region(0, 8192, "p (u t) -> p u t", u=PAIRS)
        KW = region(8192, 8192, "p (u t) -> p u t", u=PAIRS)
        VW = region(16384, 16384, "p (b u a d) -> p b u a d", b=BATCH, u=PAIRS, a=2)
        YW = [XR, WT[:, 0:PAIRS, :]]
        FH = region(0, 1536, "p (n i) -> p n i", n=3)
        FN = region(1536, 1024, "p (n i) -> p n i", n=2)
        FT = region(2560, 1024, "p (n c t) -> p n c t", n=2, c=CH)
        FCT = region(4608, 1024, "p (n c f) -> p n c f", n=2, c=CH)
        FA = region(3584, 1024, "p (n i) -> p n i", n=2)

        s_cst = sem("cst_loaded")
        s_x = sem("x_loaded")
        s_ctx = sem("ctx_loaded")
        s_w = sem("attention_weights_loaded")
        s_b = sem("biases_loaded")
        s_m = sem("masks_loaded")
        s_moe = sem("expert_weights_loaded")
        s_wide = sem("wide_weights_loaded")
        s_fc = sem("ternary_weights_loaded")
        s_half = sem("minus_half_set")
        s_mk = sem("masks_made")
        s_bfc = sem("bf16_constants_made")
        s_out = sem("output_stored")
        s_mk0 = sem("masks_started")
        s_bf = sem("bf16_identity_made")

        WNAMES = ["L0_attn_wq", "L0_attn_wk", "L0_attn_wv", "L0_attn_wp",
                  "L0_xattn_Wq", "L0_xattn_Wk", "L0_xattn_Wv", "L0_xattn_Wo",
                  "L1_xattn_Wq", "L1_xattn_Wk", "L1_xattn_Wv", "L1_xattn_Wo"]
        block = ctx.enter_context(nc.Block())

        class Group:

            def __init__(self, waits, blocks, dst):
                self.waits, self.blocks, self.dst = waits, blocks, dst

        def transposes_plan(name, groups, banks=8):
            mm, ev = sem(name + "_transposed"), [sem(name + "_copied_act"), sem(name + "_copied_dve")]

            def pe(eng):
                for g, group in enumerate(groups):
                    for s, v in group.waits:
                        eng.wait_ge(s, v)
                    if g >= banks:
                        eng.wait_ge(ev[g % 2], (g - banks) // 2 + 1)
                    for n, (src, k) in enumerate(group.blocks):
                        m = eng.transpose(PS[:, g % banks, n * P:n * P + k], src, ident[0:k, 0:k])
                    m.then_inc(mm, 1)

            def copies(eng, part):
                for g, group in enumerate(groups):
                    if g % 2 != part:
                        continue
                    n = sum(k for _, k in group.blocks)
                    eng.wait_ge(mm, g + 1)
                    src = PS[:, g % banks, 0:n]
                    if part == 0:
                        eng.activation(group.dst, src, ACT.Copy).then_inc(ev[0], 1)
                    else:
                        eng.tensor_copy(group.dst, src).then_inc(ev[1], 1)

            def done(eng):
                eng.wait_ge(ev[0], (len(groups) + 1) // 2)
                if len(groups) > 1:
                    eng.wait_ge(ev[1], len(groups) // 2)

            return pe, copies, done

        xT_groups = [Group([(s_cst, 16), (s_x, 16)], [(X[:, 4 * g + j, :], P) for j in range(4)],
                           XT[:, BANK * g:BANK * (g + 1)]) for g in range(2)]
        w_groups = [Group([(s_w, 16 * 12)], [(RAWW[:, 4 * g + j, :], P) for j in range(4)],
                          WT[:, 4 * g:4 * g + 4, :].rearrange("p w f -> p (w f)")) for g in range(3)]
        c_groups = [Group([(s_ctx, 16)], [(CTXR[:, 4 * g + j, :], P) for j in range(4)],
                          CT[:, BANK * g:BANK * (g + 1)]) for g in range(2)]
        start_pe, start_copies, start_done = transposes_plan("start", xT_groups + w_groups + c_groups)
        moe_groups = []
        for e in range(EXPERTS):
            moe_groups += [
                Group([(s_moe, 16 * 4)], [(WGR[:, e, c, :], P) for c in range(CH)], WG[:, e, :]),
                Group([], [(WUR[:, e, c, :], P) for c in range(CH)], WU[:, e, :]),
                Group([], [(WDR[:, e, c * P:(c + 1) * P], P) for c in range(CH)],
                      WD[:, e, :, :].rearrange("p c h -> p (c h)"))]
        moe_groups += [Group([], [(gw[:, :], 8)], gwT[:, :])]
        moet_pe, moet_copies, moet_done = transposes_plan("experts", moe_groups)
        s_tern = sem("ternary_weights_made")
        fc_groups = [Group([(s_tern, 1 + n)], [(FCW[:, n, c, :], P) for c in range(CH)],
                           FCT[:, n, :, :].rearrange("p c f -> p (c f)")) for n in range(2)]
        fct_pe, fct_copies, fct_done = transposes_plan("ternary", fc_groups)

        class Norm:

            def __init__(self, name):
                last = name == "ternary"
                self.r = Mark("residual_summed", 0 if name == "experts" else NT)
                self.st = Mark("stats_made", NT)
                self.mv = Mark("variance_made", NT)
                self.ve = Mark("eps_added", NT)
                self.rstd = Mark("rstd_made", NT)
                self.ln = Mark("normed", NT)
                self.xmm = Mark("x_transposed", 0 if last else NT)
                self.xev = Mark("xT_copied", 0 if last else NT)
                self.xr = Mark("bias_added", NT)

            def stats(self, dve, i, src):
                dve.wait_ge(*self.r.at(i + 1))
                dve.bn_stats(stats[:, i % 2, :], src).then_inc(self.st.sem, 1)
                dve.wait_ge(*self.st.at(i + 1))
                if i >= 2:
                    dve.wait_ge(*self.ve.at(i - 1))
                    dve.wait_ge(*self.ln.at(i - 1))
                dve.bn_aggr(mv[:, i % 2, :], stats[:, i % 2, :]).then_inc(self.mv.sem, 1)

            def rsqrt(self, pool, i):
                pool.wait_ge(*self.mv.at(i + 1))
                pool.tensor_scalar(ve[:, i % 2, :], mv[:, i % 2, 1:2], LN_EPS, None, ALU.add).then_inc(self.ve.sem, 1)
                pool.wait_ge(*self.ve.at(i + 1))
                if i >= 2:
                    pool.wait_ge(*self.ln.at(i - 1))
                pool.tensor_tensor(rstd[:, i % 2, :], ve[:, i % 2, :], half[:, :], ALU.pow).then_inc(self.rstd.sem, 1)

            def apply(self, dve, i, src):
                dve.wait_ge(*self.rstd.at(i + 1))
                dve.tensor_scalar(X[:, i, :], src, mv[:, i % 2, 0:1], rstd[:, i % 2, :],
                                  ALU.subtract, ALU.mult).then_inc(self.ln.sem, 1)

            def add_bias(self, pool, i, row):
                pool.wait_ge(*self.ln.at(i + 1))
                pool.tensor_tensor(XR[:, i, :], X[:, i, :], rowb[:, row, :], ALU.add).then_inc(self.xr.sem, 1)

            def to_xT(self, act, i, bank=7, col=256):
                act.wait_ge(*self.xmm.at(i + 1))
                act.activation(XT[:, i * P:(i + 1) * P], PS[:, bank, col:col + P], ACT.Copy).then_inc(self.xev.sem, 1)

        class Narrow:

            def __init__(self, name, w, src, prev, rope=False, bias=None, fill=None, row=None, next_row=None):
                self.name, self.w, self.src, self.prev = name, w, src, prev
                self.rope, self.bias, self.fill, self.row, self.next_row = rope, bias, fill, row, next_row
                self.fresh = name != "cross0"
                r, z = 4 if rope else 0, 1 if self.fresh else 0
                self.qk_mm, self.v_mm = Mark("qk_projected", 4), Mark("v_projected", 2)
                self.tmp, self.cosd, self.shuf, self.sind = (
                    Mark("qk_copied", r), Mark("times_cos", r), Mark("pairs_swapped", r), Mark("times_sin", r))
                self.k_ready, self.q_ready, self.v_ready = Mark("k_ready", 2), Mark("q_ready", 4), Mark("v_ready", 4)
                self.zero, self.ones = Mark("q_zeroed", z), Mark("v_zeroed", 3 * z)
                self.kb, self.s_mm = Mark("k_blocks_made", 2 * NT), Mark("scored", NT)
                self.max, self.sub, self.exp = Mark("row_max_made", NT), Mark("max_subtracted", NT), Mark("exponentials_made", NT)
                self.t_mm, self.pt, self.pv = Mark("p_transposed", 2 * NT), Mark("pT_copied", 2 * NT), Mark("v_weighed", NT)
                self.rec, self.yn, self.y_mm = Mark("reciprocals_made", NT), Mark("y_normalized", NT), Mark("y_transposed", NT)
                self.yt, self.o_mm = Mark("yT_copied", NT), Mark("y_projected", NT)
                self.norm = Norm(name)

            def start(self, pe):
                if self.prev is None:
                    start_done(pe)
                else:
                    pe.wait_ge(*self.prev.xev.at(NT))

            def project(self, pe):
                self.start(pe)
                for n, (w, g, src) in enumerate(((1, 0, self.src), (1, 1, self.src), (0, 0, XT), (0, 1, XT))):
                    for b in range(2):
                        m = pe.matmul(PS[64 * b:64 * b + 64, n, :], WT[:, self.w + w, 64 * g:64 * g + 64],
                                      src.rearrange("f (t b q) -> f b t q", b=2, q=SEQ)[:, b],
                                      start=True, stop=True)
                    m.then_inc(self.qk_mm.sem, 1)
                for b in range(BATCH):
                    for a in range(2):
                        m = pe.matmul(PS[64 * a:64 * a + 64, 4 + b // 8, 64 * (b % 8):64 * (b % 8) + 64],
                                      self.src[:, SEQ * b:SEQ * (b + 1)],
                                      WT[:, self.w + 2, :].rearrange("f (r a d) -> f a r d", a=2, d=DH)[:, a],
                                      start=True, stop=True)
                    if b % 8 == 7:
                        m.then_inc(self.v_mm.sem, 1)

            def scores(self, pe, i):
                if i == 0:
                    pe.wait_ge(*self.q_ready.at(4))
                    pe.wait_ge(s_bfc, 1)
                    if self.fill is not None:
                        pe.wait_ge(s_mk, 1)
                if i >= 2:
                    pe.wait_ge(*self.sub.at(i - 1))
                for g in range(2):
                    pe.wait_ge(*self.kb.at(2 * i + g + 1))
                    o = PS[:, 2 * (i % 2) + g, :]
                    pe.matmul(o, QS[:, g, i, :], KB[:, i % 2, g].rearrange("p h k -> p (h k)"), start=True, stop=False)
                    o = o.rearrange("q (h k) -> q h k", h=8)
                    if self.fill is None:
                        m = pe.matmul(o, idb[:, :], bc(caus[:, :], 1, 8), start=False, stop=True)
                    else:
                        m = pe.matmul(o, fills[:, self.fill, :], bc(mrb[:, i, :], 1, 8), start=False, stop=True)
                m.then_inc(self.s_mm.sem, 1)

            def transpose_p(self, pe, i):
                pe.wait_ge(*self.exp.at(i + 1))
                if i == 0:
                    pe.wait_ge(*self.v_ready.at(4))
                for n in range(2):
                    if i >= 1:
                        pe.wait_ge(*self.pt.at(2 * i - 1 + n))
                    for r in range(4 * n, 4 * n + 4):
                        m = pe.transpose(PS[:, 4 + n, P * (r % 4):P * (r % 4 + 1)], PR[:, i % 3, P * r:P * (r + 1)], ident)
                    m.then_inc(self.t_mm.sem, 1)

            def weigh(self, pe, i):
                pe.wait_ge(*self.pt.at(2 * i + 2))
                if i >= 1:
                    pe.wait_ge(*self.yn.at(i))
                for r in range(PAIRS):
                    for b in range(2):
                        m = pe.matmul(PS[64 * b:64 * b + 64, 6, 18 * r:18 * r + 18], PT[:, i % 2, r, 64 * b:64 * b + 64],
                                      VB[:, 2 * i + b, r].rearrange("p a e -> p (a e)"), start=True, stop=True)
                m.then_inc(self.pv.sem, 1)

            def transpose_y(self, pe, i):
                pe.wait_ge(*self.yn.at(i + 1))
                if i >= 2:
                    pe.wait_ge(*self.norm.xev.at(i - 1))
                pe.transpose(PS[:, 7, 0:P], ysb[:, i % 2, :], ident).then_inc(self.y_mm.sem, 1)

            def project_y(self, pe, i):
                pe.wait_ge(*self.yt.at(i + 1))
                pe.matmul(PS[:, 7, P:2 * P], yT[:, i % 2, :], WT[:, self.w + 3, :],
                          start=True, stop=True).then_inc(self.o_mm.sem, 1)

            def transpose_x(self, pe, i):
                pe.wait_ge(*self.norm.ln.at(i + 1))
                if i >= 1:
                    pe.wait_ge(*self.norm.xev.at(i))
                pe.wait_ge(*self.norm.r.at(min(i + 2, NT)))
                pe.transpose(PS[:, 7, 2 * P:3 * P], X[:, i, :], ident).then_inc(self.norm.xmm.sem, 1)

            def pe(self, pe):
                self.project(pe)
                for j in range(NT + 5):
                    if j < NT:
                        self.scores(pe, j)
                    if 0 <= j - 4 < NT:
                        self.transpose_y(pe, j - 4)
                    if 0 <= j - 2 < NT:
                        self.transpose_p(pe, j - 2)
                    if 0 <= j - 4 < NT:
                        self.project_y(pe, j - 4)
                    if 0 <= j - 3 < NT:
                        self.weigh(pe, j - 3)
                    if 0 <= j - 5 < NT:
                        self.transpose_x(pe, j - 5)

            def act(self, act):
                ab = self.bias
                if self.rope:
                    for n in range(4):
                        act.wait_ge(*self.qk_mm.at(n + 1))
                        qk = 1 if n < 2 else 0
                        act.activation(TMP[:, n].rearrange("p t k -> p (t k)"), PS[:, n, :], ACT.Identity,
                                       bias=qkb[:, ab, qk, n % 2:n % 2 + 1]).then_inc(self.tmp.sem, 1)
                else:
                    if self.fresh:
                        act.wait_ge(*self.zero.at(1))
                    for g in range(2):
                        act.wait_ge(*self.qk_mm.at(3 + g))
                        for b in range(2):
                            rows = slice(64 * b, 64 * b + 64)
                            o = QS[rows, g, :, 64 * b:64 * b + 64]
                            s = PS[rows, 2 + g, :].rearrange("p (t q) -> p t q", q=SEQ)
                            if ab is None:
                                act.activation(o, s, ACT.Copy).then_inc(self.q_ready.sem, 1)
                            else:
                                act.activation(o, s, ACT.Identity, bias=qkb[rows, ab, 0, g:g + 1]).then_inc(self.q_ready.sem, 1)
                for j in range(NT + 5):
                    if 0 <= j - 4 < NT:
                        i = j - 4
                        act.wait_ge(*self.y_mm.at(i + 1))
                        if i >= 2:
                            act.wait_ge(*self.o_mm.at(i - 1))
                        act.activation(yT[:, i % 2, :], PS[:, 7, 0:P], ACT.Copy).then_inc(self.yt.sem, 1)
                    if 0 <= j - 2 < NT:
                        i = j - 2
                        if i >= 2:
                            act.wait_ge(*self.pv.at(i - 1))
                        for n in range(2):
                            act.wait_ge(*self.t_mm.at(2 * i + n + 1))
                            act.activation(PT[:, i % 2, 4 * n:4 * n + 4, :].rearrange("p r q -> p (r q)"),
                                           PS[:, 4 + n, :], ACT.Copy).then_inc(self.pt.sem, 1)
                    if j < NT:
                        act.wait_ge(*self.sub.at(j + 1))
                        act.activation(PR[:, j % 3, :], PR[:, j % 3, :], ACT.Exp, scale=float(DH) ** -0.5)\
                           .then_inc(self.exp.sem, 1)
                    if 0 <= j - 5 < NT:
                        self.norm.to_xT(act, j - 5)

            def dve_project(self, dve):
                ab = self.bias
                if self.rope:
                    swap = [p ^ 1 for p in range(32)]
                    dve.wait_ge(*self.zero.at(1))
                    for n in range(4):
                        g = n % 2
                        dve.wait_ge(*self.tmp.at(n + 1))
                        dve.stream_shuffle(TS[:, n].rearrange("p t k -> p (t k)"),
                                           TMP[:, n].rearrange("p t k -> p (t k)"), swap).then_inc(self.shuf.sem, 1)
                        dve.wait_ge(*self.shuf.at(n + 1))
                        dve.tensor_tensor(TS[:, n], TS[:, n], bc(cst[:, C_SIN:C_SIN + SEQ], 1, NT), ALU.mult)\
                           .then_inc(self.sind.sem, 1)
                        dve.wait_ge(*self.sind.at(n + 1))
                        dve.wait_ge(*self.cosd.at(n + 1))
                        if n < 2:
                            dve.tensor_tensor(KT[:, g], TC[:, n], TS[:, n], ALU.add).then_inc(self.k_ready.sem, 1)
                        else:
                            for b in range(2):
                                rows = slice(64 * b, 64 * b + 64)
                                dve.tensor_tensor(QS[rows, g, :, 64 * b:64 * b + 64], TC[rows, n], TS[rows, n],
                                                  ALU.add).then_inc(self.q_ready.sem, 1)
                else:
                    dve.wait_ge(s_mk, 1)
                    for g in range(2):
                        dve.wait_ge(*self.qk_mm.at(1 + g))
                        s = PS[:, g, :].rearrange("p (t k) -> p t k", k=SEQ)
                        if ab is None:
                            dve.tensor_tensor(KT[:, g], s, mk[:, :, :], ALU.mult).then_inc(self.k_ready.sem, 1)
                        else:
                            dve.scalar_tensor_tensor(KT[:, g].rearrange("p t k -> p (t k)"), PS[:, g, :],
                                                     qkb[:, ab, 1, g:g + 1],
                                                     mk[:, :, :].rearrange("p t k -> p (t k)"),
                                                     ALU.add, ALU.mult).then_inc(self.k_ready.sem, 1)
                if self.fresh:
                    dve.wait_ge(*self.ones.at(3))
                for v in range(2):
                    dve.wait_ge(*self.v_mm.at(v + 1))
                    for a in range(2):
                        rows = slice(64 * a, 64 * a + 64)
                        o = VB[rows, 8 * v:8 * v + 8, :, a, 0:DH]
                        s = PS[rows, 4 + v, :].rearrange("p (b r d) -> p b r d", b=8, d=DH)
                        if self.row is None:
                            dve.tensor_copy(o, s).then_inc(self.v_ready.sem, 1)
                        else:
                            bias = rowb[rows, self.row, :].rearrange("p (r a d) -> p a r d", a=2, d=DH)[:, a]
                            dve.tensor_tensor(o, s, bc(bias, 1, 8), ALU.add).then_inc(self.v_ready.sem, 1)

            def dve(self, dve):
                if self.row is not None:
                    dve.wait_ge(s_b, 16 * NB)
                self.dve_project(dve)
                norm = self.norm
                for j in range(NT + 5):
                    if 0 <= j - 4 < NT:
                        i = j - 4
                        dve.wait_ge(*self.pv.at(i + 1))
                        y = PS[:, 6, 0:18 * PAIRS].rearrange("q (h e) -> q h e", e=DH + 1)
                        dve.reciprocal(rs[:, i % 2, :].unsqueeze(2), y[:, :, DH:DH + 1]).then_inc(self.rec.sem, 1)
                        dve.wait_ge(*self.rec.at(i + 1))
                        if i >= 2:
                            dve.wait_ge(*self.y_mm.at(i - 1))
                        dve.tensor_tensor(ysb[:, i % 2, :].rearrange("q (h d) -> q h d", d=DH), y[:, :, 0:DH],
                                          bc(rs[:, i % 2, :], 2, DH), ALU.mult).then_inc(self.yn.sem, 1)
                    if 0 <= j - 5 < NT:
                        norm.apply(dve, j - 5, R[:, (j - 5) % 2, :])
                    if j < NT:
                        dve.wait_ge(*self.s_mm.at(j + 1))
                        s = PS[:, 2 * (j % 2):2 * (j % 2) + 2, :].rearrange("q g (h k) -> q (g h) k", k=SEQ)
                        dve.tensor_reduce(mx[:, j % 2, :], s, AX.X, ALU.max).then_inc(self.max.sem, 1)
                        dve.wait_ge(*self.max.at(j + 1))
                        if j >= 3:
                            dve.wait_ge(*self.t_mm.at(2 * (j - 3) + 2))
                        dve.tensor_tensor(PR[:, j % 3, :].rearrange("q (h k) -> q h k", k=SEQ), s,
                                          bc(mx[:, j % 2, :], 2, SEQ), ALU.subtract).then_inc(self.sub.sem, 1)
                    if 0 <= j - 4 < NT:
                        i = j - 4
                        dve.wait_ge(*self.o_mm.at(i + 1))
                        res = X
                        if self.row is not None:
                            res = XR
                            dve.wait_ge(*self.res_sem.at(i + 1))
                        dve.tensor_tensor(R[:, i % 2, :], PS[:, 7, P:2 * P], res[:, i, :], ALU.add).then_inc(norm.r.sem, 1)
                        norm.stats(dve, i, R[:, i % 2, :])

            def blocks(self, pool, i):
                if i >= NT:
                    return
                if i >= 2:
                    pool.wait_ge(*self.s_mm.at(i - 1))
                for g in range(2):
                    pool.tensor_tensor(KB[:, i % 2, g], bc(KT[:, g, i, :], 1, 8),
                                       bc(cst[:, C_HEAD:C_HEAD + 8], 2, SEQ), ALU.mult).then_inc(self.kb.sem, 1)

            def pool_zero(self, pool):
                pool.memset(QS, 0.0).then_inc(self.zero.sem, 1)
                pool.memset(VB, 0.0).then_inc(self.ones.sem, 1)
                pool.wait_ge(*self.ones.at(1))
                for a in range(2):
                    pool.tensor_copy(VB[:, :, :, a, DH], bc(cst[:, C_HALF + a:C_HALF + a + 1], 1, BATCH).rearrange(
                        "p b o -> p b o").to_broadcast([P, BATCH, PAIRS])).then_inc(self.ones.sem, 1)

            def pool(self, pool):
                if self.rope:
                    for n in range(4):
                        pool.wait_ge(*self.tmp.at(n + 1))
                        pool.tensor_tensor(TC[:, n], TMP[:, n], bc(cst[:, C_COS:C_COS + SEQ], 1, NT), ALU.mult)\
                            .then_inc(self.cosd.sem, 1)
                pool.wait_ge(*self.k_ready.at(2))
                self.blocks(pool, 0)
                self.blocks(pool, 1)
                for j in range(NT + 5):
                    self.blocks(pool, j + 2)
                    if 0 <= j - 4 < NT:
                        self.norm.rsqrt(pool, j - 4)
                    if self.next_row is not None and 0 <= j - 5 < NT:
                        self.norm.add_bias(pool, j - 5, self.next_row)

        class Experts:
            def __init__(self, name, prev):
                self.prev = prev
                self.gate_mm = Mark("logits_made", 0)
                self.gate_read = Mark("logits_copied", 0)
                self.top = Mark("logits_sorted", 0)
                self.topi = Mark("experts_ranked", 0)
                self.diff = Mark("logit_difference_made", 0)
                self.e2 = Mark("second_exponential_made", 0)
                self.den = Mark("pair_sum_made", 0)
                self.p1 = Mark("first_weight_made", 0)
                self.p2 = Mark("second_weight_made", 0)
                self.oh = Mark("choices_made", 0)
                self.comb = Mark("expert_weights_made", 0)
                self.g_mm = Mark("gates_projected", 0)
                self.u_mm = Mark("ups_projected", 0)
                self.silu = Mark("silu_made", 0)
                self.mul = Mark("hidden_made", 0)
                self.d_mm = Mark("downs_projected", 0)
                self.acc = Mark("expert_added", 0)
                self.norm = Norm(name)

            def gate_up(self, pe, k, c):
                n = 4 * k + c
                e, h = k // 2, k % 2
                if n >= 2:
                    pe.wait_ge(*self.silu.at(n - 1))
                    pe.wait_ge(*self.mul.at(n - 1))
                for bank, w, s in ((n % 2, WG, self.g_mm), (2 + n % 2, WU, self.u_mm)):
                    pe.matmul(PS[:, bank, :], w[:, e, P * c:P * (c + 1)], XT[:, BANK * h:BANK * (h + 1)],
                              start=True, stop=True).then_inc(s.sem, 1)

            def down(self, pe, k, t):
                if t == 0:
                    pe.wait_ge(*self.mul.at(4 * k + 4))
                    if k >= 2:
                        pe.wait_ge(*self.acc.at(4 * (k - 1)))
                for c in range(CH):
                    m = pe.matmul(PS[:, 4 + k % 2, P * t:P * (t + 1)], HID[:, k % 2, c, P * t:P * (t + 1)],
                                  WD[:, k // 2, c, :], start=(c == 0), stop=(c == CH - 1))
                m.then_inc(self.d_mm.sem, 1)

            def pe(self, pe):
                pe.wait_ge(*self.prev.xev.at(NT))
                moet_pe(pe)
                moet_done(pe)
                for t in range(NT):
                    m = pe.matmul(PS[:, 6, 8 * t:8 * t + 8], XT[:, P * t:P * (t + 1)], gwT[:, :], start=True, stop=True)
                m.then_inc(self.gate_mm.sem, 1)
                for k in range(2 * EXPERTS + 1):
                    for c in range(CH):
                        if k < 2 * EXPERTS:
                            self.gate_up(pe, k, c)
                        if k >= 1:
                            self.down(pe, k - 1, c)
                for i in range(NT):
                    pe.wait_ge(*self.norm.ln.at(i + 1))
                    if i >= 2:
                        pe.wait_ge(*self.norm.xev.at(i - 1))
                    pe.transpose(PS[:, 6 + i % 2, 0:P], X[:, i, :], ident).then_inc(self.norm.xmm.sem, 1)

            def act(self, act):
                moet_copies(act, 0)
                act.wait_ge(*self.diff.at(1))
                act.activation(pk[:, 1, :], pk[:, 0, :], ACT.Exp).then_inc(self.e2.sem, 1)
                for n in range(8 * EXPERTS):
                    act.wait_ge(*self.g_mm.at(n + 1))
                    if n >= 2:
                        act.wait_ge(*self.mul.at(n - 1))
                    act.activation(SG[:, n % 2, :], PS[:, n % 2, :], ACT.Silu).then_inc(self.silu.sem, 1)
                for i in range(NT):
                    self.norm.to_xT(act, i, 6 + i % 2, 0)

            def route(self, dve):
                dve.wait_ge(*self.gate_mm.at(1))
                dve.tensor_copy(lg[:, :, :].rearrange("p t e -> p (t e)"), PS[:, 6, 0:8 * NT]).then_inc(self.gate_read.sem, 1)
                dve.wait_ge(*self.gate_read.at(1))
                for t in range(NT):
                    dve.max(top[:, t, :], lg[:, t, :]).then_inc(self.top.sem, 1)
                dve.wait_ge(*self.top.at(NT))
                for t in range(NT):
                    dve.max_index(topi[:, t, :], top[:, t, :], lg[:, t, :]).then_inc(self.topi.sem, 1)
                dve.tensor_tensor(pk[:, 0, :], top[:, :, 1], top[:, :, 0], ALU.subtract).then_inc(self.diff.sem, 1)
                dve.wait_ge(*self.topi.at(NT))
                dve.tensor_copy(topf[:, :, :], topi[:, :, 0:2]).then_inc(self.topi.sem, 1)
                dve.wait_ge(*self.e2.at(1))
                dve.tensor_scalar(pk[:, 2, :], pk[:, 1, :], 1.0, None, ALU.add).then_inc(self.den.sem, 1)
                dve.wait_ge(*self.den.at(1))
                dve.reciprocal(pk[:, 2, :], pk[:, 2, :]).then_inc(self.p1.sem, 1)
                dve.wait_ge(*self.p1.at(1))
                dve.tensor_tensor(pk[:, 3, :], pk[:, 1, :], pk[:, 2, :], ALU.mult).then_inc(self.p2.sem, 1)
                dve.wait_ge(*self.p2.at(1))
                dve.wait_ge(*self.topi.at(NT + 1))
                for t in range(NT):
                    for r in range(2):
                        dve.tensor_scalar(comb[:, r, t, :], cst[:, C_IOTA:C_IOTA + 8], topf[:, t, r:r + 1],
                                          pk[:, 2 + r, t:t + 1], ALU.is_equal, ALU.mult).then_inc(self.oh.sem, 1)
                dve.wait_ge(*self.oh.at(2 * NT))
                dve.tensor_tensor(comb[:, 0], comb[:, 0], comb[:, 1], ALU.add).then_inc(self.comb.sem, 1)
                dve.wait_ge(*self.comb.at(1))

            def accumulate(self, dve, k):
                dve.wait_ge(*self.d_mm.at(4 * k + 4))
                e, h = k // 2, k % 2
                if k >= 2:
                    dve.wait_ge(*self.acc.at(4 * (k - 1)))
                for j in range(4):
                    t = 4 * h + j
                    dve.scalar_tensor_tensor(XR[:, t, :], PS[:, 4 + k % 2, P * j:P * (j + 1)], comb[:, 0, t, e:e + 1],
                                             (X if e == 0 else XR)[:, t, :], ALU.mult, ALU.add).then_inc(self.acc.sem, 1)

            def dve(self, dve):
                moet_copies(dve, 1)
                self.route(dve)
                K = 2 * EXPERTS
                for k in range(K):
                    for c in range(CH):
                        n = 4 * k + c
                        dve.wait_ge(*self.silu.at(n + 1))
                        dve.wait_ge(*self.u_mm.at(n + 1))
                        if k >= 2:
                            dve.wait_ge(*self.d_mm.at(4 * (k - 1)))
                        dve.tensor_tensor(HID[:, k % 2, c, :], PS[:, 2 + n % 2, :], SG[:, n % 2, :], ALU.mult)\
                           .then_inc(self.mul.sem, 1)
                        if c == 0 and k >= 2:
                            self.accumulate(dve, k - 2)
                self.accumulate(dve, K - 2)
                self.accumulate(dve, K - 1)
                norm = self.norm
                dve.wait_ge(*self.acc.at(4 * K))
                for i in range(NT + 1):
                    if i < NT:
                        dve.bn_stats(stats[:, i % 2, :], XR[:, i, :]).then_inc(norm.st.sem, 1)
                        dve.wait_ge(*norm.st.at(i + 1))
                        dve.bn_aggr(mv[:, i % 2, :], stats[:, i % 2, :]).then_inc(norm.mv.sem, 1)
                    if i >= 1:
                        norm.apply(dve, i - 1, XR[:, i - 1, :])
                        dve.wait_ge(*norm.ln.at(i))

            def pool(self, pool):
                for i in range(NT):
                    self.norm.rsqrt(pool, i)

        class Wide:

            def __init__(self, name, prev):
                self.prev = prev
                self.qk_mm, self.qk_act, self.qk_dve = Mark("qk_projected", 32), Mark("wide_qk_act", 16), Mark("wide_qk_dve", 16)
                self.v_mm, self.v_act, self.v_dve = Mark("v_projected", 16), Mark("wide_v_act", 16), Mark("wide_v_dve", 16)
                self.zero, self.s_mm = Mark("wide_v_zeroed", 1), Mark("scored", NT)
                self.max, self.sub, self.exp = Mark("row_max_made", NT), Mark("max_subtracted", NT), Mark("exponentials_made", NT)
                self.sum, self.rec, self.pn = Mark("wide_summed", NT), Mark("reciprocals_made", NT), Mark("wide_p_normalized", NT)
                self.t_mm, self.pt, self.pv = Mark("p_transposed", 2 * NT), Mark("pT_copied", 2 * NT), Mark("v_weighed", 2 * NT)
                self.yt, self.o_mm = Mark("yT_copied", 2 * NT), Mark("y_projected", NT)
                self.norm = Norm(name)

            def pe(self, pe):
                pe.wait_ge(*self.prev.xev.at(NT))
                pe.wait_ge(s_wide, 32)
                w = WQKV[:, :].rearrange("f (m c) -> f c m", c=3)
                n = 0
                for c, _ in ((0, QW), (1, KW)):
                    for u in range(PAIRS):
                        for h in range(2):
                            if n >= 4:
                                pe.wait_ge(*(self.qk_act if n % 2 == 0 else self.qk_dve).at((n - 4) // 2 + 1))
                            pe.matmul(PS[:, n % 4, :], w[:, c, P * u:P * (u + 1)], XT[:, BANK * h:BANK * (h + 1)],
                                      start=True, stop=True).then_inc(self.qk_mm.sem, 1)
                            n += 1
                for b in range(BATCH):
                    if b >= 4:
                        pe.wait_ge(*(self.v_act if b % 2 == 0 else self.v_dve).at(2 * ((b - 4) // 2 + 1)))
                    for a in range(2):
                        m = pe.matmul(PS[64 * a:64 * a + 64, 4 + b % 4, :], XT[:, SEQ * b:SEQ * (b + 1)],
                                      w[:, 2, :].rearrange("f (u a d) -> f a u d", a=2, d=DW)[:, a], start=True, stop=True)
                    m.then_inc(self.v_mm.sem, 1)
                pe.wait_ge(*self.qk_act.at(16))
                pe.wait_ge(*self.qk_dve.at(16))
                for j in range(NT + 5):
                    if j < NT:
                        self.scores(pe, j)
                    if 0 <= j - 2 < NT:
                        self.transpose_p(pe, j - 2)
                    if 0 <= j - 3 < NT:
                        self.weigh(pe, j - 3, 0)
                    if 0 <= j - 4 < NT:
                        self.project_y(pe, j - 4)
                    if 0 <= j - 3 < NT:
                        self.weigh(pe, j - 3, 1)
                    if 0 <= j - 5 < NT:
                        self.transpose_x(pe, j - 5)

            def scores(self, pe, i):
                if i >= 2:
                    pe.wait_ge(*self.sub.at(i - 1))
                for a in range(2):
                    for b in range(2):
                        t = P * i + 64 * b
                        rows = slice(64 * a, 64 * a + 64)
                        for u in range(PAIRS):
                            m = pe.matmul(PS[64 * b:64 * b + 64, 2 * (i % 2) + a, SEQ * u:SEQ * (u + 1)],
                                          QW[rows, u, t:t + 64], KW[rows, u, t:t + 64], start=True, stop=True)
                m.then_inc(self.s_mm.sem, 1)

            def transpose_p(self, pe, i):
                pe.wait_ge(*self.pn.at(i + 1))
                if i == 0:
                    pe.wait_ge(*self.v_act.at(16))
                    pe.wait_ge(*self.v_dve.at(16))
                for n in range(2):
                    if i >= 1:
                        pe.wait_ge(*self.pt.at(2 * i - 1 + n))
                    for r in range(4 * n, 4 * n + 4):
                        m = pe.transpose(PS[:, 4 + n, P * (r % 4):P * (r % 4 + 1)], PR[:, i % 3, P * r:P * (r + 1)], ident)
                    m.then_inc(self.t_mm.sem, 1)

            def weigh(self, pe, i, n):
                pe.wait_ge(*self.pt.at(2 * i + 2))
                if 2 * i + n >= 1:
                    pe.wait_ge(*self.yt.at(2 * i + n))
                for r in range(4 * n, 4 * n + 4):
                    for b in range(2):
                        m = pe.matmul(PS[:, 6, P * (r % 4) + 64 * b:P * (r % 4) + 64 * b + 64],
                                      VW[:, 2 * i + b, r].rearrange("p a d -> p (a d)"),
                                      PT[:, i % 2, r, 64 * b:64 * b + 64], start=True, stop=True)
                m.then_inc(self.pv.sem, 1)

            def project_y(self, pe, i):
                pe.wait_ge(*self.yt.at(2 * i + 2))
                if i >= 1:
                    pe.wait_ge(*self.norm.r.at(i))
                if i >= 2:
                    pe.wait_ge(*self.norm.xev.at(i - 1))
                for u in range(PAIRS):
                    m = pe.matmul(PS[:, 7, P:2 * P], YW[i % 2][:, u, :], WOUT[:, u, :],
                                  start=(u == 0), stop=(u == PAIRS - 1))
                m.then_inc(self.o_mm.sem, 1)

            def transpose_x(self, pe, i):
                pe.wait_ge(*self.norm.ln.at(i + 1))
                if i >= 1:
                    pe.wait_ge(*self.norm.xev.at(i))
                pe.wait_ge(*self.norm.r.at(min(i + 2, NT)))
                pe.transpose(PS[:, 7, 2 * P:3 * P], X[:, i, :], ident).then_inc(self.norm.xmm.sem, 1)

            def copies(self, eng, part, copy):
                n = 0
                for dst in (QW, KW):
                    for u in range(PAIRS):
                        for h in range(2):
                            if n % 2 == part:
                                eng.wait_ge(*self.qk_mm.at(n + 1))
                                copy(dst[:, u, BANK * h:BANK * (h + 1)], PS[:, n % 4, :])\
                                    .then_inc((self.qk_act, self.qk_dve)[part].sem, 1)
                            n += 1
                eng.wait_ge(*self.zero.at(1))
                for b in range(BATCH):
                    if b % 2 == part:
                        eng.wait_ge(*self.v_mm.at(b + 1))
                        for a in range(2):
                            rows = slice(64 * a, 64 * a + 64)
                            copy(VW[rows, b, :, a, :], PS[rows, 4 + b % 4, :].rearrange("p (u d) -> p u d", d=DW))\
                                .then_inc((self.v_act, self.v_dve)[part].sem, 1)

            def act(self, act):
                self.copies(act, 0, lambda o, s: act.activation(o, s, ACT.Copy))
                for j in range(NT + 5):
                    if 0 <= j - 2 < NT:
                        i = j - 2
                        if i >= 2:
                            act.wait_ge(*self.pv.at(2 * (i - 1)))
                        for n in range(2):
                            act.wait_ge(*self.t_mm.at(2 * i + n + 1))
                            act.activation(PT[:, i % 2, 4 * n:4 * n + 4, :].rearrange("p r q -> p (r q)"),
                                           PS[:, 4 + n, :], ACT.Copy).then_inc(self.pt.sem, 1)
                    for n in range(2):
                        if n == 1 and j < NT:
                            act.wait_ge(*self.sub.at(j + 1))
                            act.activation(PR[:, j % 3, :], PR[:, j % 3, :], ACT.Exp, scale=float(DW) ** -0.5)\
                               .then_inc(self.exp.sem, 1)
                        if 0 <= j - 3 < NT:
                            i = j - 3
                            act.wait_ge(*self.pv.at(2 * i + n + 1))
                            if i >= 2:
                                act.wait_ge(*self.o_mm.at(i - 1))
                            act.activation(YW[i % 2][:, 4 * n:4 * n + 4, :].rearrange("p u q -> p (u q)"),
                                           PS[:, 6, :], ACT.Copy).then_inc(self.yt.sem, 1)
                    if 0 <= j - 5 < NT:
                        self.norm.to_xT(act, j - 5)

            def dve(self, dve):
                self.copies(dve, 1, lambda o, s: dve.tensor_copy(o, s))
                norm = self.norm

                def sums(i):
                    dve.wait_ge(*self.exp.at(i + 1))
                    s = PR[:, i % 3, :].rearrange("q (h k) -> q h k", k=SEQ)
                    dve.tensor_reduce(mx[:, i % 2, :], s, AX.X, ALU.add).then_inc(self.sum.sem, 1)
                    dve.wait_ge(*self.sum.at(i + 1))
                    if i >= 2:
                        dve.wait_ge(*self.pn.at(i - 1))
                    dve.reciprocal(rs[:, i % 2, :], mx[:, i % 2, :]).then_inc(self.rec.sem, 1)
                    dve.wait_ge(*self.rec.at(i + 1))

                for j in range(NT + 5):
                    if 0 <= j - 1 < NT:
                        sums(j - 1)
                    if 0 <= j - 5 < NT:
                        norm.apply(dve, j - 5, R[:, (j - 5) % 2, :])
                    if j < NT:
                        dve.wait_ge(*self.s_mm.at(j + 1))
                        s = PS[:, 2 * (j % 2):2 * (j % 2) + 2, :].rearrange("q g (h k) -> q (g h) k", k=SEQ)
                        dve.tensor_reduce(mx[:, j % 2, :], s, AX.X, ALU.max).then_inc(self.max.sem, 1)
                        dve.wait_ge(*self.max.at(j + 1))
                        if j >= 3:
                            dve.wait_ge(*self.t_mm.at(2 * (j - 3) + 2))
                        dve.tensor_tensor(PR[:, j % 3, :].rearrange("q (u a k) -> q a u k", a=2, k=SEQ),
                                          s.rearrange("q (a u) k -> q a u k", a=2),
                                          bc(mx[:, j % 2, :].rearrange("q (a u) -> q a u", a=2), 3, SEQ),
                                          ALU.subtract).then_inc(self.sub.sem, 1)
                        dve.wait_ge(*self.sub.at(j + 1))
                    if 0 <= j - 4 < NT:
                        i = j - 4
                        dve.wait_ge(*self.o_mm.at(i + 1))
                        dve.tensor_tensor(R[:, i % 2, :], PS[:, 7, P:2 * P], X[:, i, :], ALU.add).then_inc(norm.r.sem, 1)
                        norm.stats(dve, i, R[:, i % 2, :])

            def pool_zero(self, pool):
                pool.memset(VW, 0.0).then_inc(self.zero.sem, 1)

            def pool(self, pool):
                pool.wait_ge(*self.prev.xev.at(NT))
                self.pool_zero(pool)
                pool.wait_ge(*self.zero.at(1))
                for j in range(NT + 5):
                    if 0 <= j - 4 < NT:
                        self.norm.rsqrt(pool, j - 4)
                    if j < NT:
                        pool.wait_ge(*self.rec.at(j + 1))
                        s = PR[:, j % 3, :].rearrange("q (h k) -> q h k", k=SEQ)
                        pool.tensor_tensor(s, s, bc(rs[:, j % 2, :], 2, SEQ), ALU.mult).then_inc(self.pn.sem, 1)

        class Ternary:
            def __init__(self, name, prev):
                self.prev = prev
                self.abs = Mark("magnitudes_summed", 0)
                self.gsum = Mark("magnitude_totals_made", 0)
                self.thr = Mark("thresholds_made", 0)
                self.low = Mark("negatives_found", 0)
                self.h_mm = Mark("hidden_projected", 0)
                self.gelu = Mark("gelu_made", 0)
                self.st = Mark("hidden_stats_made", 0)
                self.mv = Mark("hidden_variance_made", 0)
                self.ve = Mark("hidden_eps_added", 0)
                self.rstd = Mark("hidden_rstd_made", 0)
                self.n = Mark("hidden_normed", 0)
                self.t_mm = Mark("hidden_transposed", 0)
                self.ht = Mark("hiddenT_copied", 0)
                self.o_mm = Mark("ternary_projected", 0)
                self.norm = Norm(name)

            def prepare_dve_a(self, dve):
                dve.wait_ge(s_fc, 64)
                for n in range(2):
                    dve.tensor_reduce(gam[:, n:n + 1], FCW[:, n].rearrange("p c f -> p (c f)"), AX.X, ALU.add,
                                      apply_absolute_value=True).then_inc(self.abs.sem, 1)

            def prepare_pe(self, pe):
                pe.wait_ge(*self.abs.at(2))
                pe.matmul(PS[:, 6, 0:2], cst[:, C_ONES:C_ONES + P], gam[:, 0:2], start=True, stop=True)\
                    .then_inc(self.gsum.sem, 1)

            def prepare_dve_b(self, dve):
                dve.wait_ge(*self.gsum.at(1))
                for s in (0.5, -0.5):
                    k = 2 if s > 0 else 4
                    dve.tensor_scalar(gam[:, k:k + 2], PS[:, 6, 0:2], s / (P * INNER), s * 1e-6, ALU.mult, ALU.add)\
                       .then_inc(self.thr.sem, 1)
                dve.wait_ge(*self.thr.at(2))
                for n in range(2):
                    w = FCW[:, n].rearrange("p c f -> p (c f)")
                    dve.tensor_scalar(FA[:, n, :], w, gam[:, 4 + n:5 + n], None, ALU.is_lt).then_inc(self.low.sem, 1)
                dve.wait_ge(*self.low.at(2))
                for n in range(2):
                    w = FCW[:, n].rearrange("p c f -> p (c f)")
                    dve.scalar_tensor_tensor(w, w, gam[:, 2 + n:3 + n], FA[:, n, :], ALU.is_gt, ALU.subtract)\
                       .then_inc(s_tern, 1)

            def pe(self, pe):
                pe.wait_ge(*self.prev.xev.at(NT))
                self.prepare_pe(pe)
                fct_pe(pe)
                fct_done(pe)
                for j in range(NT + 4):
                    if j < NT:
                        if j >= 2:
                            pe.wait_ge(*self.gelu.at(j - 1))
                        pe.matmul(PS[:, j % 2, :], XT[:, P * j:P * (j + 1)], FCT[:, 0].rearrange("p c f -> p (c f)"),
                                  start=True, stop=True).then_inc(self.h_mm.sem, 1)
                    if 0 <= j - 3 < NT:
                        i = j - 3
                        pe.wait_ge(*self.ht.at(4 * i + 4))
                        if i >= 2:
                            pe.wait_ge(*self.norm.r.at(i - 1))
                        for c in range(CH):
                            m = pe.matmul(PS[:, 4 + i % 2, 0:P], FT[:, i % 2, c, :], FCT[:, 1, c, :],
                                          start=(c == 0), stop=(c == CH - 1))
                        m.then_inc(self.o_mm.sem, 1)
                    if 0 <= j - 2 < NT:
                        i = j - 2
                        pe.wait_ge(*self.n.at(i + 1))
                        if i >= 2:
                            pe.wait_ge(*self.ht.at(4 * (i - 1)))
                        for c in range(CH):
                            m = pe.transpose(PS[:, 2 + i % 2, P * c:P * (c + 1)], FN[:, i % 2, P * c:P * (c + 1)], ident)
                        m.then_inc(self.t_mm.sem, 1)

            def act(self, act):
                fct_copies(act, 0)
                for j in range(NT + 4):
                    if j < NT:
                        act.wait_ge(*self.h_mm.at(j + 1))
                        if j >= 3:
                            act.wait_ge(*self.n.at(j - 2))
                        act.activation(FH[:, j % 3, :], PS[:, j % 2, :], ACT.Gelu).then_inc(self.gelu.sem, 1)
                    if 0 <= j - 2 < NT:
                        i = j - 2
                        act.wait_ge(*self.t_mm.at(i + 1))
                        if i >= 2:
                            act.wait_ge(*self.o_mm.at(i - 1))
                        for c in range(CH):
                            act.activation(FT[:, i % 2, c, :], PS[:, 2 + i % 2, P * c:P * (c + 1)], ACT.Identity,
                                           bias=lnwb[:, 1, c:c + 1], scale=lnwb[:, 0, c:c + 1]).then_inc(self.ht.sem, 1)

            def dve(self, dve):
                self.prepare_dve_a(dve)
                self.prepare_dve_b(dve)
                fct_copies(dve, 1)
                norm = self.norm
                hst = ysb
                for j in range(NT + 5):
                    if j < NT:
                        dve.wait_ge(*self.gelu.at(j + 1))
                        dve.bn_stats(hst[:, j % 2, 0:6], FH[:, j % 3, :]).then_inc(self.st.sem, 1)
                        dve.wait_ge(*self.st.at(j + 1))
                        if j >= 2:
                            dve.wait_ge(*self.n.at(j - 1))
                            dve.wait_ge(*self.ve.at(j - 1))
                        dve.bn_aggr(hst[:, j % 2, 8:10], hst[:, j % 2, 0:6]).then_inc(self.mv.sem, 1)
                    if 0 <= j - 1 < NT:
                        i = j - 1
                        dve.wait_ge(*self.rstd.at(i + 1))
                        if i >= 2:
                            dve.wait_ge(*self.t_mm.at(i - 1))
                        dve.tensor_scalar(FN[:, i % 2, :], FH[:, i % 3, :], hst[:, i % 2, 8:9], hst[:, i % 2, 13:14],
                                          ALU.subtract, ALU.mult).then_inc(self.n.sem, 1)
                    if 0 <= j - 4 < NT:
                        norm.apply(dve, j - 4, R[:, (j - 4) % 2, :])
                        dve.wait_ge(*norm.ln.at(j - 3))
                    if 0 <= j - 3 < NT:
                        i = j - 3
                        dve.wait_ge(*self.o_mm.at(i + 1))
                        dve.tensor_tensor(R[:, i % 2, :], PS[:, 4 + i % 2, 0:P], X[:, i, :], ALU.add).then_inc(norm.r.sem, 1)
                        norm.stats(dve, i, R[:, i % 2, :])

            def pool(self, pool):
                hst = ysb
                for j in range(NT + 4):
                    if j < NT:
                        pool.wait_ge(*self.mv.at(j + 1))
                        pool.tensor_scalar(hst[:, j % 2, 12:13], hst[:, j % 2, 9:10], LN_EPS, None, ALU.add)\
                            .then_inc(self.ve.sem, 1)
                        pool.wait_ge(*self.ve.at(j + 1))
                        if j >= 2:
                            pool.wait_ge(*self.n.at(j - 1))
                        pool.tensor_tensor(hst[:, j % 2, 13:14], hst[:, j % 2, 12:13], half[:, :], ALU.pow)\
                            .then_inc(self.rstd.sem, 1)
                    if 0 <= j - 3 < NT:
                        self.norm.rsqrt(pool, j - 3)

        a0 = Narrow("self0", 0, XT, None, rope=True, bias=0, row=0, next_row=3)
        a0.res_sem = Mark("first_residual_made", 0)
        a1 = Narrow("cross0", 4, CT, a0.norm, bias=1, fill=0, row=2)
        a1.res_sem = a0.norm.xr
        moe = Experts("experts", a1.norm)
        wide = Wide("wide", moe.norm)
        a2 = Narrow("cross1", 8, CT, wide.norm, fill=1)
        fc = Ternary("ternary", a2.norm)
        NB = 12

        @block.sync
        def _(sp):
            def load(dst, src, s, **k):
                sp.dma_start(dst, src, **k).then_inc(s, 16)

            load(X[:, :, :], A["x"].rearrange("(t b) s f -> (b s) t f", b=2), s_x)
            load(cst[:, :], table, s_cst)
            for n, name in enumerate(WNAMES):
                load(RAWW[:, n, :], A[name], s_w)
            for b, (names) in enumerate((("L0_attn_bq", "L0_attn_bk"), ("L0_xattn_bq", "L0_xattn_bk"))):
                for n, name in enumerate(names):
                    for r in range(2):
                        load(qkb[64 * r:64 * r + 64, b, n, :], A[name].rearrange("(g p) -> p g", g=2), s_b,
                             allow_slow_non_contiguous=True)
            for n, name in enumerate(("L0_attn_bv", "L0_attn_bp", "L0_xattn_bv", "L0_xattn_bo")):
                load(rowb[:, n, :], A[name].partition_broadcast(P), s_b)
            load(CTXR[:, :, :], A["ctx_1024"].rearrange("(t b) s f -> (b s) t f", b=2), s_ctx)
            mask = A["mask_Bx1x1xS2_ik0"].rearrange("(t b) x y k -> b (x y) t k", b=2)
            for b in range(2):
                load(mki[64 * b:64 * b + 64, :, :], mask[b].to_broadcast([64, NT, SEQ]), s_m)
            for j in range(3):
                load(mri[2 * j:2 * j + 2, :, :], mask[:, 0], s_m)
            for e in range(0, EXPERTS, 8):
                load(WGR[:, e:e + 8], A["L0_ffn_wg"].rearrange("e (c i) h -> i e c h", c=CH), s_moe)
                load(WUR[:, e:e + 8], A["L0_ffn_wu"].rearrange("e (c i) h -> i e c h", c=CH), s_moe)
                load(WDR[:, e:e + 8], A["L0_ffn_wd"].rearrange("e h i -> h e i"), s_moe)
            load(gw[:, :], A["L0_ffn_gate_w"], s_moe)
            load(WQKV[:, :], A["L1_attn_W_qkv"], s_wide)
            load(WOUT[:, :, :], A["L1_attn_W_out"].rearrange("(u p) f -> p u f", p=P), s_wide)
            load(FCW[:, 0], A["L1_ffn_W_fc"].rearrange("(c i) f -> i c f", c=CH), s_fc)
            load(FCW[:, 1].rearrange("p c f -> p (c f)"), A["L1_ffn_W_proj"], s_fc)
            for n, name in enumerate(("L1_ffn_ln_w", "L1_ffn_ln_b")):
                load(lnwb[:, n, :], A[name].rearrange("(c p) -> p c", c=CH), s_fc, allow_slow_non_contiguous=True)
            out_v = out.rearrange("(t b) s f -> (b s) t f", b=2)
            for i in range(NT):
                sp.wait_ge(*fc.norm.ln.at(i + 1))
                sp.dma_start(out_v[:, i, :], X[:, i, :]).then_inc(s_out, 16)
            sp.wait_ge(s_out, 16 * NT)

        @block.gpsimd
        def _(pool):
            pool.memset(half[:, :], -0.5).then_inc(s_half, 1)
            pool.wait_ge(s_cst, 16)
            a0.pool_zero(pool)
            pool.wait_ge(s_half, 1)
            pool.wait_ge(s_x, 16)
            pool.wait_ge(s_b, 16 * NB)
            for i in range(NT):
                pool.tensor_tensor(XR[:, i, :], X[:, i, :], rowb[:, 1, :], ALU.add).then_inc(a0.res_sem.sem, 1)
            pool.wait_ge(s_m, 16 * 5)
            pool.tensor_scalar(mk[:, :, :], mki[:, :, :], 0.0, 1.0, ALU.is_equal, ALU.subtract).then_inc(s_mk0, 1)
            pool.wait_ge(s_mk0, 1)
            pool.tensor_scalar(mk[:, :, :], mk[:, :, :], -1.0, None, ALU.mult).then_inc(s_mk0, 1)
            pool.wait_ge(s_mk0, 2)
            pool.tensor_scalar(mrb[:, :, :], mri[:, :, :], 0.0, None, ALU.is_equal).then_inc(s_mk, 1)
            a0.pool(pool)
            a1.pool(pool)
            moe.pool(pool)
            wide.pool(pool)
            pool.wait_ge(*wide.norm.xev.at(NT))
            a2.pool_zero(pool)
            a2.pool(pool)
            fc.pool(pool)

        @block.scalar
        def _(act):
            start_copies(act, 0)
            act.wait_ge(s_b, 16 * NB)
            a0.act(act)
            a1.act(act)
            moe.act(act)
            wide.act(act)
            a2.act(act)
            act.wait_ge(s_fc, 64)
            act.wait_ge(s_half, 1)
            fc.act(act)

        @block.vector
        def _(dve):
            dve.wait_ge(s_cst, 16)
            dve.tensor_copy(idb[:, :], ident).then_inc(s_bf, 1)
            dve.tensor_copy(caus[:, :], cst[:, C_CAUSAL:C_CAUSAL + SEQ]).then_inc(s_bf, 1)
            dve.wait_ge(s_bf, 2)
            dve.tensor_copy(fills[:, :, :], cst[0:6, C_FILL0:C_FILL0 + 2 * P].rearrange("p (l q) -> p l q", l=2))\
               .then_inc(s_bfc, 1)
            start_copies(dve, 1)
            a0.dve(dve)
            a1.dve(dve)
            moe.dve(dve)
            wide.dve(dve)
            a2.dve(dve)
            fc.dve(dve)

        @block.tensor
        def _(pe):
            start_pe(pe)
            a0.pe(pe)
            a1.pe(pe)
            moe.pe(pe)
            wide.pe(pe)
            a2.pe(pe)
            fc.pe(pe)


def kernel(**inputs):
    import concourse.bacc as _bacc
    from concourse.bass_utils import run_bass_kernel_spmd as _run

    nc = _bacc.Bacc("TRN2", target_bir_lowering=False, num_devices=1)
    arrays, args = {}, {}
    for name in inputs:
        a = np.ascontiguousarray(inputs[name])
        arrays[f"in_{name}_dram"] = a
        args[name] = nc.dram_tensor(f"in_{name}_dram", a.shape, mybir.dt.from_np(a.dtype), kind="ExternalInput").ap()
    out = nc.dram_tensor("out_0_dram", (BATCH, SEQ, P), F32, kind="ExternalOutput").ap()
    decoder_kernel(nc, args, out)
    r = _run(nc, [arrays], core_ids=[0])
    return r.results[0]["out_0_dram"]
```

```python
from contextlib import ExitStack

import numpy as np

import concourse.bass as bass
from concourse import mybir

F32 = mybir.dt.float32
BF16 = mybir.dt.bfloat16
F32R = mybir.dt.float32r
I32 = mybir.dt.int32
U32 = mybir.dt.uint32
ALU = mybir.AluOpType
ACT = mybir.ActivationFunctionType
AX = mybir.AxisListType

P = 128
BATCH, SEQ = 16, 64
NT = BATCH * SEQ // P
HEADS = 16
DH = 8
DW = 64
PAIRS = HEADS // 2
EXPERTS, INNER = 8, 512
CH = INNER // P
BANK = 512
LN_EPS = 1e-5

C_ID, C_COS, C_SIN, C_HEAD, C_CAUSAL, C_IOTA, C_FILL0, C_FILL1, C_ONES, C_HALF, C_END = (
    0, 128, 192, 256, 264, 328, 336, 464, 592, 720, 722)
CAUSAL_FILL = -(2.0 ** 100)


def bf16_parts(value):
    parts, rest = [], np.float32(value)
    for _ in range(3):
        bits = np.array(rest, np.float32).view(np.uint32)
        part = np.array(bits & np.uint32(0xFFFF0000), np.uint32).view(np.float32)
        parts.append(float(part))
        rest = np.float32(rest - part)
    assert float(rest) == 0.0
    return parts


def constants():
    c = np.zeros((P, C_END), np.float32)
    c[:, C_ID:C_ID + P] = np.eye(P)
    d = np.arange(P) % DH
    theta = np.power(np.float32(10000.0), (np.float32(-2.0) * (d // 2).astype(np.float32) / np.float32(DH)).astype(np.float32))
    angle = theta[:, None].astype(np.float32) * np.arange(SEQ, dtype=np.float32)[None, :]
    c[:, C_COS:C_COS + SEQ] = np.cos(angle)
    c[:, C_SIN:C_SIN + SEQ] = np.sin(angle) * np.where(d % 2 == 0, -1.0, 1.0)[:, None]
    c[:, C_HEAD:C_HEAD + 8] = (np.arange(P)[:, None] % 64) // DH == np.arange(8)[None, :]
    c[:, C_CAUSAL:C_CAUSAL + SEQ] = np.where(np.arange(SEQ)[None, :] > np.arange(P)[:, None] % SEQ, CAUSAL_FILL, 0.0)
    c[:, C_IOTA:C_IOTA + 8] = np.arange(8)[None, :]
    for col, fill in ((C_FILL0, -1e9), (C_FILL1, -1e12)):
        for j, part in enumerate(bf16_parts(fill * np.sqrt(DH))):
            for b in range(2):
                c[2 * j + b, col + SEQ * b:col + SEQ * (b + 1)] = part
    c[:, C_ONES:C_ONES + P] = 1.0
    c[:, C_HALF:C_HALF + 2] = np.arange(P)[:, None] // 64 == np.arange(2)[None, :]
    return c


def decoder_kernel(nc, A, out):
    with ExitStack() as ctx:
        def sb(name, shape, dt=F32):
            return ctx.enter_context(nc.sbuf_tensor(name, shape, dt))

        def sem(name):
            return ctx.enter_context(nc.semaphore(name))

        running = {}

        class Mark:

            def __init__(self, name, total=0):
                if name not in running:
                    running[name] = [sem(name), 0]
                self.sem, self.base = running[name]
                running[name][1] += total

            def at(self, n):
                return self.sem, self.base + n

        def bc(ap, axis, n):
            shape = list(ap.shape)
            shape.insert(axis, n)
            return ap.unsqueeze(axis).to_broadcast(shape)

        table = nc.inline_tensor(constants(), "shape_constants").ap()
        PS = ctx.enter_context(nc.psum_tensor("banks", [P, 8, BANK], F32))
        B_S, B_PT, B_Y, B_OX, B_K, B_Q = 0, 2, 4, 5, 6, 7
        cst = sb("cst", [P, C_END])
        X = sb("X", [P, NT, P])
        XR = sb("XR", [P, NT, P])
        XT = sb("XT", [P, NT * P])
        CT = sb("CT", [P, NT * P])
        WT = sb("WT", [P, 12, P])
        PR = sb("PR", [P, 2, HEADS * SEQ])
        PT = sb("PT", [P, 2, PAIRS, P])
        WQKV = sb("WQKV", [P, 3 * HEADS * DW])
        WOUT = sb("WOUT", [P, PAIRS, P])
        FCW = sb("FCW", [P, 2, CH, P])
        FCT = sb("FCT", [P, 2, CH, P])
        lnwb = sb("lnwb", [P, 2, CH])
        gw = sb("gw", [8, P])
        gwT = sb("gwT", [P, 8])
        qkb = sb("qkb", [P, 2, 2, 2])
        bvc = sb("bvc", [P, 2])
        rowb = sb("rowb", [P, 2, P])
        mk = sb("mk", [P, NT, SEQ])
        mrb = sb("mrb", [6, NT, SEQ], BF16)
        idb = sb("idb", [P, P], BF16)
        caus = sb("caus", [P, SEQ], BF16)
        fills = sb("fills", [6, 2, P], BF16)
        QS = sb("QS", [P, 3, 2, P])
        TMP = sb("TMP", [P, 2, 4, SEQ])
        TC = sb("TC", [P, 2, 4, SEQ])
        TS = sb("TS", [P, 2, 4, SEQ])
        KT = sb("KT", [P, 2, 2, SEQ])
        KB = sb("KB", [P, 2, 2, 8, SEQ])
        VB = sb("VB", [P, 3, PAIRS, 2, 2, DH + 1])
        mx = sb("mx", [P, 2, HEADS])
        rs = sb("rs", [P, 2, HEADS])
        ysb = sb("ysb", [P, 2, P])
        yT = sb("yT", [P, 2, P])
        R = sb("R", [P, 2, P])
        stats = sb("stats", [P, 2, 6])
        mv = sb("mv", [P, 2, 2])
        ve = sb("ve", [P, 2, 1])
        rstd = sb("rstd", [P, 2, 1])
        hst = sb("hst", [P, 2, 16])
        half = sb("half", [P, 1])
        lg = sb("lg", [P, NT, 8])
        top = sb("top", [P, NT, 8])
        topi = sb("topi", [P, NT, 8], U32)
        topf = sb("topf", [P, NT, 2])
        pk = sb("pk", [P, 4, NT])
        comb = sb("comb", [P, 2, NT, EXPERTS])
        gam = sb("gam", [P, 8])
        U = sb("U", [P, 10240])
        XS = sb("XS", [P, 2, NT * P], F32R)
        WS = sb("WS", [P, 2, 3, 2, BANK], F32R)
        HS = sb("HS", [P, 2, 2, CH, BANK], F32R)
        ident = cst[:, C_ID:C_ID + P]

        def region(start, size, pattern=None, **k):
            v = U[:, start:start + size]
            return v.rearrange(pattern, **k) if pattern else v

        RAWW = region(0, 1536, "p (w f) -> p w f", w=12)
        CTXR = region(1536, 1024, "p (t f) -> p t f", t=NT)
        mki = region(2560, 512).bitcast(I32).rearrange("p (t k) -> p t k", t=NT)
        mri = U[0:6, 3072:3584].bitcast(I32).rearrange("p (t k) -> p t k", t=NT)
        RAW = region(4096, 6144, "p (n w i) -> p n w i", n=4, w=3)
        SG = PR[:, 0, :].rearrange("p (k t) -> p k t", k=2)
        HF = PR[:, 1, :].rearrange("p (k t) -> p k t", k=2)
        YE = PT[:, 1].rearrange("p r q -> p (r q)")[:, 0:BANK]
        FA = PT[:, 0].rearrange("p (n c) q -> p n (c q)", n=2)
        QK = region(0, 4096, "p (n c u t) -> p n c u t", n=2, c=2, u=PAIRS)
        VW = region(4096, 6144, "p (n b u a d) -> p n b u a d", n=3, b=2, u=PAIRS, a=2)
        YW = [XR, WT[:, 0:PAIRS, :]]
        FH = region(0, 1024, "p (n i) -> p n i", n=2)
        FN = region(1024, 1024, "p (n i) -> p n i", n=2)
        FT = region(2048, 1024, "p (n c t) -> p n c t", n=2, c=CH)

        s_cst = sem("cst_loaded")
        s_x = sem("x_loaded")
        s_ctx = sem("ctx_loaded")
        s_w0 = sem("first_weights_loaded")
        s_w = sem("later_weights_loaded")
        s_b = sem("biases_loaded")
        s_m = sem("masks_loaded")
        s_raw = [sem("expert_weights_loaded_%d" % n) for n in range(4)]
        s_wide = sem("wide_weights_loaded")
        s_fc = sem("ternary_weights_loaded")
        s_half = sem("minus_half_set")
        s_mk0 = sem("masks_started")
        s_mk = sem("masks_made")
        s_bf = sem("bf16_identity_made")
        s_bfc = sem("bf16_constants_made")
        s_z = sem("blocks_zeroed")
        s_wz = sem("wide_blocks_zeroed")
        s_tern = sem("ternary_weights_made")
        s_out = sem("output_stored")

        WNAMES = ["L0_attn_wq", "L0_attn_wk", "L0_attn_wv", "L0_attn_wp",
                  "L0_xattn_Wq", "L0_xattn_Wk", "L0_xattn_Wv", "L0_xattn_Wo",
                  "L1_xattn_Wq", "L1_xattn_Wk", "L1_xattn_Wv", "L1_xattn_Wo"]
        block = ctx.enter_context(nc.Block())

        class Transposes:

            def __init__(self, name, groups, banks):
                self.groups, self.banks = groups, banks
                self.mm, self.copied = sem(name + "_transposed"), [sem(name + "_copied_act"), sem(name + "_copied_dve")]

            def pe(self, pe, some=None):
                for g in some or range(len(self.groups)):
                    waits, blocks, _ = self.groups[g]
                    for s, v in waits:
                        pe.wait_ge(s, v)
                    last = g - len(self.banks)
                    if last >= 0:
                        pe.wait_ge(self.copied[last % 2], last // 2 + 1)
                    bank = self.banks[g % len(self.banks)]
                    for n, (src, k) in enumerate(blocks):
                        m = pe.transpose(PS[:, bank, n * P:n * P + k], src, ident[0:k, 0:k])
                    m.then_inc(self.mm, 1)

            def copies(self, eng, part, some=None):
                for g in some or range(len(self.groups)):
                    if g % 2 != part:
                        continue
                    _, blocks, dst = self.groups[g]
                    eng.wait_ge(self.mm, g + 1)
                    src = PS[:, self.banks[g % len(self.banks)], 0:sum(k for _, k in blocks)]
                    if part == 0:
                        eng.activation(dst, src, ACT.Copy).then_inc(self.copied[0], 1)
                    else:
                        eng.tensor_copy(dst, src).then_inc(self.copied[1], 1)

            def done(self, eng, n=None):
                n = len(self.groups) if n is None else n
                eng.wait_ge(self.copied[0], (n + 1) // 2)
                if n > 1:
                    eng.wait_ge(self.copied[1], n // 2)

        def x_group(g):
            return ([(s_cst, 16), (s_x, 16)], [(X[:, 4 * g + j, :], P) for j in range(4)], XT[:, BANK * g:BANK * (g + 1)])

        def w_group(g):
            return ([(s_w, 16 * 9)] if g else [(s_w0, 16 * 4)], [(RAWW[:, 4 * g + j, :], P) for j in range(4)],
                    WT[:, 4 * g:4 * g + 4, :].rearrange("p w f -> p (w f)"))

        def c_group(g):
            return ([(s_ctx, 16)], [(CTXR[:, 4 * g + j, :], P) for j in range(4)], CT[:, BANK * g:BANK * (g + 1)])

        first = Transposes("first", [x_group(0), w_group(0), x_group(1)], [0, 1, 2])
        later = Transposes("later", [c_group(0), c_group(1), w_group(1), w_group(2),
                                      ([], [(gw[:, :], 8)], gwT[:, :])], [3, 4, 5, 0])
        fct = Transposes("ternary", [([(s_tern, 1 + n)], [(FCW[:, n, c, :], P) for c in range(CH)],
                                      FCT[:, n, :, :].rearrange("p c f -> p (c f)")) for n in range(2)], [6, 7])

        class Norm:

            def __init__(self, name):
                self.r = Mark("residual_summed", 0 if name == "experts" else NT)
                self.st = Mark("stats_made", NT)
                self.mv = Mark("variance_made", NT)
                self.ve = Mark("eps_added", NT)
                self.rstd = Mark("rstd_made", NT)
                self.ln = Mark("normed", NT)
                self.xmm = Mark("x_transposed", NT)
                self.xev = Mark("xT_copied", NT)
                self.xr = Mark("bias_added", NT)

            def stats(self, dve, i, src):
                dve.bn_stats(stats[:, i % 2, :], src).then_inc(self.st.sem, 1)
                dve.wait_ge(*self.st.at(i + 1))
                dve.bn_aggr(mv[:, i % 2, :], stats[:, i % 2, :]).then_inc(self.mv.sem, 1)

            def rsqrt(self, pool, i):
                pool.wait_ge(*self.mv.at(i + 1))
                pool.tensor_scalar(ve[:, i % 2, :], mv[:, i % 2, 1:2], LN_EPS, None, ALU.add).then_inc(self.ve.sem, 1)
                pool.wait_ge(*self.ve.at(i + 1))
                pool.tensor_tensor(rstd[:, i % 2, :], ve[:, i % 2, :], half[:, :], ALU.pow).then_inc(self.rstd.sem, 1)

            def apply(self, dve, i, src):
                dve.wait_ge(*self.rstd.at(i + 1))
                dve.tensor_scalar(X[:, i, :], src, mv[:, i % 2, 0:1], rstd[:, i % 2, :],
                                  ALU.subtract, ALU.mult).then_inc(self.ln.sem, 1)
                dve.wait_ge(*self.ln.at(i + 1))

        class Stage:

            def none(self, eng, job):
                pass

            qk_pe = qkw_pe = v_pe = s_pe = t_pe = va_pe = vb_pe = y_pe = o_pe = x_pe = none
            qk_act = v_act = pt_act = y_act = exp_act = x_act = ya_act = yb_act = wide_act = none
            y_dve = sum_dve = max_dve = qk_dve = wide_dve = none
            blocks_pool = cos_pool = norm_pool = hidden_pool = bias_pool = none
            wide = False

            def qkw_copies(self, eng, part, job):
                pass

            vw_copies = qkw_copies

            def x_pe(self, pe, job):
                i = job.i
                pe.wait_ge(*self.norm.ln.at(i + 1))
                if i + 1 < NT:
                    pe.wait_ge(*self.norm.r.at(i + 2))
                elif job.after is not None:
                    pe.wait_ge(*job.after.stage.norm.r.at(1))
                if i >= 1:
                    pe.wait_ge(*self.norm.xev.at(i))
                pe.transpose(PS[:, B_OX, 2 * P:3 * P], X[:, i, :], ident).then_inc(self.norm.xmm.sem, 1)

            def x_act(self, act, job):
                i = job.i
                act.wait_ge(*self.norm.xmm.at(i + 1))
                act.activation(XT[:, i * P:(i + 1) * P], PS[:, B_OX, 2 * P:3 * P], ACT.Copy).then_inc(self.norm.xev.sem, 1)

            def r_dve(self, dve, job):
                i = job.i
                dve.wait_ge(*self.o_mm.at(i + 1))
                res = X
                if self.row is not None:
                    res = XR
                    dve.wait_ge(*self.res.at(i + 1))
                dve.tensor_tensor(R[:, i % 2, :], PS[:, B_OX, P:2 * P], res[:, i, :], ALU.add).then_inc(self.norm.r.sem, 1)
                dve.wait_ge(*self.norm.r.at(i + 1))
                self.norm.stats(dve, i, R[:, i % 2, :])

            def ln_dve(self, dve, job):
                self.norm.apply(dve, job.i, R[:, job.i % 2, :])

            def rsqrt_pool(self, pool, job):
                self.norm.rsqrt(pool, job.i)

            def max_dve(self, dve, job):
                i, n = job.i, job.n
                dve.wait_ge(*self.s_mm.at(i + 1))
                s = PS[:, B_S:B_S + 2, :].rearrange("q g (h k) -> q (g h) k", k=SEQ)
                dve.tensor_reduce(mx[:, n % 2, :], s, AX.X, ALU.max).then_inc(self.max.sem, 1)
                dve.wait_ge(*self.max.at(i + 1))
                if job.ago(2):
                    dve.wait_ge(*job.ago(2).p_used())
                if self.wide:
                    o = PR[:, n % 2, :].rearrange("q (u a k) -> q a u k", a=2, k=SEQ)
                    dve.tensor_tensor(o, s.rearrange("q (a u) k -> q a u k", a=2),
                                      bc(mx[:, n % 2, :].rearrange("q (a u) -> q a u", a=2), 3, SEQ),
                                      ALU.subtract).then_inc(self.sub.sem, 1)
                else:
                    dve.tensor_tensor(PR[:, n % 2, :].rearrange("q (h k) -> q h k", k=SEQ), s,
                                      bc(mx[:, n % 2, :], 2, SEQ), ALU.subtract).then_inc(self.sub.sem, 1)

            def exp_act(self, act, job):
                act.wait_ge(*self.sub.at(job.i + 1))
                p = PR[:, job.n % 2, :]
                act.activation(p, p, ACT.Exp, scale=self.scale).then_inc(self.exp.sem, 1)

            def t_pe(self, pe, job):
                i, n = job.i, job.n
                pe.wait_ge(*(self.pn if self.wide else self.exp).at(i + 1))
                for m in range(2):
                    if job.before:
                        pe.wait_ge(*job.before.pt_read(m))
                    for r in range(4 * m, 4 * m + 4):
                        t = pe.transpose(PS[:, B_PT + m, P * (r % 4):P * (r % 4 + 1)], PR[:, n % 2, P * r:P * (r + 1)], ident)
                    t.then_inc(self.t_mm.sem, 1)

            def pt_act(self, act, job):
                i, n = job.i, job.n
                if job.ago(2):
                    act.wait_ge(*job.ago(2).pt_used())
                for m in range(2):
                    act.wait_ge(*self.t_mm.at(2 * i + m + 1))
                    act.activation(PT[:, n % 2, 4 * m:4 * m + 4, :].rearrange("p r q -> p (r q)"),
                                   PS[:, B_PT + m, :], ACT.Copy).then_inc(self.pt.sem, 1)

            def p_used(self, i):
                return self.t_mm.at(2 * i + 2)

            def pt_read(self, i, m):
                return self.pt.at(2 * i + m + 1)

            def s_read(self, i):
                return self.sub.at(i + 1)

        class Narrow(Stage):

            def __init__(self, name, w, src, rope=False, bias=None, fill=None, row=None, next_row=None):
                self.w, self.src, self.rope, self.bias, self.fill = w, src, rope, bias, fill
                self.row, self.next_row, self.scale = row, next_row, float(DH) ** -0.5
                r = NT if rope else 0
                self.k_mm, self.q_mm, self.v_mm = Mark("k_projected", NT), Mark("q_projected", NT), Mark("v_projected", NT)
                self.tmpk, self.tmpq, self.cosd, self.shuf, self.sind = (
                    Mark("k_copied", r), Mark("q_copied", r), Mark("times_cos", r), Mark("pairs_swapped", r), Mark("times_sin", r))
                self.k_ready, self.q_ready, self.v_ready = Mark("k_ready", NT), Mark("q_ready", NT), Mark("v_ready", NT)
                self.kb, self.s_mm = Mark("k_blocks_made", 2 * NT), Mark("scored", NT)
                self.max, self.sub, self.exp = Mark("row_max_made", NT), Mark("max_subtracted", NT), Mark("exponentials_made", NT)
                self.t_mm, self.pt, self.pv = Mark("p_transposed", 2 * NT), Mark("pT_copied", 2 * NT), Mark("v_weighed", NT)
                self.rec, self.yn, self.y_mm = Mark("reciprocals_made", NT), Mark("y_normalized", NT), Mark("y_transposed", NT)
                self.yt, self.o_mm = Mark("yT_copied", NT), Mark("y_projected", NT)
                self.norm = Norm(name)

            def pt_used(self, i):
                return self.pv.at(i + 1)

            def y_read(self, i):
                return self.yn.at(i + 1)

            def qk_read(self, i):
                return [(self.tmpk if self.rope else self.k_ready).at(i + 1), (self.tmpq if self.rope else self.q_ready).at(i + 1)]

            def qk_pe(self, pe, job):
                i = job.i
                if self.input is not None:
                    pe.wait_ge(*self.input.xev.at(i + 1))
                if job.before:
                    for s in job.before.stage.qk_read(job.before.i):
                        pe.wait_ge(*s)
                if job.ago(3) and job.ago(3).stage.wide:
                    for s in job.ago(3).v_read():
                        pe.wait_ge(*s)
                for bank, w, src, s in ((B_K, 1, self.src, self.k_mm), (B_Q, 0, XT, self.q_mm)):
                    for g in range(2):
                        for b in range(2):
                            m = pe.matmul(PS[64 * b:64 * b + 64, bank, 64 * g:64 * g + 64],
                                          WT[:, self.w + w, 64 * g:64 * g + 64],
                                          src[:, SEQ * (2 * i + b):SEQ * (2 * i + b + 1)], start=True, stop=True)
                    m.then_inc(s.sem, 1)

            def v_pe(self, pe, job):
                i = job.i
                if job.ago(3):
                    pe.wait_ge(*job.ago(3).y_read())
                if job.before and not job.before.stage.wide:
                    for s in job.before.v_read():
                        pe.wait_ge(*s)
                for b in range(2):
                    for a in range(2):
                        m = pe.matmul(PS[64 * a:64 * a + 64, B_Y, 384 + 64 * b:448 + 64 * b],
                                      self.src[:, SEQ * (2 * i + b):SEQ * (2 * i + b + 1)],
                                      WT[:, self.w + 2, :].rearrange("f (r a d) -> f a r d", a=2, d=DH)[:, a],
                                      start=True, stop=True)
                m.then_inc(self.v_mm.sem, 1)

            def s_pe(self, pe, job):
                i, n = job.i, job.n
                pe.wait_ge(*self.q_ready.at(i + 1))
                if job.before:
                    pe.wait_ge(*job.before.s_read())
                for g in range(2):
                    pe.wait_ge(*self.kb.at(2 * i + g + 1))
                    o = PS[:, B_S + g, :]
                    pe.matmul(o, QS[:, n % 3, g, :], KB[:, n % 2, g].rearrange("p h k -> p (h k)"), start=True, stop=False)
                    o = o.rearrange("q (h k) -> q h k", h=8)
                    if self.fill is None:
                        m = pe.matmul(o, idb[:, :], bc(caus[:, :], 1, 8), start=False, stop=True)
                    else:
                        m = pe.matmul(o, fills[:, self.fill, :], bc(mrb[:, i, :], 1, 8), start=False, stop=True)
                m.then_inc(self.s_mm.sem, 1)

            def va_pe(self, pe, job):
                i, n = job.i, job.n
                pe.wait_ge(*self.pt.at(2 * i + 2))
                pe.wait_ge(*self.v_ready.at(i + 1))
                if job.after2:
                    for s in job.after2.v_read():
                        pe.wait_ge(*s)
                if job.before:
                    pe.wait_ge(*job.before.y_read())
                for r in range(PAIRS):
                    m = pe.matmul(PS[:, B_Y, 36 * r:36 * r + 36], PT[:, n % 2, r, :],
                                  VB[:, n % 3, r].rearrange("p b a e -> p (b a e)"), start=True, stop=True)
                m.then_inc(self.pv.sem, 1)

            def v_read(self, i):
                return [self.v_ready.at(i + 1)]

            def y_pe(self, pe, job):
                i, n = job.i, job.n
                pe.wait_ge(*self.yn.at(i + 1))
                if job.ago(2):
                    pe.wait_ge(*job.ago(2).x_read())
                if job.before:
                    pe.wait_ge(*job.before.r_read())
                pe.transpose(PS[:, B_OX, 0:P], ysb[:, n % 2, :], ident).then_inc(self.y_mm.sem, 1)

            def o_pe(self, pe, job):
                pe.wait_ge(*self.yt.at(job.i + 1))
                pe.matmul(PS[:, B_OX, P:2 * P], yT[:, job.n % 2, :], WT[:, self.w + 3, :],
                          start=True, stop=True).then_inc(self.o_mm.sem, 1)

            def qk_act(self, act, job):
                i, n, ab = job.i, job.n, self.bias
                if self.rope:
                    for qk, bank, s, d in ((1, B_K, self.k_mm, self.tmpk), (0, B_Q, self.q_mm, self.tmpq)):
                        act.wait_ge(*s.at(i + 1))
                        if i >= 2:
                            act.wait_ge(*self.cosd.at(i - 1))
                            act.wait_ge(*self.shuf.at(i - 1))
                        for g in range(2):
                            m = act.activation(TMP[:, n % 2, 2 * (1 - qk) + g, :], PS[:, bank, 64 * g:64 * g + 64],
                                               ACT.Identity, bias=qkb[:, ab, qk, g:g + 1])
                        m.then_inc(d.sem, 1)
                    return
                act.wait_ge(*self.q_mm.at(i + 1))
                if job.ago(3):
                    act.wait_ge(*job.ago(3).stage.s_mm.at(job.ago(3).i + 1))
                act.wait_ge(s_z, 2)
                for b in range(2):
                    rows = slice(64 * b, 64 * b + 64)
                    if ab is None:
                        m = act.activation(QS[rows, n % 3, :, 64 * b:64 * b + 64],
                                           PS[rows, B_Q, 0:P].rearrange("p (g q) -> p g q", g=2), ACT.Copy)
                    else:
                        for g in range(2):
                            m = act.activation(QS[rows, n % 3, g, 64 * b:64 * b + 64], PS[rows, B_Q, 64 * g:64 * g + 64],
                                               ACT.Identity, bias=qkb[rows, ab, 0, g:g + 1])
                m.then_inc(self.q_ready.sem, 1)

            def v_act(self, act, job):
                i, n = job.i, job.n
                act.wait_ge(*self.v_mm.at(i + 1))
                act.wait_ge(s_z, 6)
                if job.ago(3):
                    act.wait_ge(*job.ago(3).pt_used())
                for a in range(2):
                    rows = slice(64 * a, 64 * a + 64)
                    m = act.activation(VB[rows, n % 3, :, :, a, 0:DH].rearrange("p r b d -> p b r d"),
                                       PS[rows, B_Y, 384:512].rearrange("p (b r d) -> p b r d", b=2, d=DH), ACT.Copy)
                m.then_inc(self.v_ready.sem, 1)

            def y_act(self, act, job):
                i, n = job.i, job.n
                act.wait_ge(*self.y_mm.at(i + 1))
                if i >= 2:
                    act.wait_ge(*self.o_mm.at(i - 1))
                if self.bias is None:
                    m = act.activation(yT[:, n % 2, :], PS[:, B_OX, 0:P], ACT.Copy)
                else:
                    m = act.activation(yT[:, n % 2, :], PS[:, B_OX, 0:P], ACT.Identity, bias=bvc[:, self.bias:self.bias + 1])
                m.then_inc(self.yt.sem, 1)

            def qk_dve(self, dve, job):
                i, n, ab = job.i, job.n, self.bias
                if self.rope:
                    swap = [p ^ 1 for p in range(32)]
                    dve.wait_ge(*self.tmpq.at(i + 1))
                    dve.stream_shuffle(TS[:, n % 2].rearrange("p n k -> p (n k)"),
                                       TMP[:, n % 2].rearrange("p n k -> p (n k)"), swap).then_inc(self.shuf.sem, 1)
                    dve.wait_ge(*self.shuf.at(i + 1))
                    dve.tensor_tensor(TS[:, n % 2], TS[:, n % 2], bc(cst[:, C_SIN:C_SIN + SEQ], 1, 4), ALU.mult)\
                       .then_inc(self.sind.sem, 1)
                    dve.wait_ge(*self.sind.at(i + 1))
                    dve.wait_ge(*self.cosd.at(i + 1))
                    if i >= 2:
                        dve.wait_ge(*self.kb.at(2 * (i - 1)))
                    dve.tensor_tensor(KT[:, n % 2], TC[:, n % 2, 0:2], TS[:, n % 2, 0:2], ALU.add).then_inc(self.k_ready.sem, 1)
                    if i >= 3:
                        dve.wait_ge(*self.s_mm.at(i - 2))
                    dve.wait_ge(s_z, 2)
                    for b in range(2):
                        rows = slice(64 * b, 64 * b + 64)
                        m = dve.tensor_tensor(QS[rows, n % 3, :, 64 * b:64 * b + 64], TC[rows, n % 2, 2:4],
                                              TS[rows, n % 2, 2:4], ALU.add)
                    m.then_inc(self.q_ready.sem, 1)
                    return
                dve.wait_ge(s_mk, 1)
                dve.wait_ge(*self.k_mm.at(i + 1))
                if job.ago(2):
                    dve.wait_ge(*job.ago(2).kt_used())
                if ab is None:
                    m = dve.tensor_tensor(KT[:, n % 2], PS[:, B_K, 0:P].rearrange("p (g k) -> p g k", g=2),
                                          bc(mk[:, i, :], 1, 2), ALU.mult)
                else:
                    for g in range(2):
                        m = dve.scalar_tensor_tensor(KT[:, n % 2, g], PS[:, B_K, 64 * g:64 * g + 64],
                                                     qkb[:, ab, 1, g:g + 1], mk[:, i, :], ALU.add, ALU.mult)
                m.then_inc(self.k_ready.sem, 1)

            def kt_used(self, i):
                return self.kb.at(2 * i + 2)

            def y_dve(self, dve, job):
                i, n = job.i, job.n
                dve.wait_ge(*self.pv.at(i + 1))
                y = PS[:, B_Y, 0:36 * PAIRS].rearrange("q (r b a e) -> q b r a e", b=2, a=2, e=DH + 1)
                for b in range(2):
                    rows = slice(64 * b, 64 * b + 64)
                    m = dve.reciprocal(rs[rows, n % 2, :].rearrange("q (r a) -> q r a", a=2), y[rows, b, :, :, DH])
                m.then_inc(self.rec.sem, 1)
                dve.wait_ge(*self.rec.at(i + 1))
                if i >= 2:
                    dve.wait_ge(*self.y_mm.at(i - 1))
                for b in range(2):
                    rows = slice(64 * b, 64 * b + 64)
                    m = dve.tensor_tensor(ysb[rows, n % 2, :].rearrange("q (r a d) -> q r a d", a=2, d=DH), y[rows, b, :, :, 0:DH],
                                          bc(rs[rows, n % 2, :].rearrange("q (r a) -> q r a", a=2), 3, DH), ALU.mult)
                m.then_inc(self.yn.sem, 1)

            def blocks_pool(self, pool, job):
                i, n = job.i, job.n
                pool.wait_ge(*self.k_ready.at(i + 1))
                if job.ago(2):
                    pool.wait_ge(*job.ago(2).kb_used())
                for g in range(2):
                    pool.tensor_tensor(KB[:, n % 2, g], bc(KT[:, n % 2, g, :], 1, 8),
                                       bc(cst[:, C_HEAD:C_HEAD + 8], 2, SEQ), ALU.mult).then_inc(self.kb.sem, 1)

            def kb_used(self, i):
                return self.s_mm.at(i + 1)

            def cos_pool(self, pool, job):
                if self.rope:
                    i, n = job.i, job.n
                    pool.wait_ge(*self.tmpq.at(i + 1))
                    if i >= 2:
                        pool.wait_ge(*self.q_ready.at(i - 1))
                    pool.tensor_tensor(TC[:, n % 2], TMP[:, n % 2], bc(cst[:, C_COS:C_COS + SEQ], 1, 4), ALU.mult)\
                        .then_inc(self.cosd.sem, 1)

            def bias_pool(self, pool, job):
                if self.next_row is not None:
                    i = job.i
                    pool.wait_ge(*self.norm.ln.at(i + 1))
                    pool.tensor_tensor(XR[:, i, :], X[:, i, :], rowb[:, self.next_row, :], ALU.add).then_inc(self.norm.xr.sem, 1)

        class Wide(Stage):
            wide = True

            def __init__(self, name):
                self.scale, self.row = float(DW) ** -0.5, None
                self.f_mm, self.f_act, self.f_dve = Mark("wide_projected"), Mark("wide_copied_act"), Mark("wide_copied_dve")
                self.s_mm = Mark("scored", NT)
                self.max, self.sub, self.exp = Mark("row_max_made", NT), Mark("max_subtracted", NT), Mark("exponentials_made", NT)
                self.sum, self.rec, self.pn = Mark("wide_summed", NT), Mark("reciprocals_made", NT), Mark("wide_p_normalized", NT)
                self.t_mm, self.pt, self.pv = Mark("p_transposed", 2 * NT), Mark("pT_copied", 2 * NT), Mark("v_weighed", 2 * NT)
                self.yt, self.o_mm = Mark("yT_copied", 2 * NT), Mark("y_projected", NT)
                self.norm = Norm(name)

            def pt_used(self, i):
                return self.pv.at(2 * i + 2)

            def y_read(self, i):
                return self.yt.at(2 * i + 2)

            def kt_used(self, i):
                return self.s_mm.at(i + 1)

            kb_used = kt_used

            def v_read(self, i):
                return self.fills_read(self.v_fill(i) + 1)

            def fills_read(self, f):
                return [self.f_act.at(f // 2 + 1), self.f_dve.at((f + 1) // 2)]

            def qk_read(self, i):
                return self.fills_read(self.qk_fill(i) + 3)

            def qk_fill(self, i):
                return 6 * i - 2 if i else 0

            def v_fill(self, i):
                return 6 * i + 8 if i < NT - 1 else 6 * NT - 2

            def fill(self, pe, f):
                if f >= 2:
                    pe.wait_ge(*self.fills_read(f - 2)[f % 2])
                return B_K + f % 2

            def qkw_pe(self, pe, job):
                i = job.i
                pe.wait_ge(*self.input.xev.at(i + 1))
                if i == 0:
                    pe.wait_ge(s_wide, 32)
                w = WQKV[:, :].rearrange("f (m c) -> f c m", c=3)
                for f in range(4):
                    bank = self.fill(pe, self.qk_fill(i) + f)
                    for k in range(4):
                        u = 4 * (f % 2) + k
                        m = pe.matmul(PS[:, bank, P * k:P * (k + 1)], w[:, f // 2, P * u:P * (u + 1)],
                                      XT[:, P * i:P * (i + 1)], start=True, stop=True)
                    m.then_inc(self.f_mm.sem, 1)

            def v_pe(self, pe, job):
                i = job.i
                w = WQKV[:, :].rearrange("f (u a d c) -> f c a u d", c=3, a=2, d=DW)
                for b in range(2):
                    bank = self.fill(pe, self.v_fill(i) + b)
                    if b == 0 and job.after2_any and not job.after2_any.stage.wide:
                        for s in job.after2_any.stage.qk_read(job.after2_any.i):
                            pe.wait_ge(*s)
                    for a in range(2):
                        m = pe.matmul(PS[64 * a:64 * a + 64, bank, :], XT[:, SEQ * (2 * i + b):SEQ * (2 * i + b + 1)],
                                      w[:, 2, a], start=True, stop=True)
                    m.then_inc(self.f_mm.sem, 1)

            def s_pe(self, pe, job):
                i, n = job.i, job.n
                for s in self.fills_read(self.qk_fill(i) + 3):
                    pe.wait_ge(*s)
                if job.before:
                    pe.wait_ge(*job.before.s_read())
                for a in range(2):
                    rows = slice(64 * a, 64 * a + 64)
                    for b in range(2):
                        for u in range(PAIRS):
                            m = pe.matmul(PS[64 * b:64 * b + 64, B_S + a, SEQ * u:SEQ * (u + 1)],
                                          QK[rows, n % 2, 0, u, 64 * b:64 * b + 64], QK[rows, n % 2, 1, u, 64 * b:64 * b + 64],
                                          start=True, stop=True)
                m.then_inc(self.s_mm.sem, 1)

            def weigh(self, pe, job, m):
                i, n = job.i, job.n
                pe.wait_ge(*self.pt.at(2 * i + 2))
                for s in self.v_read(i):
                    pe.wait_ge(*s)
                if m == 1:
                    pe.wait_ge(*self.yt.at(2 * i + 1))
                else:
                    if job.after2:
                        for s in job.after2.v_read():
                            pe.wait_ge(*s)
                    if job.before:
                        pe.wait_ge(*job.before.y_read())
                for r in range(4 * m, 4 * m + 4):
                    for b in range(2):
                        t = pe.matmul(PS[:, B_Y, P * (r % 4) + 64 * b:P * (r % 4) + 64 * b + 64],
                                      VW[:, n % 3, b, r].rearrange("p a d -> p (a d)"),
                                      PT[:, n % 2, r, 64 * b:64 * b + 64], start=True, stop=True)
                t.then_inc(self.pv.sem, 1)

            def va_pe(self, pe, job):
                self.weigh(pe, job, 0)

            def vb_pe(self, pe, job):
                self.weigh(pe, job, 1)

            def o_pe(self, pe, job):
                i, n = job.i, job.n
                pe.wait_ge(*self.yt.at(2 * i + 2))
                if job.before:
                    pe.wait_ge(*job.before.r_read())
                if job.ago(2):
                    pe.wait_ge(*job.ago(2).x_read())
                for u in range(PAIRS):
                    m = pe.matmul(PS[:, B_OX, P:2 * P], YW[n % 2][:, u, :], WOUT[:, u, :],
                                  start=(u == 0), stop=(u == PAIRS - 1))
                m.then_inc(self.o_mm.sem, 1)

            def copy(self, eng, part, o, s):
                return eng.activation(o, s, ACT.Copy) if part == 0 else eng.tensor_copy(o, s)

            def qkw_copies(self, eng, part, job):
                i, n = job.i, job.n
                if i >= 2:
                    eng.wait_ge(*self.s_mm.at(i - 1))
                for c in range(2):
                    f = self.qk_fill(i) + 2 * c + part
                    eng.wait_ge(*self.f_mm.at(f + 1))
                    self.copy(eng, part, QK[:, n % 2, c, 4 * part:4 * part + 4, :].rearrange("p u t -> p (u t)"),
                              PS[:, B_K + part, :]).then_inc((self.f_act, self.f_dve)[part].sem, 1)

            def vw_copies(self, eng, part, job):
                i, n = job.i, job.n
                if i >= 3:
                    eng.wait_ge(*self.pv.at(2 * (i - 2)))
                eng.wait_ge(s_wz, 1)
                eng.wait_ge(*self.f_mm.at(self.v_fill(i) + part + 1))
                for a in range(2):
                    rows = slice(64 * a, 64 * a + 64)
                    m = self.copy(eng, part, VW[rows, n % 3, part, :, a, :],
                                  PS[rows, B_K + part, :].rearrange("p (u d) -> p u d", d=DW))
                m.then_inc((self.f_act, self.f_dve)[part].sem, 1)

            def ya_act(self, act, job, m=0):
                i, n = job.i, job.n
                act.wait_ge(*self.pv.at(2 * i + m + 1))
                if i >= 2:
                    act.wait_ge(*self.o_mm.at(i - 1))
                act.activation(YW[n % 2][:, 4 * m:4 * m + 4, :].rearrange("p u q -> p (u q)"),
                               PS[:, B_Y, :], ACT.Copy).then_inc(self.yt.sem, 1)

            def yb_act(self, act, job):
                self.ya_act(act, job, 1)

            def sum_dve(self, dve, job):
                i, n = job.i, job.n
                dve.wait_ge(*self.exp.at(i + 1))
                s = PR[:, n % 2, :].rearrange("q (h k) -> q h k", k=SEQ)
                dve.tensor_reduce(mx[:, n % 2, :], s, AX.X, ALU.add).then_inc(self.sum.sem, 1)
                dve.wait_ge(*self.sum.at(i + 1))
                if i >= 2:
                    dve.wait_ge(*self.pn.at(i - 1))
                dve.reciprocal(rs[:, n % 2, :], mx[:, n % 2, :]).then_inc(self.rec.sem, 1)

            def norm_pool(self, pool, job):
                i, n = job.i, job.n
                pool.wait_ge(*self.rec.at(i + 1))
                s = PR[:, n % 2, :].rearrange("q (h k) -> q h k", k=SEQ)
                pool.tensor_tensor(s, s, bc(rs[:, n % 2, :], 2, SEQ), ALU.mult).then_inc(self.pn.sem, 1)

        class Ternary(Stage):
            def __init__(self, name):
                self.row = None
                self.abs, self.gsum, self.thr, self.low = (
                    Mark("magnitudes_summed"), Mark("magnitude_totals_made"), Mark("thresholds_made"), Mark("negatives_found"))
                self.h_mm, self.gelu, self.st, self.mv = (
                    Mark("hidden_projected"), Mark("gelu_made"), Mark("hidden_stats_made"), Mark("hidden_variance_made"))
                self.ve, self.rstd, self.n = Mark("hidden_eps_added"), Mark("hidden_rstd_made"), Mark("hidden_normed")
                self.t_mm, self.ht, self.o_mm = Mark("hidden_transposed"), Mark("hiddenT_copied"), Mark("ternary_projected")
                self.norm = Norm(name)

            def s_read(self, i):
                return self.gelu.at(i + 1)

            def magnitudes(self, dve):
                dve.wait_ge(s_fc, 64)
                for n in range(2):
                    dve.tensor_reduce(gam[:, n:n + 1], FCW[:, n].rearrange("p c f -> p (c f)"), AX.X, ALU.add,
                                      apply_absolute_value=True).then_inc(self.abs.sem, 1)

            def totals(self, pe, bank_read):
                pe.wait_ge(*bank_read)
                pe.wait_ge(*self.abs.at(2))
                pe.matmul(PS[:, 6, 0:2], cst[:, C_ONES:C_ONES + P], gam[:, 0:2], start=True, stop=True)\
                    .then_inc(self.gsum.sem, 1)

            def quantize(self, dve):
                dve.wait_ge(*self.gsum.at(1))
                for s in (0.5, -0.5):
                    k = 2 if s > 0 else 4
                    dve.tensor_scalar(gam[:, k:k + 2], PS[:, 6, 0:2], s / (P * INNER), s * 1e-6, ALU.mult, ALU.add)\
                       .then_inc(self.thr.sem, 1)
                dve.wait_ge(*self.thr.at(2))
                for n in range(2):
                    w = FCW[:, n].rearrange("p c f -> p (c f)")
                    dve.tensor_scalar(FA[:, n, :], w, gam[:, 4 + n:5 + n], None, ALU.is_lt).then_inc(self.low.sem, 1)
                dve.wait_ge(*self.low.at(2))
                for n in range(2):
                    w = FCW[:, n].rearrange("p c f -> p (c f)")
                    dve.scalar_tensor_tensor(w, w, gam[:, 2 + n:3 + n], FA[:, n, :], ALU.is_gt, ALU.subtract)\
                       .then_inc(s_tern, 1)

            def s_pe(self, pe, job):
                i = job.i
                pe.wait_ge(*self.input.xev.at(i + 1))
                if job.before:
                    pe.wait_ge(*job.before.s_read())
                pe.matmul(PS[:, B_S, :], XT[:, P * i:P * (i + 1)], FCT[:, 0].rearrange("p c f -> p (c f)"),
                          start=True, stop=True).then_inc(self.h_mm.sem, 1)

            def t_pe(self, pe, job):
                pass

            def pt_act(self, act, job):
                pass

            def max_dve(self, dve, job):
                pass

            def exp_act(self, act, job):
                i = job.i
                act.wait_ge(*self.h_mm.at(i + 1))
                if i >= 2:
                    act.wait_ge(*self.n.at(i - 1))
                act.activation(FH[:, i % 2, :], PS[:, B_S, :], ACT.Gelu).then_inc(self.gelu.sem, 1)

            def sum_dve(self, dve, job):
                i = job.i
                dve.wait_ge(*self.gelu.at(i + 1))
                dve.bn_stats(hst[:, i % 2, 0:6], FH[:, i % 2, :]).then_inc(self.st.sem, 1)
                dve.wait_ge(*self.st.at(i + 1))
                dve.bn_aggr(hst[:, i % 2, 8:10], hst[:, i % 2, 0:6]).then_inc(self.mv.sem, 1)

            def hidden_pool(self, pool, job):
                i = job.i
                pool.wait_ge(*self.mv.at(i + 1))
                pool.tensor_scalar(hst[:, i % 2, 12:13], hst[:, i % 2, 9:10], LN_EPS, None, ALU.add).then_inc(self.ve.sem, 1)
                pool.wait_ge(*self.ve.at(i + 1))
                pool.tensor_tensor(hst[:, i % 2, 13:14], hst[:, i % 2, 12:13], half[:, :], ALU.pow).then_inc(self.rstd.sem, 1)

            def hidden_dve(self, dve, job):
                i = job.i
                dve.wait_ge(*self.rstd.at(i + 1))
                if i >= 2:
                    dve.wait_ge(*self.t_mm.at(i - 1))
                dve.tensor_scalar(FN[:, i % 2, :], FH[:, i % 2, :], hst[:, i % 2, 8:9], hst[:, i % 2, 13:14],
                                  ALU.subtract, ALU.mult).then_inc(self.n.sem, 1)
                dve.wait_ge(*self.n.at(i + 1))

            def va_pe(self, pe, job):
                i = job.i
                pe.wait_ge(*self.n.at(i + 1))
                if i >= 1:
                    pe.wait_ge(*self.ht.at(i))
                elif job.before:
                    pe.wait_ge(*job.before.pt_read(0))
                for c in range(CH):
                    m = pe.transpose(PS[:, B_PT, P * c:P * (c + 1)], FN[:, i % 2, P * c:P * (c + 1)], ident)
                m.then_inc(self.t_mm.sem, 1)

            def ya_act(self, act, job):
                i = job.i
                act.wait_ge(*self.t_mm.at(i + 1))
                if i >= 2:
                    act.wait_ge(*self.o_mm.at(i - 1))
                for c in range(CH):
                    m = act.activation(FT[:, i % 2, c, :], PS[:, B_PT, P * c:P * (c + 1)], ACT.Identity,
                                       bias=lnwb[:, 1, c:c + 1], scale=lnwb[:, 0, c:c + 1])
                m.then_inc(self.ht.sem, 1)

            def o_pe(self, pe, job):
                i = job.i
                pe.wait_ge(*self.ht.at(i + 1))
                if job.before:
                    pe.wait_ge(*job.before.r_read())
                if job.ago(2) and job.ago(2).stage is not self:
                    pe.wait_ge(*job.ago(2).x_read())
                for c in range(CH):
                    m = pe.matmul(PS[:, B_OX, P:2 * P], FT[:, i % 2, c, :], FCT[:, 1, c, :], start=(c == 0), stop=(c == CH - 1))
                m.then_inc(self.o_mm.sem, 1)

            def x_pe(self, pe, job):
                pass

            def x_act(self, act, job):
                pass

        class Tile:

            def __init__(self, stage, i, n, stream):
                self.stage, self.i, self.n, self.stream = stage, i, n, stream

            def ago(self, k):
                return self.stream[self.n - k] if self.n >= k else None

            @property
            def before(self):
                return self.ago(1)

            @property
            def after(self):
                return self.stream[self.n + 1] if self.n + 1 < len(self.stream) else None

            @property
            def after2_any(self):
                return self.stream[self.n + 2] if self.n + 2 < len(self.stream) else None

            @property
            def after2(self):
                t = self.after2_any
                return t if t and not isinstance(t.stage, Ternary) and not t.stage.wide else None

            def p_used(self):
                return self.stage.p_used(self.i)

            def pt_used(self):
                return self.stage.pt_used(self.i)

            def pt_read(self, m):
                return self.stage.pt_read(self.i, m)

            def s_read(self):
                return self.stage.s_read(self.i)

            def y_read(self):
                return self.stage.y_read(self.i)

            def v_read(self):
                return self.stage.v_read(self.i)

            def kt_used(self):
                return self.stage.kt_used(self.i)

            def kb_used(self):
                return self.stage.kb_used(self.i)

            def x_read(self):
                return self.stage.norm.xev.at(self.i + 1)

            def r_read(self):
                return self.stage.norm.r.at(self.i + 1)

        def stream_of(*stages):
            tiles = []
            for st in stages:
                for i in range(NT):
                    tiles.append(Tile(st, i, len(tiles), tiles))
            return tiles

        DEPTH = 6

        def at(tiles, j):
            return tiles[j] if 0 <= j < len(tiles) else None

        def stream_pe(pe, tiles, extra):
            for j in range(len(tiles) + DEPTH):
                a = at(tiles, j - 2)
                if a:
                    a.stage.s_pe(pe, a)
                y = at(tiles, j - 5)
                if y:
                    y.stage.y_pe(pe, y)
                b = at(tiles, j - 1)
                if b:
                    b.stage.qkw_pe(pe, b)
                b = at(tiles, j)
                if b:
                    b.stage.qk_pe(pe, b)
                if a:
                    a.stage.v_pe(pe, a)
                extra(pe, j)
                t = at(tiles, j - 3)
                if t:
                    t.stage.t_pe(pe, t)
                v = at(tiles, j - 4)
                if v and (v.stage.wide or (y and y.stage.wide)):
                    v.stage.va_pe(pe, v)
                if y:
                    y.stage.o_pe(pe, y)
                if v and not (v.stage.wide or (y and y.stage.wide)):
                    v.stage.va_pe(pe, v)
                if v:
                    v.stage.vb_pe(pe, v)
                x = at(tiles, j - 6)
                if x:
                    x.stage.x_pe(pe, x)

        def stream_act(act, tiles, extra):
            for j in range(len(tiles) + DEPTH):
                y = at(tiles, j - 5)
                if y:
                    y.stage.y_act(act, y)
                b, q, v = at(tiles, j), at(tiles, j - 1), at(tiles, j - 2)
                if q:
                    q.stage.qkw_copies(act, 0, q)
                if b:
                    b.stage.qk_act(act, b)
                if v:
                    v.stage.vw_copies(act, 0, v)
                    v.stage.v_act(act, v)
                extra(act, j)
                t = at(tiles, j - 3)
                if t:
                    t.stage.pt_act(act, t)
                w = at(tiles, j - 4)
                if w:
                    w.stage.ya_act(act, w)
                if v:
                    v.stage.exp_act(act, v)
                if w:
                    w.stage.yb_act(act, w)
                x = at(tiles, j - 6)
                if x:
                    x.stage.x_act(act, x)

        def stream_dve(dve, tiles, extra):
            for j in range(len(tiles) + DEPTH):
                y = at(tiles, j - 5)
                if y:
                    y.stage.y_dve(dve, y)
                x = at(tiles, j - 6)
                if x:
                    x.stage.ln_dve(dve, x)
                t = at(tiles, j - 3)
                if t:
                    t.stage.sum_dve(dve, t)
                v = at(tiles, j - 2)
                if v:
                    v.stage.max_dve(dve, v)
                if t and isinstance(t.stage, Ternary):
                    t.stage.hidden_dve(dve, t)
                b, q = at(tiles, j), at(tiles, j - 1)
                if q:
                    q.stage.qkw_copies(dve, 1, q)
                early = v and v.stage.wide
                if b and early:
                    b.stage.qk_dve(dve, b)
                if v:
                    v.stage.vw_copies(dve, 1, v)
                extra(dve, j)
                if y:
                    y.stage.r_dve(dve, y)
                if b and not early:
                    b.stage.qk_dve(dve, b)

        def stream_pool(pool, tiles):
            for j in range(len(tiles) + DEPTH):
                b = at(tiles, j - 1)
                if b:
                    b.stage.blocks_pool(pool, b)
                b = at(tiles, j)
                if b:
                    b.stage.cos_pool(pool, b)
                t = at(tiles, j - 3)
                if t:
                    t.stage.norm_pool(pool, t)
                    t.stage.hidden_pool(pool, t)
                y = at(tiles, j - 5)
                if y:
                    y.stage.rsqrt_pool(pool, y)
                x = at(tiles, j - 6)
                if x:
                    x.stage.bias_pool(pool, x)

        def nothing(eng, j):
            pass

        STEPS, LAG = 8 * EXPERTS, 3

        class Experts:
            def __init__(self, prev):
                self.prev = prev
                self.gate_mm, self.gate_read = Mark("logits_made"), Mark("logits_copied")
                self.top, self.topi = Mark("logits_sorted"), Mark("experts_ranked")
                self.diff, self.e2, self.den = Mark("logit_difference_made"), Mark("second_exponential_made"), Mark("pair_sum_made")
                self.p1, self.p2, self.oh, self.comb = (
                    Mark("first_weight_made"), Mark("second_weight_made"), Mark("choices_made"), Mark("expert_weights_made"))
                self.g_mm, self.u_mm, self.silu, self.mul = (
                    Mark("gates_projected"), Mark("ups_projected"), Mark("silu_made"), Mark("hidden_made"))
                self.d_mm, self.acc = Mark("downs_projected"), Mark("expert_added")
                self.w_mm, self.w_hi, self.w_lo = (
                    Mark("expert_weights_transposed"), Mark("weights_high_made"), Mark("weights_low_made"))
                self.x_hi, self.x_lo = Mark("x_high_made"), Mark("x_low_made")
                self.h_hi, self.h_lo = Mark("hidden_high_made"), Mark("hidden_low_made")
                self.y_cp, self.y_mm = Mark("expert_output_copied"), Mark("expert_output_transposed")
                self.norm = Norm("experts")

            PARTS = ((0, 0), (0, 1), (1, 0))

            def weights_free(self, eng, g):
                e, w = g // 3, g % 3
                if e >= 2:
                    eng.wait_ge(*(self.g_mm, self.u_mm, self.d_mm)[w].at(8 * (e - 1)))

            def weights_pe(self, pe, g):
                e = g // 3
                if g % 3 == 0:
                    pe.wait_ge(s_raw[e % 4], 48 * (e // 4 + 1))
                if g >= 2:
                    pe.wait_ge(*self.w_lo.at(g - 1))
                for c in range(CH):
                    m = pe.transpose(PS[:, 6 + g % 2, P * c:P * (c + 1)], RAW[:, e % 4, g % 3, P * c:P * (c + 1)], ident)
                m.then_inc(self.w_mm.sem, 1)

            def weights_act(self, act, g):
                act.wait_ge(*self.w_mm.at(g + 1))
                self.weights_free(act, g)
                act.activation(WS[:, g // 3 % 2, g % 3, 0, :], PS[:, 6 + g % 2, :], ACT.Copy).then_inc(self.w_hi.sem, 1)

            def weights_dve(self, dve, g):
                dve.wait_ge(*self.w_hi.at(g + 1))
                w = WS[:, g // 3 % 2, g % 3]
                dve.tensor_tensor(w[:, 1, :], PS[:, 6 + g % 2, :], w[:, 0, :], ALU.subtract).then_inc(self.w_lo.sem, 1)

            def later_weights(self, n):
                k, c = n // 4, n % 4
                if 2 <= k < 14 and k % 2 == 0 and c == 1:
                    return [3 * (k // 2 + 1), 3 * (k // 2 + 1) + 1]
                if 2 <= k < 14 and k % 2 == 1 and c == 2:
                    return [3 * (k // 2 + 1) + 2]
                return []

            def gate_up(self, pe, n):
                k, c = n // 4, n % 4
                e, h = k // 2, k % 2
                if c == 0 and h == 0:
                    pe.wait_ge(*self.w_lo.at(3 * e + 3))
                if n < 8:
                    pe.wait_ge(*self.x_lo.at(h + 1))
                if n >= 2:
                    pe.wait_ge(*self.silu.at(n - 1))
                    pe.wait_ge(*self.mul.at(n - 1))
                for bank, w, s in ((n % 2, 0, self.g_mm), (2 + n % 2, 1, self.u_mm)):
                    for q, (a, b) in enumerate(self.PARTS):
                        m = pe.matmul(PS[:, bank, :], WS[:, e % 2, w, a, P * c:P * (c + 1)], XS[:, b, BANK * h:BANK * (h + 1)],
                                      start=(q == 0), stop=(q == 2))
                    m.then_inc(s.sem, 1)

            def down(self, pe, m):
                k, c = m // 4, m % 4
                pe.wait_ge(*self.h_lo.at(m + 1))
                if c == 0 and k >= 2:
                    pe.wait_ge(*self.acc.at(4 * (k - 1)))
                for q, (a, b) in enumerate(self.PARTS):
                    t = pe.matmul(PS[:, 4 + k % 2, :], WS[:, k // 2 % 2, 2, a, P * c:P * (c + 1)], HS[:, k % 2, b, c, :],
                                  start=(c == 0 and q == 0), stop=(c == CH - 1 and q == 2))
                t.then_inc(self.d_mm.sem, 1)

            def turn_pe(self, pe, k):
                pe.wait_ge(*self.y_cp.at(k + 1))
                for t in range(4):
                    m = pe.transpose(PS[:, 4 + k % 2, P * t:P * (t + 1)], YE[:, P * t:P * (t + 1)], ident)
                m.then_inc(self.y_mm.sem, 1)

            def turn_act(self, act, k):
                act.wait_ge(*self.d_mm.at(4 * k + 4))
                if k >= 1:
                    act.wait_ge(*self.y_mm.at(k))
                act.activation(YE, PS[:, 4 + k % 2, :], ACT.Copy).then_inc(self.y_cp.sem, 1)

            def pe(self, pe):
                pe.wait_ge(*self.prev.xev.at(NT))
                for t in range(NT):
                    m = pe.matmul(PS[:, 6, 8 * t:8 * t + 8], XT[:, P * t:P * (t + 1)], gwT[:, :], start=True, stop=True)
                m.then_inc(self.gate_mm.sem, 1)
                for n in range(STEPS + LAG):
                    if n < STEPS:
                        self.gate_up(pe, n)
                    if LAG <= n < STEPS + LAG:
                        self.down(pe, n - LAG)
                    if n % 4 == 0 and n >= 8:
                        self.turn_pe(pe, n // 4 - 2)
                    for g in self.later_weights(n):
                        if g == 6:
                            pe.wait_ge(*self.gate_read.at(1))
                        self.weights_pe(pe, g)
                    if n == 56:
                        fc.totals(pe, self.w_lo.at(3 * EXPERTS))
                self.turn_pe(pe, 2 * EXPERTS - 1)
                fct.pe(pe)
                for i in range(NT):
                    pe.wait_ge(*self.norm.ln.at(i + 1))
                    if i >= 2:
                        pe.wait_ge(*self.norm.xev.at(i - 1))
                    pe.transpose(PS[:, i % 2, 0:P], X[:, i, :], ident).then_inc(self.norm.xmm.sem, 1)
                pe.wait_ge(*self.norm.xev.at(NT))

            def hidden_high(self, act, n):
                k, c = n // 4, n % 4
                act.wait_ge(*self.mul.at(n + 1))
                if k >= 2:
                    act.wait_ge(*self.d_mm.at(n - 7))
                act.activation(HS[:, k % 2, 0, c, :], HF[:, n % 2, :], ACT.Copy).then_inc(self.h_hi.sem, 1)

            def hidden_low(self, dve, n):
                k, c = n // 4, n % 4
                dve.wait_ge(*self.h_hi.at(n + 1))
                dve.tensor_tensor(HS[:, k % 2, 1, c, :], HF[:, n % 2, :], HS[:, k % 2, 0, c, :], ALU.subtract)\
                   .then_inc(self.h_lo.sem, 1)

            def act(self, act):
                act.wait_ge(*self.prev.xev.at(NT))
                for h in range(2):
                    act.activation(XS[:, 0, BANK * h:BANK * (h + 1)], XT[:, BANK * h:BANK * (h + 1)], ACT.Copy)\
                       .then_inc(self.x_hi.sem, 1)
                act.wait_ge(*self.diff.at(1))
                act.activation(pk[:, 1, :], pk[:, 0, :], ACT.Exp).then_inc(self.e2.sem, 1)
                for n in range(STEPS + 1):
                    if n < STEPS:
                        act.wait_ge(*self.g_mm.at(n + 1))
                        if n >= 2:
                            act.wait_ge(*self.mul.at(n - 1))
                        act.activation(SG[:, n % 2, :], PS[:, n % 2, :], ACT.Silu).then_inc(self.silu.sem, 1)
                    if n >= 1:
                        self.hidden_high(act, n - 1)
                    if n % 4 == 3 and n >= 7:
                        self.turn_act(act, n // 4 - 1)
                    for g in self.later_weights(n):
                        self.weights_act(act, g)
                self.turn_act(act, 2 * EXPERTS - 1)
                fct.copies(act, 0)
                for i in range(NT):
                    act.wait_ge(*self.norm.xmm.at(i + 1))
                    act.activation(XT[:, i * P:(i + 1) * P], PS[:, i % 2, 0:P], ACT.Copy).then_inc(self.norm.xev.sem, 1)

            def route(self, dve):
                dve.wait_ge(*self.gate_mm.at(1))
                dve.tensor_copy(lg[:, :, :].rearrange("p t e -> p (t e)"), PS[:, 6, 0:8 * NT]).then_inc(self.gate_read.sem, 1)
                dve.wait_ge(*self.gate_read.at(1))
                for t in range(NT):
                    dve.max(top[:, t, :], lg[:, t, :]).then_inc(self.top.sem, 1)
                dve.wait_ge(*self.top.at(NT))
                dve.tensor_tensor(pk[:, 0, :], top[:, :, 1], top[:, :, 0], ALU.subtract).then_inc(self.diff.sem, 1)
                for h in range(2):
                    dve.wait_ge(*self.x_hi.at(h + 1))
                    x = slice(BANK * h, BANK * (h + 1))
                    dve.tensor_tensor(XS[:, 1, x], XT[:, x], XS[:, 0, x], ALU.subtract).then_inc(self.x_lo.sem, 1)
                for t in range(NT):
                    dve.max_index(topi[:, t, :], top[:, t, :], lg[:, t, :]).then_inc(self.topi.sem, 1)
                dve.wait_ge(*self.topi.at(NT))
                dve.tensor_copy(topf[:, :, :], topi[:, :, 0:2]).then_inc(self.topi.sem, 1)
                dve.wait_ge(*self.e2.at(1))
                dve.tensor_scalar(pk[:, 2, :], pk[:, 1, :], 1.0, None, ALU.add).then_inc(self.den.sem, 1)
                dve.wait_ge(*self.den.at(1))
                dve.reciprocal(pk[:, 2, :], pk[:, 2, :]).then_inc(self.p1.sem, 1)
                dve.wait_ge(*self.p1.at(1))
                dve.tensor_tensor(pk[:, 3, :], pk[:, 1, :], pk[:, 2, :], ALU.mult).then_inc(self.p2.sem, 1)
                dve.wait_ge(*self.p2.at(1))
                dve.wait_ge(*self.topi.at(NT + 1))
                for r in range(2):
                    dve.tensor_tensor(comb[:, r], bc(cst[:, C_IOTA:C_IOTA + 8], 1, NT), bc(topf[:, :, r], 2, 8),
                                      ALU.is_equal).then_inc(self.oh.sem, 1)
                dve.wait_ge(*self.oh.at(2))
                for r in range(2):
                    dve.tensor_tensor(comb[:, r], comb[:, r], bc(pk[:, 2 + r, :], 2, 8), ALU.mult).then_inc(self.oh.sem, 1)
                dve.wait_ge(*self.oh.at(4))
                dve.tensor_tensor(comb[:, 0], comb[:, 0], comb[:, 1], ALU.add).then_inc(self.comb.sem, 1)
                dve.wait_ge(*self.comb.at(1))

            def accumulate(self, dve, k):
                dve.wait_ge(*self.y_mm.at(k + 1))
                e, h = k // 2, k % 2
                if k >= 2:
                    dve.wait_ge(*self.acc.at(4 * (k - 1)))
                for j in range(4):
                    t = 4 * h + j
                    dve.scalar_tensor_tensor(XR[:, t, :], PS[:, 4 + k % 2, P * j:P * (j + 1)], comb[:, 0, t, e:e + 1],
                                             (X if e == 0 else XR)[:, t, :], ALU.mult, ALU.add).then_inc(self.acc.sem, 1)

            def dve(self, dve):
                self.route(dve)
                K = 2 * EXPERTS
                for n in range(STEPS + 1):
                    k, c = n // 4, n % 4
                    if n < STEPS:
                        dve.wait_ge(*self.silu.at(n + 1))
                        dve.wait_ge(*self.u_mm.at(n + 1))
                        if n >= 2:
                            dve.wait_ge(*self.h_lo.at(n - 1))
                        dve.tensor_tensor(HF[:, n % 2, :], PS[:, 2 + n % 2, :], SG[:, n % 2, :], ALU.mult).then_inc(self.mul.sem, 1)
                    if n >= 1:
                        self.hidden_low(dve, n - 1)
                    for g in self.later_weights(n):
                        self.weights_dve(dve, g)
                    if c == 1 and k >= 2:
                        self.accumulate(dve, k - 2)
                    if n == 50:
                        fc.magnitudes(dve)
                    if n == 60:
                        fc.quantize(dve)
                self.accumulate(dve, K - 2)
                self.accumulate(dve, K - 1)
                fct.copies(dve, 1)
                norm = self.norm
                dve.wait_ge(*self.acc.at(4 * K))
                for i in range(NT + 1):
                    if i < NT:
                        norm.stats(dve, i, XR[:, i, :])
                    if i >= 1:
                        norm.apply(dve, i - 1, XR[:, i - 1, :])

            def pool(self, pool):
                pool.wait_ge(*self.w_mm.at(3 * EXPERTS))
                pool.memset(VW, 0.0).then_inc(s_wz, 1)
                for i in range(NT):
                    self.norm.rsqrt(pool, i)

        a0 = Narrow("self0", 0, XT, rope=True, bias=0, row=0, next_row=1)
        a0.res, a0.input = Mark("first_residual_made"), None
        a1 = Narrow("cross0", 4, CT, bias=1, fill=0, row=1)
        a1.res, a1.input = a0.norm.xr, a0.norm
        moe = Experts(a1.norm)
        wide = Wide("wide")
        wide.input = moe.norm
        a2 = Narrow("cross1", 8, CT, fill=1)
        a2.input = wide.norm
        fc = Ternary("ternary")
        fc.input = a2.norm
        pre, post = stream_of(a0, a1), stream_of(wide, a2, fc)
        NB = 8 + 2 + 2

        DRAIN = len(pre)

        def pre_pe(pe, j):
            if j == 0:
                later.pe(pe)
            if j == DRAIN:
                for s in pre[-1].stage.qk_read(NT - 1):
                    pe.wait_ge(*s)
            if j >= DRAIN:
                moe.weights_pe(pe, j - DRAIN)

        def pre_act(act, j):
            if j == 0:
                later.copies(act, 0)
            if j >= DRAIN:
                moe.weights_act(act, j - DRAIN)

        def pre_dve(dve, j):
            if j == 0:
                later.copies(dve, 1)
            if j >= DRAIN:
                moe.weights_dve(dve, j - DRAIN)

        @block.sync
        def _(sp):
            def load(dst, src, s, **k):
                sp.dma_start(dst, src, **k).then_inc(s, 16)

            load(X[:, :, :], A["x"].rearrange("(t b) s f -> (b s) t f", b=2), s_x)
            load(cst[:, :], table, s_cst)
            for n in range(4):
                load(RAWW[:, n, :], A[WNAMES[n]], s_w0)
            for b, (names) in enumerate((("L0_attn_bq", "L0_attn_bk"), ("L0_xattn_bq", "L0_xattn_bk"))):
                for n, name in enumerate(names):
                    for r in range(2):
                        load(qkb[64 * r:64 * r + 64, b, n, :], A[name].rearrange("(g p) -> p g", g=2), s_b,
                             allow_slow_non_contiguous=True)
            for n, name in enumerate(("L0_attn_bp", "L0_xattn_bo")):
                load(rowb[:, n, :], A[name].partition_broadcast(P), s_b)
            for n, name in enumerate(("L0_attn_bv", "L0_xattn_bv")):
                load(bvc[:, n:n + 1], A[name].rearrange("(p o) -> p o", o=1), s_b)
            load(CTXR[:, :, :], A["ctx_1024"].rearrange("(t b) s f -> (b s) t f", b=2), s_ctx)
            for n in range(4, 12):
                load(RAWW[:, n, :], A[WNAMES[n]], s_w)
            load(gw[:, :], A["L0_ffn_gate_w"], s_w)
            mask = A["mask_Bx1x1xS2_ik0"].rearrange("(t b) x y k -> b (x y) t k", b=2)
            for b in range(2):
                load(mki[64 * b:64 * b + 64, :, :], mask[b].to_broadcast([64, NT, SEQ]), s_m)
            for j in range(3):
                load(mri[2 * j:2 * j + 2, :, :], mask[:, 0], s_m)
            def load_expert(e):
                for w, name in enumerate(("L0_ffn_wg", "L0_ffn_wu")):
                    load(RAW[:, e % 4, w].rearrange("p (c h) -> p c h", c=CH),
                         A[name][e].rearrange("(c i) h -> i c h", c=CH), s_raw[e % 4])
                load(RAW[:, e % 4, 2], A["L0_ffn_wd"][e], s_raw[e % 4])

            for e in range(4):
                load_expert(e)
            load(WQKV[:, :], A["L1_attn_W_qkv"], s_wide)
            load(WOUT[:, :, :], A["L1_attn_W_out"].rearrange("(u p) f -> p u f", p=P), s_wide)
            load(FCW[:, 0], A["L1_ffn_W_fc"].rearrange("(c i) f -> i c f", c=CH), s_fc)
            load(FCW[:, 1].rearrange("p c f -> p (c f)"), A["L1_ffn_W_proj"], s_fc)
            for n, name in enumerate(("L1_ffn_ln_w", "L1_ffn_ln_b")):
                load(lnwb[:, n, :], A[name].rearrange("(c p) -> p c", c=CH), s_fc, allow_slow_non_contiguous=True)
            for e in range(4, EXPERTS):
                sp.wait_ge(*moe.w_mm.at(3 * (e - 3)))
                load_expert(e)
            out_v = out.rearrange("(t b) s f -> (b s) t f", b=2)
            for i in range(NT):
                sp.wait_ge(*fc.norm.ln.at(i + 1))
                sp.dma_start(out_v[:, i, :], X[:, i, :]).then_inc(s_out, 16)
            sp.wait_ge(s_out, 16 * NT)

        @block.gpsimd
        def _(pool):
            pool.memset(half[:, :], -0.5).then_inc(s_half, 1)
            pool.memset(QS[:, :, :, :], 0.0).then_inc(s_z, 1)
            pool.memset(VB[:, :, :, :, :, :], 0.0).then_inc(s_z, 1)
            pool.wait_ge(s_cst, 16)
            pool.wait_ge(s_z, 2)
            for b in range(2):
                for a in range(2):
                    pool.tensor_copy(VB[:, :, :, b, a, DH], bc(cst[:, C_HALF + a:C_HALF + a + 1], 1, 3).to_broadcast([P, 3, PAIRS]))\
                        .then_inc(s_z, 1)
            pool.wait_ge(s_half, 1)
            pool.wait_ge(s_x, 16)
            pool.wait_ge(s_b, 16 * NB)
            for i in range(NT):
                pool.tensor_tensor(XR[:, i, :], X[:, i, :], rowb[:, 0, :], ALU.add).then_inc(a0.res.sem, 1)
            pool.wait_ge(s_m, 16 * 5)
            pool.tensor_scalar(mk[:, :, :], mki[:, :, :], 0.0, 1.0, ALU.is_equal, ALU.subtract).then_inc(s_mk0, 1)
            pool.wait_ge(s_mk0, 1)
            pool.tensor_scalar(mk[:, :, :], mk[:, :, :], -1.0, None, ALU.mult).then_inc(s_mk0, 1)
            pool.wait_ge(s_mk0, 2)
            pool.tensor_scalar(mrb[:, :, :], mri[:, :, :], 0.0, None, ALU.is_equal).then_inc(s_mk, 1)
            stream_pool(pool, pre)
            moe.pool(pool)
            stream_pool(pool, post)

        @block.scalar
        def _(act):
            first.copies(act, 0)
            act.wait_ge(s_b, 16 * NB)
            stream_act(act, pre, pre_act)
            moe.act(act)
            act.wait_ge(s_fc, 64)
            stream_act(act, post, nothing)

        @block.vector
        def _(dve):
            dve.wait_ge(s_cst, 16)
            dve.tensor_copy(idb[:, :], ident).then_inc(s_bf, 1)
            dve.tensor_copy(caus[:, :], cst[:, C_CAUSAL:C_CAUSAL + SEQ]).then_inc(s_bf, 1)
            dve.wait_ge(s_bf, 2)
            dve.tensor_copy(fills[:, :, :], cst[0:6, C_FILL0:C_FILL0 + 2 * P].rearrange("p (l q) -> p l q", l=2))\
               .then_inc(s_bfc, 1)
            first.copies(dve, 1)
            stream_dve(dve, pre, pre_dve)
            moe.dve(dve)
            stream_dve(dve, post, nothing)

        @block.tensor
        def _(pe):
            first.pe(pe)
            first.done(pe)
            pe.wait_ge(s_bfc, 1)
            stream_pe(pe, pre, pre_pe)
            moe.pe(pe)
            stream_pe(pe, post, nothing)


def kernel(**inputs):
    import concourse.bacc as _bacc
    from concourse.bass_utils import run_bass_kernel_spmd as _run

    nc = _bacc.Bacc("TRN2", target_bir_lowering=False, num_devices=1)
    arrays, args = {}, {}
    for name in inputs:
        a = np.ascontiguousarray(inputs[name])
        arrays[f"in_{name}_dram"] = a
        args[name] = nc.dram_tensor(f"in_{name}_dram", a.shape, mybir.dt.from_np(a.dtype), kind="ExternalInput").ap()
    out = nc.dram_tensor("out_0_dram", (BATCH, SEQ, P), F32, kind="ExternalOutput").ap()
    decoder_kernel(nc, args, out)
    r = _run(nc, [arrays], core_ids=[0])
    return r.results[0]["out_0_dram"]
```

```python
from contextlib import ExitStack

import numpy as np

import concourse.bass as bass
from concourse import mybir

F32 = mybir.dt.float32
BF16 = mybir.dt.bfloat16
F32R = mybir.dt.float32r
I32 = mybir.dt.int32
U32 = mybir.dt.uint32
ALU = mybir.AluOpType
ACT = mybir.ActivationFunctionType
AX = mybir.AxisListType

P = 128
BATCH, SEQ = 16, 64
NT = BATCH * SEQ // P
HEADS = 16
DH = 8
DW = 64
PAIRS = HEADS // 2
EXPERTS, INNER = 8, 512
CH = INNER // P
BANK = 512
LN_EPS = 1e-5

C_ID, C_COS, C_SIN, C_HEAD, C_CAUSAL, C_IOTA, C_FILL0, C_FILL1, C_ONES, C_HALF, C_END = (
    0, 128, 192, 256, 264, 328, 336, 464, 592, 720, 722)
CAUSAL_FILL = -(2.0 ** 100)


def bf16_parts(value):
    parts, rest = [], np.float32(value)
    for _ in range(3):
        bits = np.array(rest, np.float32).view(np.uint32)
        part = np.array(bits & np.uint32(0xFFFF0000), np.uint32).view(np.float32)
        parts.append(float(part))
        rest = np.float32(rest - part)
    assert float(rest) == 0.0
    return parts


def constants():
    c = np.zeros((P, C_END), np.float32)
    c[:, C_ID:C_ID + P] = np.eye(P)
    d = np.arange(P) % DH
    theta = np.power(np.float32(10000.0), (np.float32(-2.0) * (d // 2).astype(np.float32) / np.float32(DH)).astype(np.float32))
    angle = theta[:, None].astype(np.float32) * np.arange(SEQ, dtype=np.float32)[None, :]
    c[:, C_COS:C_COS + SEQ] = np.cos(angle)
    c[:, C_SIN:C_SIN + SEQ] = np.sin(angle) * np.where(d % 2 == 0, -1.0, 1.0)[:, None]
    c[:, C_HEAD:C_HEAD + 8] = (np.arange(P)[:, None] % 64) // DH == np.arange(8)[None, :]
    c[:, C_CAUSAL:C_CAUSAL + SEQ] = np.where(np.arange(SEQ)[None, :] > np.arange(P)[:, None] % SEQ, CAUSAL_FILL, 0.0)
    c[:, C_IOTA:C_IOTA + 8] = np.arange(8)[None, :]
    for col, fill in ((C_FILL0, -1e9), (C_FILL1, -1e12)):
        for j, part in enumerate(bf16_parts(fill * np.sqrt(DH))):
            for b in range(2):
                c[2 * j + b, col + SEQ * b:col + SEQ * (b + 1)] = part
    c[:, C_ONES:C_ONES + P] = 1.0
    c[:, C_HALF:C_HALF + 2] = np.arange(P)[:, None] // 64 == np.arange(2)[None, :]
    return c


def decoder_kernel(nc, A, out):
    with ExitStack() as ctx:
        def sb(name, shape, dt=F32):
            return ctx.enter_context(nc.sbuf_tensor(name, shape, dt))

        def sem(name):
            return ctx.enter_context(nc.semaphore(name))

        running = {}

        class Mark:

            def __init__(self, name, total=0):
                if name not in running:
                    running[name] = [sem(name), 0]
                self.sem, self.base = running[name]
                running[name][1] += total

            def at(self, n):
                return self.sem, self.base + n

        def bc(ap, axis, n):
            shape = list(ap.shape)
            shape.insert(axis, n)
            return ap.unsqueeze(axis).to_broadcast(shape)

        table = nc.inline_tensor(constants(), "shape_constants").ap()
        PS = ctx.enter_context(nc.psum_tensor("banks", [P, 8, BANK], F32))
        B_S, B_PT, B_Y, B_OX, B_K, B_Q = 0, 2, 4, 5, 6, 7
        cst = sb("cst", [P, C_END])
        X = sb("X", [P, NT, P])
        XR = sb("XR", [P, NT, P])
        XT = sb("XT", [P, NT * P])
        CT = sb("CT", [P, NT * P])
        WT = sb("WT", [P, 12, P])
        PR = sb("PR", [P, 2, HEADS * SEQ])
        PT = sb("PT", [P, 2, PAIRS, P])
        WQKV = sb("WQKV", [P, 3 * HEADS * DW])
        WOUT = sb("WOUT", [P, PAIRS, P])
        FCW = sb("FCW", [P, 2, CH, P])
        FCT = sb("FCT", [P, 2, CH, P])
        lnwb = sb("lnwb", [P, 2, CH])
        gw = sb("gw", [8, P])
        gwT = sb("gwT", [P, 8])
        qkb = sb("qkb", [P, 2, 2, 2])
        bvc = sb("bvc", [P, 2])
        rowb = sb("rowb", [P, 3, P])
        mk = sb("mk", [P, NT, SEQ])
        mrb = sb("mrb", [6, NT, SEQ], BF16)
        idb = sb("idb", [P, P], BF16)
        caus = sb("caus", [P, SEQ], BF16)
        fills = sb("fills", [6, 2, P], BF16)
        QS = sb("QS", [P, 3, 2, P])
        TMP = sb("TMP", [P, 2, 4, SEQ])
        TC = sb("TC", [P, 2, 4, SEQ])
        TS = sb("TS", [P, 2, 4, SEQ])
        KT = sb("KT", [P, 2, 2, SEQ])
        KB = sb("KB", [P, 2, 2, 8, SEQ])
        VB = sb("VB", [P, 3, PAIRS, 2, 2, DH + 1])
        mx = sb("mx", [P, 2, HEADS])
        rs = sb("rs", [P, 2, HEADS])
        ysb = sb("ysb", [P, 2, P])
        yT = sb("yT", [P, 2, P])
        R = sb("R", [P, 2, P])
        stats = sb("stats", [P, 2, 6])
        mv = sb("mv", [P, 2, 2])
        YN = sb("YN", [P, 2, BANK])
        ve = sb("ve", [P, 2, 1])
        rstd = sb("rstd", [P, 2, 1])
        hst = sb("hst", [P, 2, 16])
        st8 = sb("st8", [P, NT, 6])
        mv8 = sb("mv8", [P, NT, 2])
        ve8 = sb("ve8", [P, NT, 1])
        rstd8 = sb("rstd8", [P, NT, 1])
        half = sb("half", [P, 1])
        lg = sb("lg", [P, NT, 8])
        top = sb("top", [P, NT, 8])
        topi = sb("topi", [P, NT, 8], U32)
        topf = sb("topf", [P, NT, 2])
        pk = sb("pk", [P, 4, NT])
        comb = sb("comb", [P, 2, NT, EXPERTS])
        gam = sb("gam", [P, 8])
        U = sb("U", [P, 10240])
        XS = sb("XS", [P, 2, NT * P], F32R)
        WS = sb("WS", [P, 2, 3, 2, BANK], F32R)
        HS = sb("HS", [P, 2, 2, CH, BANK], F32R)
        ident = cst[:, C_ID:C_ID + P]

        def region(start, size, pattern=None, **k):
            v = U[:, start:start + size]
            return v.rearrange(pattern, **k) if pattern else v

        RAWW = region(0, 1536, "p (w f) -> p w f", w=12)
        CTXR = region(1536, 1024, "p (t f) -> p t f", t=NT)
        mki = region(2560, 512).bitcast(I32).rearrange("p (t k) -> p t k", t=NT)
        mri = U[0:6, 3072:3584].bitcast(I32).rearrange("p (t k) -> p t k", t=NT)
        RAW = region(4096, 6144, "p (n w i) -> p n w i", n=4, w=3)
        SG = PR[:, 0, :].rearrange("p (k t) -> p k t", k=2)
        HF = PR[:, 1, :].rearrange("p (k t) -> p k t", k=2)
        YE = PT[:, 1].rearrange("p r q -> p (r q)")[:, 0:BANK]
        LB = PT[:, 0, 0:4]
        FA = PT[:, 0].rearrange("p (n c) q -> p n (c q)", n=2)
        QK = region(0, 4096, "p (n c u t) -> p n c u t", n=2, c=2, u=PAIRS)
        VW = region(4096, 6144, "p (n b u a d) -> p n b u a d", n=3, b=2, u=PAIRS, a=2)
        YW = [XR, WT[:, 0:PAIRS, :]]
        FH = region(0, 1024, "p (n i) -> p n i", n=2)
        FN = region(1024, 1024, "p (n i) -> p n i", n=2)
        FT = region(2048, 1024, "p (n c t) -> p n c t", n=2, c=CH)

        s_id = sem("identity_loaded")
        s_cst = sem("cst_loaded")
        s_x = [sem("x_loaded_%d" % h) for h in range(2)]
        s_ctx = sem("ctx_loaded")
        s_w0 = sem("first_weights_loaded")
        s_w = sem("later_weights_loaded")
        s_b = [sem("first_biases_loaded"), sem("second_biases_loaded")]
        s_m = sem("masks_loaded")
        s_raw = [sem("expert_weights_loaded_%d" % n) for n in range(4)]
        s_wide = sem("wide_weights_loaded")
        s_fc = sem("ternary_weights_loaded")
        s_half = sem("minus_half_set")
        s_mk0 = sem("masks_started")
        s_mk = sem("masks_made")
        s_bf = sem("bf16_identity_made")
        s_bfc = sem("bf16_constants_made")
        s_z = sem("blocks_zeroed")
        s_wz = sem("wide_blocks_zeroed")
        s_tern = sem("ternary_weights_made")
        s_out = sem("output_stored")

        WNAMES = ["L0_attn_wq", "L0_attn_wk", "L0_attn_wv", "L0_attn_wp",
                  "L0_xattn_Wq", "L0_xattn_Wk", "L0_xattn_Wv", "L0_xattn_Wo",
                  "L1_xattn_Wq", "L1_xattn_Wk", "L1_xattn_Wv", "L1_xattn_Wo"]
        block = ctx.enter_context(nc.Block())

        class Transposes:

            def __init__(self, name, groups, banks):
                self.groups, self.banks = groups, banks
                self.mm, self.copied = sem(name + "_transposed"), [sem(name + "_copied_act"), sem(name + "_copied_dve")]

            def pe(self, pe, some=None):
                for g in some or range(len(self.groups)):
                    waits, blocks, _ = self.groups[g]
                    for s, v in waits:
                        pe.wait_ge(s, v)
                    last = g - len(self.banks)
                    if last >= 0:
                        pe.wait_ge(self.copied[last % 2], last // 2 + 1)
                    bank = self.banks[g % len(self.banks)]
                    for n, (src, k) in enumerate(blocks):
                        m = pe.transpose(PS[:, bank, n * P:n * P + k], src, ident[0:k, 0:k])
                    m.then_inc(self.mm, 1)

            def copies(self, eng, part, some=None):
                for g in some or range(len(self.groups)):
                    if g % 2 != part:
                        continue
                    _, blocks, dst = self.groups[g]
                    eng.wait_ge(self.mm, g + 1)
                    src = PS[:, self.banks[g % len(self.banks)], 0:sum(k for _, k in blocks)]
                    if part == 0:
                        eng.activation(dst, src, ACT.Copy).then_inc(self.copied[0], 1)
                    else:
                        eng.tensor_copy(dst, src).then_inc(self.copied[1], 1)

            def done(self, eng, n=None):
                n = len(self.groups) if n is None else n
                eng.wait_ge(self.copied[0], (n + 1) // 2)
                if n > 1:
                    eng.wait_ge(self.copied[1], n // 2)

        def x_group(g):
            return ([(s_id, 16), (s_x[g], 16)], [(X[:, 4 * g + j, :], P) for j in range(4)], XT[:, BANK * g:BANK * (g + 1)])

        def w_group(g):
            return ([(s_w, 16 * 8)] if g else [(s_w0, 16 * 4)], [(RAWW[:, 4 * g + j, :], P) for j in range(4)],
                    WT[:, 4 * g:4 * g + 4, :].rearrange("p w f -> p (w f)"))

        def c_group(g):
            return ([(s_ctx, 32)], [(CTXR[:, 4 * g + j, :], P) for j in range(4)], CT[:, BANK * g:BANK * (g + 1)])

        first = Transposes("first", [x_group(0), w_group(0)], [0, 1])
        later = Transposes("later", [x_group(1), c_group(0), c_group(1), ([], [(gw[:, :], 8)], gwT[:, :])], [2, 3, 5])
        weights = Transposes("weights", [w_group(1), w_group(2)], [5])
        fct = Transposes("ternary", [([(s_tern, 1 + n)], [(FCW[:, n, c, :], P) for c in range(CH)],
                                      FCT[:, n, :, :].rearrange("p c f -> p (c f)")) for n in range(2)], [6, 7])

        class Norm:

            def __init__(self, name):
                self.r = Mark("residual_summed", 0 if name == "experts" else NT)
                self.st = Mark("stats_made", NT)
                self.mv = Mark("variance_made", NT)
                self.ve = Mark("eps_added", NT)
                self.rstd = Mark("rstd_made", NT)
                self.ln = Mark("normed", NT)
                self.xmm = Mark("x_transposed", NT)
                self.xev = Mark("xT_copied", NT)

            def stats(self, dve, i, src):
                dve.bn_stats(stats[:, i % 2, :], src).then_inc(self.st.sem, 1)
                dve.wait_ge(*self.st.at(i + 1))
                dve.bn_aggr(mv[:, i % 2, :], stats[:, i % 2, :]).then_inc(self.mv.sem, 1)

            def rsqrt(self, pool, i):
                pool.wait_ge(*self.mv.at(i + 1))
                pool.tensor_scalar(ve[:, i % 2, :], mv[:, i % 2, 1:2], LN_EPS, None, ALU.add).then_inc(self.ve.sem, 1)
                pool.wait_ge(*self.ve.at(i + 1))
                pool.tensor_tensor(rstd[:, i % 2, :], ve[:, i % 2, :], half[:, :], ALU.pow).then_inc(self.rstd.sem, 1)

            def apply(self, dve, i, src):
                dve.wait_ge(*self.rstd.at(i + 1))
                dve.tensor_scalar(X[:, i, :], src, mv[:, i % 2, 0:1], rstd[:, i % 2, :],
                                  ALU.subtract, ALU.mult).then_inc(self.ln.sem, 1)
                dve.wait_ge(*self.ln.at(i + 1))

        class Stage:

            def none(self, eng, job):
                pass

            qk_pe = qkw_pe = v_pe = s_pe = t_pe = va_pe = ty_pe = vb_pe = y_pe = o_pe = x_pe = none
            qk_act = v_act = pt_act = y_act = exp_act = x_act = ya_act = none
            y_dve = ya_dve = sum_dve = max_dve = qk_dve = none
            blocks_pool = cos_pool = hidden_pool = bias_pool = none
            wide = False

            def qkw_copies(self, eng, part, job):
                pass

            vw_copies = qkw_copies

            def x_pe(self, pe, job):
                i = job.i
                pe.wait_ge(*self.norm.ln.at(i + 1))
                if i + 1 < NT:
                    pe.wait_ge(*self.norm.r.at(i + 2))
                elif job.after is not None:
                    pe.wait_ge(*job.after.stage.norm.r.at(1))
                if i >= 1:
                    pe.wait_ge(*self.norm.xev.at(i))
                pe.transpose(PS[:, B_OX, 2 * P:3 * P], X[:, i, :], ident).then_inc(self.norm.xmm.sem, 1)

            def x_act(self, act, job):
                i = job.i
                act.wait_ge(*self.norm.xmm.at(i + 1))
                act.activation(XT[:, i * P:(i + 1) * P], PS[:, B_OX, 2 * P:3 * P], ACT.Copy).then_inc(self.norm.xev.sem, 1)

            def r_dve(self, dve, job):
                i = job.i
                dve.wait_ge(*self.o_mm.at(i + 1))
                res = X
                if self.row is not None:
                    res = XR
                    dve.wait_ge(*self.res.at(i + 1))
                dve.tensor_tensor(R[:, i % 2, :], PS[:, B_OX, P:2 * P], res[:, i, :], ALU.add).then_inc(self.norm.r.sem, 1)
                dve.wait_ge(*self.norm.r.at(i + 1))
                self.norm.stats(dve, i, R[:, i % 2, :])

            def ln_dve(self, dve, job):
                self.norm.apply(dve, job.i, R[:, job.i % 2, :])

            def rsqrt_pool(self, pool, job):
                self.norm.rsqrt(pool, job.i)

            def max_dve(self, dve, job):
                i, n = job.i, job.n
                dve.wait_ge(*self.s_mm.at(i + 1))
                s = PS[:, B_S:B_S + 2, :].rearrange("q g (h k) -> q (g h) k", k=SEQ)
                dve.tensor_reduce(mx[:, n % 2, :], s, AX.X, ALU.max).then_inc(self.max.sem, 1)
                dve.wait_ge(*self.max.at(i + 1))
                if job.ago(2):
                    dve.wait_ge(*job.ago(2).p_used())
                if self.wide:
                    o = PR[:, n % 2, :].rearrange("q (u a k) -> q a u k", a=2, k=SEQ)
                    dve.tensor_tensor(o, s.rearrange("q (a u) k -> q a u k", a=2),
                                      bc(mx[:, n % 2, :].rearrange("q (a u) -> q a u", a=2), 3, SEQ),
                                      ALU.subtract).then_inc(self.sub.sem, 1)
                else:
                    dve.tensor_tensor(PR[:, n % 2, :].rearrange("q (h k) -> q h k", k=SEQ), s,
                                      bc(mx[:, n % 2, :], 2, SEQ), ALU.subtract).then_inc(self.sub.sem, 1)

            def exp_act(self, act, job):
                act.wait_ge(*self.sub.at(job.i + 1))
                p = PR[:, job.n % 2, :]
                act.activation(p, p, ACT.Exp, scale=self.scale).then_inc(self.exp.sem, 1)

            def t_pe(self, pe, job):
                i, n = job.i, job.n
                pe.wait_ge(*self.exp.at(i + 1))
                for m in range(2):
                    if job.before:
                        pe.wait_ge(*job.before.pt_read(m))
                    for r in range(4 * m, 4 * m + 4):
                        t = pe.transpose(PS[:, B_PT + m, P * (r % 4):P * (r % 4 + 1)], PR[:, n % 2, P * r:P * (r + 1)], ident)
                    t.then_inc(self.t_mm.sem, 1)

            def pt_act(self, act, job):
                i, n = job.i, job.n
                if job.ago(2):
                    act.wait_ge(*job.ago(2).pt_used())
                for m in range(2):
                    act.wait_ge(*self.t_mm.at(2 * i + m + 1))
                    act.activation(PT[:, n % 2, 4 * m:4 * m + 4, :].rearrange("p r q -> p (r q)"),
                                   PS[:, B_PT + m, :], ACT.Copy).then_inc(self.pt.sem, 1)

            def p_used(self, i):
                return self.t_mm.at(2 * i + 2)

            def pt_read(self, i, m):
                return self.pt.at(2 * i + m + 1)

            def s_read(self, i):
                return self.sub.at(i + 1)

        class Narrow(Stage):

            def __init__(self, name, w, src, rope=False, bias=None, fill=None, row=None, next_row=None):
                self.w, self.src, self.rope, self.bias, self.fill = w, src, rope, bias, fill
                self.row, self.next_row, self.scale = row, next_row, float(DH) ** -0.5
                r = NT if rope else 0
                self.k_mm, self.q_mm, self.v_mm = Mark("k_projected", NT), Mark("q_projected", NT), Mark("v_projected", NT)
                self.tmpk, self.tmpq, self.cosd, self.shuf, self.sind = (
                    Mark("k_copied", r), Mark("q_copied", r), Mark("times_cos", r), Mark("pairs_swapped", r), Mark("times_sin", r))
                self.k_ready, self.q_ready, self.v_ready = Mark("k_ready", NT), Mark("q_ready", NT), Mark("v_ready", NT)
                self.kb, self.s_mm = Mark("k_blocks_made", 2 * NT), Mark("scored", NT)
                self.max, self.sub, self.exp = Mark("row_max_made", NT), Mark("max_subtracted", NT), Mark("exponentials_made", NT)
                self.t_mm, self.pt, self.pv = Mark("p_transposed", 2 * NT), Mark("pT_copied", 2 * NT), Mark("v_weighed", NT)
                self.rec, self.yn, self.y_mm = Mark("reciprocals_made", NT), Mark("y_normalized", NT), Mark("y_transposed", NT)
                self.yt, self.o_mm = Mark("yT_copied", NT), Mark("y_projected", NT)
                self.norm = Norm(name)
                self.norm.xr = Mark("bias_added", NT if next_row is not None else 0)

            def pt_used(self, i):
                return self.pv.at(i + 1)

            def y_read(self, i):
                return self.yn.at(i + 1)

            def qk_read(self, i):
                return [(self.tmpk if self.rope else self.k_ready).at(i + 1), (self.tmpq if self.rope else self.q_ready).at(i + 1)]

            def qk_pe(self, pe, job):
                i = job.i
                if self.input is not None:
                    pe.wait_ge(*self.input.xev.at(i + 1))
                if job.before:
                    for s in job.before.stage.qk_read(job.before.i):
                        pe.wait_ge(*s)
                if job.ago(2) and job.ago(2).stage.wide:
                    for s in job.ago(2).v_read():
                        pe.wait_ge(*s)
                for bank, w, src, s in ((B_K, 1, self.src, self.k_mm), (B_Q, 0, XT, self.q_mm)):
                    for g in range(2):
                        for b in range(2):
                            m = pe.matmul(PS[64 * b:64 * b + 64, bank, 64 * g:64 * g + 64],
                                          WT[:, self.w + w, 64 * g:64 * g + 64],
                                          src[:, SEQ * (2 * i + b):SEQ * (2 * i + b + 1)], start=True, stop=True)
                    m.then_inc(s.sem, 1)

            def v_pe(self, pe, job):
                i = job.i
                if job.ago(3):
                    pe.wait_ge(*job.ago(3).y_read())
                if job.before and not job.before.stage.wide:
                    for s in job.before.v_read():
                        pe.wait_ge(*s)
                for b in range(2):
                    for a in range(2):
                        m = pe.matmul(PS[64 * a:64 * a + 64, B_Y, 384 + 64 * b:448 + 64 * b],
                                      self.src[:, SEQ * (2 * i + b):SEQ * (2 * i + b + 1)],
                                      WT[:, self.w + 2, :].rearrange("f (r a d) -> f a r d", a=2, d=DH)[:, a],
                                      start=True, stop=True)
                m.then_inc(self.v_mm.sem, 1)

            def s_pe(self, pe, job):
                i, n = job.i, job.n
                pe.wait_ge(*self.q_ready.at(i + 1))
                if job.before:
                    pe.wait_ge(*job.before.s_read())
                for g in range(2):
                    pe.wait_ge(*self.kb.at(2 * i + g + 1))
                    o = PS[:, B_S + g, :]
                    pe.matmul(o, QS[:, n % 3, g, :], KB[:, n % 2, g].rearrange("p h k -> p (h k)"), start=True, stop=False)
                    o = o.rearrange("q (h k) -> q h k", h=8)
                    if self.fill is None:
                        m = pe.matmul(o, idb[:, :], bc(caus[:, :], 1, 8), start=False, stop=True)
                    else:
                        m = pe.matmul(o, fills[:, self.fill, :], bc(mrb[:, i, :], 1, 8), start=False, stop=True)
                m.then_inc(self.s_mm.sem, 1)

            def va_pe(self, pe, job):
                i, n = job.i, job.n
                pe.wait_ge(*self.pt.at(2 * i + 2))
                pe.wait_ge(*self.v_ready.at(i + 1))
                if job.after2:
                    for s in job.after2.v_read():
                        pe.wait_ge(*s)
                if job.before:
                    pe.wait_ge(*job.before.y_read())
                w = 2 * (DH + 1)
                for b in range(2):
                    for r in range(PAIRS):
                        m = pe.matmul(PS[64 * b:64 * b + 64, B_Y, w * r:w * (r + 1)], PT[:, n % 2, r, 64 * b:64 * b + 64],
                                      VB[:, n % 3, r, b].rearrange("p a e -> p (a e)"), start=True, stop=True)
                m.then_inc(self.pv.sem, 1)

            def v_read(self, i):
                return [self.v_ready.at(i + 1)]

            def y_pe(self, pe, job):
                i, n = job.i, job.n
                pe.wait_ge(*self.yn.at(i + 1))
                if job.ago(2):
                    pe.wait_ge(*job.ago(2).x_read())
                if job.before:
                    pe.wait_ge(*job.before.r_read())
                pe.transpose(PS[:, B_OX, 0:P], ysb[:, n % 2, :], ident).then_inc(self.y_mm.sem, 1)

            def o_pe(self, pe, job):
                pe.wait_ge(*self.yt.at(job.i + 1))
                pe.matmul(PS[:, B_OX, P:2 * P], yT[:, job.n % 2, :], WT[:, self.w + 3, :],
                          start=True, stop=True).then_inc(self.o_mm.sem, 1)

            def qk_act(self, act, job):
                i, n, ab = job.i, job.n, self.bias
                if ab == 1 and i == 0:
                    act.wait_ge(s_b[1], 16 * NB)
                if self.rope:
                    for qk, bank, s, d in ((1, B_K, self.k_mm, self.tmpk), (0, B_Q, self.q_mm, self.tmpq)):
                        act.wait_ge(*s.at(i + 1))
                        if i >= 2:
                            act.wait_ge(*self.cosd.at(i - 1))
                            act.wait_ge(*self.shuf.at(i - 1))
                        for g in range(2):
                            m = act.activation(TMP[:, n % 2, 2 * (1 - qk) + g, :], PS[:, bank, 64 * g:64 * g + 64],
                                               ACT.Identity, bias=qkb[:, ab, qk, g:g + 1])
                        m.then_inc(d.sem, 1)
                    return
                act.wait_ge(*self.q_mm.at(i + 1))
                if job.ago(3):
                    act.wait_ge(*job.ago(3).stage.s_mm.at(job.ago(3).i + 1))
                act.wait_ge(s_z, 2)
                for b in range(2):
                    rows = slice(64 * b, 64 * b + 64)
                    if ab is None:
                        m = act.activation(QS[rows, n % 3, :, 64 * b:64 * b + 64],
                                           PS[rows, B_Q, 0:P].rearrange("p (g q) -> p g q", g=2), ACT.Copy)
                    else:
                        for g in range(2):
                            m = act.activation(QS[rows, n % 3, g, 64 * b:64 * b + 64], PS[rows, B_Q, 64 * g:64 * g + 64],
                                               ACT.Identity, bias=qkb[rows, ab, 0, g:g + 1])
                m.then_inc(self.q_ready.sem, 1)

            def v_act(self, act, job):
                i, n = job.i, job.n
                act.wait_ge(*self.v_mm.at(i + 1))
                act.wait_ge(s_z, 6)
                if job.ago(3):
                    act.wait_ge(*job.ago(3).pt_used())
                for a in range(2):
                    rows = slice(64 * a, 64 * a + 64)
                    m = act.activation(VB[rows, n % 3, :, :, a, 0:DH].rearrange("p r b d -> p b r d"),
                                       PS[rows, B_Y, 384:512].rearrange("p (b r d) -> p b r d", b=2, d=DH), ACT.Copy)
                m.then_inc(self.v_ready.sem, 1)

            def y_act(self, act, job):
                i, n = job.i, job.n
                act.wait_ge(*self.y_mm.at(i + 1))
                if i >= 2:
                    act.wait_ge(*self.o_mm.at(i - 1))
                if self.bias is None:
                    m = act.activation(yT[:, n % 2, :], PS[:, B_OX, 0:P], ACT.Copy)
                else:
                    m = act.activation(yT[:, n % 2, :], PS[:, B_OX, 0:P], ACT.Identity, bias=bvc[:, self.bias:self.bias + 1])
                m.then_inc(self.yt.sem, 1)

            def qk_dve(self, dve, job):
                i, n, ab = job.i, job.n, self.bias
                if self.rope:
                    swap = [p ^ 1 for p in range(32)]
                    dve.wait_ge(*self.tmpq.at(i + 1))
                    dve.stream_shuffle(TS[:, n % 2].rearrange("p n k -> p (n k)"),
                                       TMP[:, n % 2].rearrange("p n k -> p (n k)"), swap).then_inc(self.shuf.sem, 1)
                    dve.wait_ge(*self.shuf.at(i + 1))
                    dve.tensor_tensor(TS[:, n % 2], TS[:, n % 2], bc(cst[:, C_SIN:C_SIN + SEQ], 1, 4), ALU.mult)\
                       .then_inc(self.sind.sem, 1)
                    dve.wait_ge(*self.sind.at(i + 1))
                    dve.wait_ge(*self.cosd.at(i + 1))
                    if i >= 2:
                        dve.wait_ge(*self.kb.at(2 * (i - 1)))
                    dve.tensor_tensor(KT[:, n % 2], TC[:, n % 2, 0:2], TS[:, n % 2, 0:2], ALU.add).then_inc(self.k_ready.sem, 1)
                    if i >= 3:
                        dve.wait_ge(*self.s_mm.at(i - 2))
                    dve.wait_ge(s_z, 2)
                    for b in range(2):
                        rows = slice(64 * b, 64 * b + 64)
                        m = dve.tensor_tensor(QS[rows, n % 3, :, 64 * b:64 * b + 64], TC[rows, n % 2, 2:4],
                                              TS[rows, n % 2, 2:4], ALU.add)
                    m.then_inc(self.q_ready.sem, 1)
                    return
                dve.wait_ge(s_mk, 1)
                if ab == 1 and i == 0:
                    dve.wait_ge(s_b[1], 16 * NB)
                dve.wait_ge(*self.k_mm.at(i + 1))
                if job.ago(2):
                    dve.wait_ge(*job.ago(2).kt_used())
                if ab is None:
                    m = dve.tensor_tensor(KT[:, n % 2], PS[:, B_K, 0:P].rearrange("p (g k) -> p g k", g=2),
                                          bc(mk[:, i, :], 1, 2), ALU.mult)
                else:
                    for g in range(2):
                        m = dve.scalar_tensor_tensor(KT[:, n % 2, g], PS[:, B_K, 64 * g:64 * g + 64],
                                                     qkb[:, ab, 1, g:g + 1], mk[:, i, :], ALU.add, ALU.mult)
                m.then_inc(self.k_ready.sem, 1)

            def kt_used(self, i):
                return self.kb.at(2 * i + 2)

            def y_dve(self, dve, job):
                i, n = job.i, job.n
                dve.wait_ge(*self.pv.at(i + 1))
                y = PS[:, B_Y, 0:(DH + 1) * HEADS].rearrange("q (h e) -> q h e", e=DH + 1)
                dve.reciprocal(rs[:, n % 2, :], y[:, :, DH]).then_inc(self.rec.sem, 1)
                dve.wait_ge(*self.rec.at(i + 1))
                if i >= 2:
                    dve.wait_ge(*self.y_mm.at(i - 1))
                dve.tensor_tensor(ysb[:, n % 2, :].rearrange("q (h d) -> q h d", d=DH), y[:, :, 0:DH],
                                  bc(rs[:, n % 2, :], 2, DH), ALU.mult).then_inc(self.yn.sem, 1)

            def blocks_pool(self, pool, job):
                i, n = job.i, job.n
                pool.wait_ge(*self.k_ready.at(i + 1))
                if job.ago(2):
                    pool.wait_ge(*job.ago(2).kb_used())
                for g in range(2):
                    pool.tensor_tensor(KB[:, n % 2, g], bc(KT[:, n % 2, g, :], 1, 8),
                                       bc(cst[:, C_HEAD:C_HEAD + 8], 2, SEQ), ALU.mult).then_inc(self.kb.sem, 1)

            def kb_used(self, i):
                return self.s_mm.at(i + 1)

            def cos_pool(self, pool, job):
                if self.rope:
                    i, n = job.i, job.n
                    pool.wait_ge(*self.tmpq.at(i + 1))
                    if i >= 2:
                        pool.wait_ge(*self.q_ready.at(i - 1))
                    pool.tensor_tensor(TC[:, n % 2], TMP[:, n % 2], bc(cst[:, C_COS:C_COS + SEQ], 1, 4), ALU.mult)\
                        .then_inc(self.cosd.sem, 1)
                    pool.tensor_tensor(XR[:, i, :], X[:, i, :], rowb[:, 0, :], ALU.add).then_inc(self.res.sem, 1)

            def bias_pool(self, pool, job):
                if self.next_row is not None:
                    i = job.i
                    if i == 0 and self.next_row == 2:
                        pool.wait_ge(*fc.bias.at(1))
                    elif i == 0:
                        pool.wait_ge(s_b[1], 16 * NB)
                    pool.wait_ge(*self.norm.ln.at(i + 1))
                    pool.tensor_tensor(XR[:, i, :], X[:, i, :], rowb[:, self.next_row, :], ALU.add).then_inc(self.norm.xr.sem, 1)

        class Wide(Stage):
            wide = True

            def __init__(self, name):
                self.scale, self.row = float(DW) ** -0.5, None
                self.f_mm, self.f_act, self.f_dve = Mark("wide_projected"), Mark("wide_copied_act"), Mark("wide_copied_dve")
                self.s_mm = Mark("scored", NT)
                self.max, self.sub, self.exp = Mark("row_max_made", NT), Mark("max_subtracted", NT), Mark("exponentials_made", NT)
                self.sum, self.rec = Mark("wide_summed", NT), Mark("reciprocals_made", NT)
                self.yn, self.y_mm = Mark("y_normalized", 2 * NT), Mark("y_transposed", 2 * NT)
                self.t_mm, self.pt, self.pv = Mark("p_transposed", 2 * NT), Mark("pT_copied", 2 * NT), Mark("v_weighed", 2 * NT)
                self.yt, self.o_mm = Mark("yT_copied", 2 * NT), Mark("y_projected", NT)
                self.norm = Norm(name)

            def pt_used(self, i):
                return self.pv.at(2 * i + 2)

            def y_read(self, i):
                return self.yt.at(2 * i + 2)

            def kt_used(self, i):
                return self.s_mm.at(i + 1)

            kb_used = kt_used

            def v_read(self, i):
                return self.fills_read(self.v_fill(i) + 1)

            def fills_read(self, f):
                return [self.f_act.at(f // 2 + 1), self.f_dve.at((f + 1) // 2)]

            def qk_read(self, i):
                return self.fills_read(self.qk_fill(i) + 3)

            def qk_fill(self, i):
                return 6 * i - 2 if i else 0

            def v_fill(self, i):
                return 6 * i + 8 if i < NT - 1 else 6 * NT - 2

            def fill(self, pe, f):
                if f >= 2:
                    pe.wait_ge(*self.fills_read(f - 2)[f % 2])
                return B_K + f % 2

            def qkw_pe(self, pe, job):
                i = job.i
                pe.wait_ge(*self.input.xev.at(i + 1))
                if i == 0:
                    pe.wait_ge(s_wide, 32)
                w = WQKV[:, :].rearrange("f (m c) -> f c m", c=3)
                for f in range(4):
                    bank = self.fill(pe, self.qk_fill(i) + f)
                    for k in range(4):
                        u = 4 * (f % 2) + k
                        m = pe.matmul(PS[:, bank, P * k:P * (k + 1)], w[:, f // 2, P * u:P * (u + 1)],
                                      XT[:, P * i:P * (i + 1)], start=True, stop=True)
                    m.then_inc(self.f_mm.sem, 1)

            def v_pe(self, pe, job):
                i = job.i
                w = WQKV[:, :].rearrange("f (u a d c) -> f c a u d", c=3, a=2, d=DW)
                for b in range(2):
                    bank = self.fill(pe, self.v_fill(i) + b)
                    if b == 0 and job.after and not job.after.stage.wide:
                        for s in job.after.stage.qk_read(job.after.i):
                            pe.wait_ge(*s)
                    for a in range(2):
                        m = pe.matmul(PS[64 * a:64 * a + 64, bank, :], XT[:, SEQ * (2 * i + b):SEQ * (2 * i + b + 1)],
                                      w[:, 2, a], start=True, stop=True)
                    m.then_inc(self.f_mm.sem, 1)

            def s_pe(self, pe, job):
                i, n = job.i, job.n
                for s in self.fills_read(self.qk_fill(i) + 3):
                    pe.wait_ge(*s)
                if job.before:
                    pe.wait_ge(*job.before.s_read())
                for a in range(2):
                    rows = slice(64 * a, 64 * a + 64)
                    for b in range(2):
                        for u in range(PAIRS):
                            m = pe.matmul(PS[64 * b:64 * b + 64, B_S + a, SEQ * u:SEQ * (u + 1)],
                                          QK[rows, n % 2, 0, u, 64 * b:64 * b + 64], QK[rows, n % 2, 1, u, 64 * b:64 * b + 64],
                                          start=True, stop=True)
                m.then_inc(self.s_mm.sem, 1)

            def weigh(self, pe, job, m):
                i, n = job.i, job.n
                pe.wait_ge(*self.pt.at(2 * i + 2))
                for s in self.v_read(i):
                    pe.wait_ge(*s)
                if m == 1:
                    pe.wait_ge(*self.yt.at(2 * i + 1))
                else:
                    if job.after2:
                        for s in job.after2.v_read():
                            pe.wait_ge(*s)
                    if job.before:
                        pe.wait_ge(*job.before.y_read())
                for b in range(2):
                    for r in range(4 * m, 4 * m + 4):
                        t = pe.matmul(PS[64 * b:64 * b + 64, B_Y, P * (r % 4):P * (r % 4 + 1)], PT[:, n % 2, r, 64 * b:64 * b + 64],
                                      VW[:, n % 3, b, r].rearrange("p a d -> p (a d)"), start=True, stop=True)
                t.then_inc(self.pv.sem, 1)

            def turn(self, pe, job, m):
                pe.wait_ge(*self.yn.at(2 * job.i + m + 1))
                for c in range(4):
                    t = pe.transpose(PS[:, B_Y, P * c:P * (c + 1)], YN[:, m, P * c:P * (c + 1)], ident)
                t.then_inc(self.y_mm.sem, 1)

            def ty_pe(self, pe, job):
                self.turn(pe, job, 0)

            def y_pe(self, pe, job):
                self.turn(pe, job, 1)

            def va_pe(self, pe, job):
                self.weigh(pe, job, 0)

            def vb_pe(self, pe, job):
                self.weigh(pe, job, 1)

            def o_pe(self, pe, job):
                i, n = job.i, job.n
                pe.wait_ge(*self.yt.at(2 * i + 2))
                if job.before:
                    pe.wait_ge(*job.before.r_read())
                if job.ago(2):
                    pe.wait_ge(*job.ago(2).x_read())
                for u in range(PAIRS):
                    m = pe.matmul(PS[:, B_OX, P:2 * P], YW[n % 2][:, u, :], WOUT[:, u, :],
                                  start=(u == 0), stop=(u == PAIRS - 1))
                m.then_inc(self.o_mm.sem, 1)

            def copy(self, eng, part, o, s):
                return eng.activation(o, s, ACT.Copy) if part == 0 else eng.tensor_copy(o, s)

            def qkw_copies(self, eng, part, job):
                i, n = job.i, job.n
                if i >= 2:
                    eng.wait_ge(*self.s_mm.at(i - 1))
                for c in range(2):
                    f = self.qk_fill(i) + 2 * c + part
                    eng.wait_ge(*self.f_mm.at(f + 1))
                    self.copy(eng, part, QK[:, n % 2, c, 4 * part:4 * part + 4, :].rearrange("p u t -> p (u t)"),
                              PS[:, B_K + part, :]).then_inc((self.f_act, self.f_dve)[part].sem, 1)

            def vw_copies(self, eng, part, job):
                i, n = job.i, job.n
                if i >= 3:
                    eng.wait_ge(*self.pv.at(2 * (i - 2)))
                eng.wait_ge(s_wz, 1)
                eng.wait_ge(*self.f_mm.at(self.v_fill(i) + part + 1))
                for a in range(2):
                    rows = slice(64 * a, 64 * a + 64)
                    m = self.copy(eng, part, VW[rows, n % 3, part, :, a, :],
                                  PS[rows, B_K + part, :].rearrange("p (u d) -> p u d", d=DW))
                m.then_inc((self.f_act, self.f_dve)[part].sem, 1)

            def ya_act(self, act, job, m=0):
                i, n = job.i, job.n
                act.wait_ge(*self.y_mm.at(2 * i + m + 1))
                if i >= 2:
                    act.wait_ge(*self.o_mm.at(i - 1))
                act.activation(YW[n % 2][:, 4 * m:4 * m + 4, :].rearrange("p u q -> p (u q)"),
                               PS[:, B_Y, :], ACT.Copy).then_inc(self.yt.sem, 1)

            def y_act(self, act, job):
                self.ya_act(act, job, 1)

            def ya_dve(self, dve, job, m=0):
                i, n = job.i, job.n
                dve.wait_ge(*self.pv.at(2 * i + m + 1))
                dve.wait_ge(*self.rec.at(i + 1))
                if i >= 1:
                    dve.wait_ge(*self.y_mm.at(2 * i + m - 1))
                dve.tensor_tensor(YN[:, m].rearrange("q (h d) -> q h d", d=DW), PS[:, B_Y, :].rearrange("q (h d) -> q h d", d=DW),
                                  bc(rs[:, n % 2, 8 * m:8 * m + 8], 2, DW), ALU.mult).then_inc(self.yn.sem, 1)

            def y_dve(self, dve, job):
                self.ya_dve(dve, job, 1)

            def sum_dve(self, dve, job):
                i, n = job.i, job.n
                dve.wait_ge(*self.exp.at(i + 1))
                s = PR[:, n % 2, :].rearrange("q (h k) -> q h k", k=SEQ)
                dve.tensor_reduce(mx[:, n % 2, :], s, AX.X, ALU.add).then_inc(self.sum.sem, 1)
                dve.wait_ge(*self.sum.at(i + 1))
                if i >= 2:
                    dve.wait_ge(*self.yn.at(2 * i - 2))
                dve.reciprocal(rs[:, n % 2, :], mx[:, n % 2, :]).then_inc(self.rec.sem, 1)

        class Ternary(Stage):
            def __init__(self, name):
                self.row = 2
                self.blocks, self.b_mm, self.bias, self.scaled = (
                    Mark("norm_biases_spread"), Mark("norm_biases_projected"), Mark("output_bias_made"), Mark("projection_scaled"))
                self.abs, self.gsum, self.thr, self.low = (
                    Mark("magnitudes_summed"), Mark("magnitude_totals_made"), Mark("thresholds_made"), Mark("negatives_found"))
                self.h_mm, self.gelu, self.st, self.mv = (
                    Mark("hidden_projected"), Mark("gelu_made"), Mark("hidden_stats_made"), Mark("hidden_variance_made"))
                self.ve, self.rstd, self.n = Mark("hidden_eps_added"), Mark("hidden_rstd_made"), Mark("hidden_normed")
                self.t_mm, self.ht, self.o_mm = Mark("hidden_transposed"), Mark("hiddenT_copied"), Mark("ternary_projected")
                self.norm = Norm(name)

            def s_read(self, i):
                return self.gelu.at(i + 1)

            def magnitudes(self, dve):
                dve.wait_ge(s_fc, 64)
                for n in range(2):
                    dve.tensor_reduce(gam[:, n:n + 1], FCW[:, n].rearrange("p c f -> p (c f)"), AX.X, ALU.add,
                                      apply_absolute_value=True).then_inc(self.abs.sem, 1)

            def totals(self, pe, bank_read):
                pe.wait_ge(*bank_read)
                pe.wait_ge(*self.abs.at(2))
                pe.matmul(PS[:, 6, 0:2], cst[:, C_ONES:C_ONES + P], gam[:, 0:2], start=True, stop=True)\
                    .then_inc(self.gsum.sem, 1)

            def thresholds(self, dve):
                dve.wait_ge(*self.gsum.at(1))
                for s in (0.5, -0.5):
                    k = 2 if s > 0 else 4
                    dve.tensor_scalar(gam[:, k:k + 2], PS[:, 6, 0:2], s / (P * INNER), s * 1e-6, ALU.mult, ALU.add)\
                       .then_inc(self.thr.sem, 1)

            def quantize(self, dve):
                dve.wait_ge(*self.thr.at(2))
                for n in range(2):
                    w = FCW[:, n].rearrange("p c f -> p (c f)")
                    dve.tensor_scalar(FA[:, n, :], w, gam[:, 4 + n:5 + n], None, ALU.is_lt).then_inc(self.low.sem, 1)
                dve.wait_ge(*self.low.at(2))
                for n in range(2):
                    w = FCW[:, n].rearrange("p c f -> p (c f)")
                    dve.scalar_tensor_tensor(w, w, gam[:, 2 + n:3 + n], FA[:, n, :], ALU.is_gt, ALU.subtract)\
                       .then_inc(s_tern, 1)

            def spread(self, dve):
                dve.tensor_copy(LB, bc(lnwb[:, 1, :], 2, P)).then_inc(self.blocks.sem, 1)

            def project_bias(self, pe):
                pe.wait_ge(*self.blocks.at(1))
                fct.done(pe)
                for c in range(CH):
                    m = pe.matmul(PS[:, 6, 0:P], LB[:, c, :], FCT[:, 1, c, :], start=(c == 0), stop=(c == CH - 1))
                m.then_inc(self.b_mm.sem, 1)

            def fold(self, dve):
                dve.wait_ge(*self.b_mm.at(1))
                dve.tensor_copy(rowb[:, 2, :], PS[:, 6, 0:P]).then_inc(self.bias.sem, 1)
                fct.done(dve)
                for c in range(CH):
                    dve.tensor_scalar(FCT[:, 1, c, :], FCT[:, 1, c, :], lnwb[:, 0, c:c + 1], None, ALU.mult)\
                       .then_inc(self.scaled.sem, 1)

            def s_pe(self, pe, job):
                i = job.i
                pe.wait_ge(*self.input.xev.at(i + 1))
                if i == 0:
                    pe.wait_ge(*self.scaled.at(CH))
                if i < 2:
                    pe.wait_ge(*job.ago(i + 1).s_read())
                else:
                    pe.wait_ge(*self.gelu.at(i - 1))
                pe.matmul(PS[:, B_S + i % 2, :], XT[:, P * i:P * (i + 1)], FCT[:, 0].rearrange("p c f -> p (c f)"),
                          start=True, stop=True).then_inc(self.h_mm.sem, 1)

            def t_pe(self, pe, job):
                pass

            def pt_act(self, act, job):
                pass

            def max_dve(self, dve, job):
                pass

            def exp_act(self, act, job):
                i = job.i
                act.wait_ge(*self.h_mm.at(i + 1))
                if i >= 2:
                    act.wait_ge(*self.n.at(i - 1))
                act.activation(FH[:, i % 2, :], PS[:, B_S + i % 2, :], ACT.Gelu).then_inc(self.gelu.sem, 1)

            def sum_dve(self, dve, job):
                i = job.i
                dve.wait_ge(*self.gelu.at(i + 1))
                dve.bn_stats(hst[:, i % 2, 0:6], FH[:, i % 2, :]).then_inc(self.st.sem, 1)
                dve.wait_ge(*self.st.at(i + 1))
                dve.bn_aggr(hst[:, i % 2, 8:10], hst[:, i % 2, 0:6]).then_inc(self.mv.sem, 1)

            def hidden_pool(self, pool, job):
                i = job.i
                pool.wait_ge(*self.mv.at(i + 1))
                pool.tensor_scalar(hst[:, i % 2, 12:13], hst[:, i % 2, 9:10], LN_EPS, None, ALU.add).then_inc(self.ve.sem, 1)
                pool.wait_ge(*self.ve.at(i + 1))
                pool.tensor_tensor(hst[:, i % 2, 13:14], hst[:, i % 2, 12:13], half[:, :], ALU.pow).then_inc(self.rstd.sem, 1)

            def hidden_dve(self, dve, job):
                i = job.i
                dve.wait_ge(*self.rstd.at(i + 1))
                if i >= 2:
                    dve.wait_ge(*self.t_mm.at(i - 1))
                dve.tensor_scalar(FN[:, i % 2, :], FH[:, i % 2, :], hst[:, i % 2, 8:9], hst[:, i % 2, 13:14],
                                  ALU.subtract, ALU.mult).then_inc(self.n.sem, 1)
                dve.wait_ge(*self.n.at(i + 1))

            def va_pe(self, pe, job):
                i = job.i
                pe.wait_ge(*self.n.at(i + 1))
                if i >= 2:
                    pe.wait_ge(*self.ht.at(i - 1))
                else:
                    pe.wait_ge(*job.ago(i + 1).pt_read(i))
                for c in range(CH):
                    m = pe.transpose(PS[:, B_PT + i % 2, P * c:P * (c + 1)], FN[:, i % 2, P * c:P * (c + 1)], ident)
                m.then_inc(self.t_mm.sem, 1)

            def ya_act(self, act, job):
                i = job.i
                act.wait_ge(*self.t_mm.at(i + 1))
                if i >= 2:
                    act.wait_ge(*self.o_mm.at(i - 1))
                act.activation(FT[:, i % 2].rearrange("p c t -> p (c t)"), PS[:, B_PT + i % 2, :], ACT.Copy).then_inc(self.ht.sem, 1)

            def o_pe(self, pe, job):
                i = job.i
                pe.wait_ge(*self.ht.at(i + 1))
                if job.before:
                    pe.wait_ge(*job.before.r_read())
                if job.ago(2) and job.ago(2).stage is not self:
                    pe.wait_ge(*job.ago(2).x_read())
                for c in range(CH):
                    m = pe.matmul(PS[:, B_OX, P:2 * P], FT[:, i % 2, c, :], FCT[:, 1, c, :], start=(c == 0), stop=(c == CH - 1))
                m.then_inc(self.o_mm.sem, 1)

            def x_pe(self, pe, job):
                pass

            def x_act(self, act, job):
                pass

        class Tile:

            def __init__(self, stage, i, n, stream):
                self.stage, self.i, self.n, self.stream = stage, i, n, stream

            def ago(self, k):
                return self.stream[self.n - k] if self.n >= k else None

            @property
            def before(self):
                return self.ago(1)

            @property
            def after(self):
                return self.stream[self.n + 1] if self.n + 1 < len(self.stream) else None

            @property
            def after2_any(self):
                return self.stream[self.n + 2] if self.n + 2 < len(self.stream) else None

            @property
            def after2(self):
                t = self.after2_any
                return t if t and not isinstance(t.stage, Ternary) and not t.stage.wide else None

            def p_used(self):
                return self.stage.p_used(self.i)

            def pt_used(self):
                return self.stage.pt_used(self.i)

            def pt_read(self, m):
                return self.stage.pt_read(self.i, m)

            def s_read(self):
                return self.stage.s_read(self.i)

            def y_read(self):
                return self.stage.y_read(self.i)

            def v_read(self):
                return self.stage.v_read(self.i)

            def kt_used(self):
                return self.stage.kt_used(self.i)

            def kb_used(self):
                return self.stage.kb_used(self.i)

            def x_read(self):
                return self.stage.norm.xev.at(self.i + 1)

            def r_read(self):
                return self.stage.norm.r.at(self.i + 1)

        def stream_of(*stages):
            tiles = []
            for st in stages:
                for i in range(NT):
                    tiles.append(Tile(st, i, len(tiles), tiles))
            return tiles

        DEPTH = 6

        def at(tiles, j):
            return tiles[j] if 0 <= j < len(tiles) else None

        def stream_pe(pe, tiles, extra):
            for j in range(len(tiles) + DEPTH):
                a = at(tiles, j - 2)
                if a:
                    a.stage.s_pe(pe, a)
                y = at(tiles, j - 5)
                if y:
                    y.stage.y_pe(pe, y)
                b = at(tiles, j - 1)
                if b:
                    b.stage.qkw_pe(pe, b)
                b = at(tiles, j)
                after_v = a and a.stage.wide
                if b and not after_v:
                    b.stage.qk_pe(pe, b)
                if a:
                    a.stage.v_pe(pe, a)
                extra(pe, j, False)
                t, v = at(tiles, j - 3), at(tiles, j - 4)
                if v and v.stage.wide:
                    v.stage.va_pe(pe, v)
                if t:
                    t.stage.t_pe(pe, t)
                if v:
                    v.stage.ty_pe(pe, v)
                first_v = v and not v.stage.wide and y and y.stage.wide
                if first_v:
                    v.stage.va_pe(pe, v)
                if y:
                    y.stage.o_pe(pe, y)
                if v and not first_v and not v.stage.wide:
                    v.stage.va_pe(pe, v)
                if v:
                    v.stage.vb_pe(pe, v)
                if b and after_v:
                    b.stage.qk_pe(pe, b)
                x = at(tiles, j - 6)
                if x:
                    x.stage.x_pe(pe, x)
                extra(pe, j, True)

        def stream_act(act, tiles, extra):
            for j in range(len(tiles) + DEPTH):
                y = at(tiles, j - 5)
                if y:
                    y.stage.y_act(act, y)
                b, q, v = at(tiles, j), at(tiles, j - 1), at(tiles, j - 2)
                if q:
                    q.stage.qkw_copies(act, 0, q)
                after_v = v and v.stage.wide
                if b and not after_v:
                    b.stage.qk_act(act, b)
                if v:
                    v.stage.vw_copies(act, 0, v)
                    v.stage.v_act(act, v)
                extra(act, j, False)
                t = at(tiles, j - 3)
                if t:
                    t.stage.pt_act(act, t)
                w = at(tiles, j - 4)
                hidden = v and isinstance(v.stage, Ternary)
                if hidden:
                    v.stage.exp_act(act, v)
                if w:
                    w.stage.ya_act(act, w)
                if v and not hidden:
                    v.stage.exp_act(act, v)
                if b and after_v:
                    b.stage.qk_act(act, b)
                x = at(tiles, j - 6)
                if x:
                    x.stage.x_act(act, x)
                extra(act, j, True)

        def stream_dve(dve, tiles, extra):
            for j in range(len(tiles) + DEPTH):
                y = at(tiles, j - 5)
                if y:
                    y.stage.y_dve(dve, y)
                t, x = at(tiles, j - 3), at(tiles, j - 6)
                hidden = t and isinstance(t.stage, Ternary)
                if hidden:
                    t.stage.sum_dve(dve, t)
                if x:
                    x.stage.ln_dve(dve, x)
                if t and not hidden:
                    t.stage.sum_dve(dve, t)
                v = at(tiles, j - 2)
                if v:
                    v.stage.max_dve(dve, v)
                b, q = at(tiles, j), at(tiles, j - 1)
                if q:
                    q.stage.qkw_copies(dve, 1, q)
                if v:
                    v.stage.vw_copies(dve, 1, v)
                extra(dve, j, False)
                w = at(tiles, j - 4)
                if w:
                    w.stage.ya_dve(dve, w)
                if y:
                    y.stage.r_dve(dve, y)
                if hidden:
                    t.stage.hidden_dve(dve, t)
                if b:
                    b.stage.qk_dve(dve, b)
                extra(dve, j, True)

        def stream_pool(pool, tiles):
            for j in range(len(tiles) + DEPTH):
                b = at(tiles, j - 1)
                if b:
                    b.stage.blocks_pool(pool, b)
                b = at(tiles, j)
                if b:
                    b.stage.cos_pool(pool, b)
                t = at(tiles, j - 3)
                if t:
                    t.stage.hidden_pool(pool, t)
                y = at(tiles, j - 5)
                if y:
                    y.stage.rsqrt_pool(pool, y)
                x = at(tiles, j - 6)
                if x:
                    x.stage.bias_pool(pool, x)


        ROUNDS = [(0, 0), (1, 0), (0, 1), (1, 1)] + [(e, h) for e in range(2, EXPERTS) for h in range(2)]
        STEPS = 4 * len(ROUNDS)

        TERNARY = 42

        def down_step(m):
            return m + 6

        def turn_step(k):
            return down_step(4 * k + 3) + 2

        LAST = turn_step(len(ROUNDS) - 1) + 2


        class Experts:
            def __init__(self, prev):
                self.prev = prev
                self.gate_mm, self.gate_read = Mark("logits_made"), Mark("logits_copied")
                self.top, self.topi = Mark("logits_sorted"), Mark("experts_ranked")
                self.diff, self.e2, self.den = Mark("logit_difference_made"), Mark("second_exponential_made"), Mark("pair_sum_made")
                self.p1, self.p2, self.oh, self.comb = (
                    Mark("first_weight_made"), Mark("second_weight_made"), Mark("choices_made"), Mark("expert_weights_made"))
                self.g_mm, self.u_mm, self.silu, self.mul = (
                    Mark("gates_projected"), Mark("ups_projected"), Mark("silu_made"), Mark("hidden_made"))
                self.d_mm, self.acc = Mark("downs_projected"), Mark("expert_added")
                self.w_mm, self.w_hi, self.w_lo = (
                    Mark("expert_weights_transposed"), Mark("weights_high_made"), Mark("weights_low_made"))
                self.x_hi, self.x_lo = Mark("x_high_made"), Mark("x_low_made")
                self.h_hi, self.h_lo = Mark("hidden_high_made"), Mark("hidden_low_made")
                self.y_cp, self.y_mm = Mark("expert_output_copied"), Mark("expert_output_transposed")
                self.norm = Norm("experts")

            PARTS = ((0, 0), (0, 1), (1, 0))

            def weights_free(self, eng, g):
                e, w = g // 3, g % 3
                if e >= 2:
                    steps = 4 * (ROUNDS.index((e - 2, 1)) + 1)
                    eng.wait_ge(*(self.g_mm, self.u_mm, self.d_mm)[w].at(steps))

            def weights_pe(self, pe, g):
                e = g // 3
                if g % 3 == 0:
                    pe.wait_ge(s_raw[e % 4], 48 * (e // 4 + 1))
                if g >= 2:
                    pe.wait_ge(*self.w_lo.at(g - 1))
                for c in range(CH):
                    m = pe.transpose(PS[:, 6 + g % 2, P * c:P * (c + 1)], RAW[:, e % 4, g % 3, P * c:P * (c + 1)], ident)
                m.then_inc(self.w_mm.sem, 1)

            def weights_act(self, act, g):
                act.wait_ge(*self.w_mm.at(g + 1))
                self.weights_free(act, g)
                act.activation(WS[:, g // 3 % 2, g % 3, 0, :], PS[:, 6 + g % 2, :], ACT.Copy).then_inc(self.w_hi.sem, 1)

            def weights_dve(self, dve, g):
                dve.wait_ge(*self.w_hi.at(g + 1))
                w = WS[:, g // 3 % 2, g % 3]
                dve.tensor_tensor(w[:, 1, :], PS[:, 6 + g % 2, :], w[:, 0, :], ALU.subtract).then_inc(self.w_lo.sem, 1)

            def later_weights(self, n):
                for e in range(2, EXPERTS):
                    steps = 4 * (ROUNDS.index((e - 2, 1)) + 1)
                    if n == steps + (4 if e == 3 else 1):
                        return [3 * e, 3 * e + 1]
                    if n == down_step(steps - 1) + 1:
                        return [3 * e + 2]
                return []

            def gate_up(self, pe, n):
                k, c = n // 4, n % 4
                e, h = ROUNDS[k]
                if c == 0:
                    pe.wait_ge(*self.w_lo.at(3 * e + 2))
                    pe.wait_ge(*self.x_lo.at(h + 1))
                if n >= 2:
                    pe.wait_ge(*self.silu.at(n - 1))
                    pe.wait_ge(*self.mul.at(n - 1))
                for bank, w, s in ((n % 2, 0, self.g_mm), (2 + n % 2, 1, self.u_mm)):
                    for q, (a, b) in enumerate(self.PARTS):
                        m = pe.matmul(PS[:, bank, :], WS[:, e % 2, w, a, P * c:P * (c + 1)], XS[:, b, BANK * h:BANK * (h + 1)],
                                      start=(q == 0), stop=(q == 2))
                    m.then_inc(s.sem, 1)

            def down(self, pe, m):
                k, c = m // 4, m % 4
                pe.wait_ge(*self.h_lo.at(m + 1))
                if c == 0:
                    pe.wait_ge(*self.w_lo.at(3 * ROUNDS[k][0] + 3))
                if c == 0 and k >= 2:
                    pe.wait_ge(*self.acc.at(4 * (k - 1)))
                for q, (a, b) in enumerate(self.PARTS):
                    t = pe.matmul(PS[:, 4 + k % 2, :], WS[:, ROUNDS[k][0] % 2, 2, a, P * c:P * (c + 1)], HS[:, k % 2, b, c, :],
                                  start=(c == 0 and q == 0), stop=(c == CH - 1 and q == 2))
                t.then_inc(self.d_mm.sem, 1)

            def turn_pe(self, pe, k):
                pe.wait_ge(*self.y_cp.at(k + 1))
                for t in range(4):
                    m = pe.transpose(PS[:, 4 + k % 2, P * t:P * (t + 1)], YE[:, P * t:P * (t + 1)], ident)
                m.then_inc(self.y_mm.sem, 1)

            def turn_act(self, act, k):
                act.wait_ge(*self.d_mm.at(4 * k + 4))
                if k >= 1:
                    act.wait_ge(*self.y_mm.at(k))
                act.activation(YE, PS[:, 4 + k % 2, :], ACT.Copy).then_inc(self.y_cp.sem, 1)

            def step_pe(self, pe, n):
                if n == 0:
                    last = pre[-1]
                    pe.wait_ge(*last.s_read())
                    pe.wait_ge(*last.pt_read(1))
                if n < STEPS:
                    self.gate_up(pe, n)
                for m in range(STEPS):
                    if down_step(m) == n:
                        self.down(pe, m)
                for k in range(len(ROUNDS)):
                    if turn_step(k) == n:
                        self.turn_pe(pe, k)
                for g in self.later_weights(n):
                    if g == 6:
                        pe.wait_ge(*self.gate_read.at(1))
                    if g == 3 * (EXPERTS - 1) + 1:
                        pe.wait_ge(*fc.thr.at(2))
                    self.weights_pe(pe, g)
                if n == TERNARY + 5:
                    fc.totals(pe, self.w_lo.at(3 * (EXPERTS - 1)))
                if n == TERNARY + 16:
                    pe.wait_ge(*self.w_lo.at(3 * EXPERTS))
                    fct.pe(pe)
                if n == TERNARY + 18:
                    fc.project_bias(pe)

            def step_act(self, act, n):
                if n < STEPS:
                    act.wait_ge(*self.g_mm.at(n + 1))
                    if n >= 2:
                        act.wait_ge(*self.mul.at(n - 1))
                    act.activation(SG[:, n % 2, :], PS[:, n % 2, :], ACT.Silu).then_inc(self.silu.sem, 1)
                if 1 <= n <= STEPS:
                    self.hidden_high(act, n - 1)
                for k in range(len(ROUNDS)):
                    if turn_step(k) == n + 1:
                        self.turn_act(act, k)
                for g in self.later_weights(n):
                    self.weights_act(act, g)
                if n == TERNARY + 16:
                    fct.copies(act, 0)
                if n == 9:
                    act.wait_ge(*self.diff.at(1))
                    act.activation(pk[:, 1, :], pk[:, 0, :], ACT.Exp).then_inc(self.e2.sem, 1)

            def step_dve(self, dve, n):
                if n < STEPS:
                    dve.wait_ge(*self.silu.at(n + 1))
                    dve.wait_ge(*self.u_mm.at(n + 1))
                    if n >= 2:
                        dve.wait_ge(*self.h_lo.at(n - 1))
                    dve.tensor_tensor(HF[:, n % 2, :], PS[:, 2 + n % 2, :], SG[:, n % 2, :], ALU.mult).then_inc(self.mul.sem, 1)
                if 1 <= n <= STEPS:
                    self.hidden_low(dve, n - 1)
                for g in self.later_weights(n):
                    self.weights_dve(dve, g)
                for k in range(len(ROUNDS)):
                    if turn_step(k) == n - 1:
                        self.accumulate(dve, k)
                if n == turn_step(len(ROUNDS) - 2) + 2:
                    self.statistics(dve, 0)
                if n == turn_step(len(ROUNDS) - 2) + 3:
                    self.apply(dve, 0)
                if n == 10:
                    self.route(dve)
                if n == TERNARY:
                    fc.magnitudes(dve)
                if n == TERNARY + 5:
                    fc.thresholds(dve)
                if n == TERNARY + 7:
                    fc.quantize(dve)
                if n == TERNARY + 16:
                    fct.copies(dve, 1)
                    fc.spread(dve)
                if n == TERNARY + 19:
                    fc.fold(dve)

            def x_high(self, act, h):
                act.wait_ge(*self.prev.xev.at(4 * h + 4))
                act.activation(XS[:, 0, BANK * h:BANK * (h + 1)], XT[:, BANK * h:BANK * (h + 1)], ACT.Copy)\
                   .then_inc(self.x_hi.sem, 1)

            def x_low(self, dve, h):
                dve.wait_ge(*self.x_hi.at(h + 1))
                x = slice(BANK * h, BANK * (h + 1))
                dve.tensor_tensor(XS[:, 1, x], XT[:, x], XS[:, 0, x], ALU.subtract).then_inc(self.x_lo.sem, 1)

            def pe(self, pe):
                pe.wait_ge(*self.prev.xev.at(NT))
                pe.wait_ge(*self.w_lo.at(6))
                for t in range(NT):
                    m = pe.matmul(PS[:, 6, 8 * t:8 * t + 8], XT[:, P * t:P * (t + 1)], gwT[:, :], start=True, stop=True)
                m.then_inc(self.gate_mm.sem, 1)
                for n in range(EARLY, LAST):
                    self.step_pe(pe, n)
                pe.wait_ge(*fc.bias.at(1))
                self.x_pe(pe, 0)

            def x_pe(self, pe, h):
                for i in range(4 * h, 4 * h + 4):
                    pe.wait_ge(*self.norm.ln.at(i + 1))
                    if i >= 2:
                        pe.wait_ge(*self.norm.xev.at(i - 1))
                    pe.transpose(PS[:, i % 2, 0:P], X[:, i, :], ident).then_inc(self.norm.xmm.sem, 1)
                if h == 1:
                    pe.wait_ge(*self.norm.xev.at(NT))

            def x_act(self, act, h):
                for i in range(4 * h, 4 * h + 4):
                    act.wait_ge(*self.norm.xmm.at(i + 1))
                    act.activation(XT[:, i * P:(i + 1) * P], PS[:, i % 2, 0:P], ACT.Copy).then_inc(self.norm.xev.sem, 1)

            def hidden_high(self, act, n):
                k, c = n // 4, n % 4
                act.wait_ge(*self.mul.at(n + 1))
                if k >= 2:
                    act.wait_ge(*self.d_mm.at(n - 7))
                act.activation(HS[:, k % 2, 0, c, :], HF[:, n % 2, :], ACT.Copy).then_inc(self.h_hi.sem, 1)

            def hidden_low(self, dve, n):
                k, c = n // 4, n % 4
                dve.wait_ge(*self.h_hi.at(n + 1))
                dve.tensor_tensor(HS[:, k % 2, 1, c, :], HF[:, n % 2, :], HS[:, k % 2, 0, c, :], ALU.subtract)\
                   .then_inc(self.h_lo.sem, 1)

            def act(self, act):
                self.x_high(act, 1)
                for n in range(EARLY, LAST):
                    self.step_act(act, n)
                self.x_act(act, 0)

            def largest(self, dve):
                dve.wait_ge(*self.gate_mm.at(1))
                dve.tensor_copy(lg[:, :, :].rearrange("p t e -> p (t e)"), PS[:, 6, 0:8 * NT]).then_inc(self.gate_read.sem, 1)
                dve.wait_ge(*self.gate_read.at(1))
                for t in range(NT):
                    dve.max(top[:, t, :], lg[:, t, :]).then_inc(self.top.sem, 1)
                dve.wait_ge(*self.top.at(NT))
                dve.tensor_tensor(pk[:, 0, :], top[:, :, 1], top[:, :, 0], ALU.subtract).then_inc(self.diff.sem, 1)

            def route(self, dve):
                for t in range(NT):
                    dve.max_index(topi[:, t, :], top[:, t, :], lg[:, t, :]).then_inc(self.topi.sem, 1)
                dve.wait_ge(*self.topi.at(NT))
                dve.tensor_copy(topf[:, :, :], topi[:, :, 0:2]).then_inc(self.topi.sem, 1)
                dve.wait_ge(*self.e2.at(1))
                dve.tensor_scalar(pk[:, 2, :], pk[:, 1, :], 1.0, None, ALU.add).then_inc(self.den.sem, 1)
                dve.wait_ge(*self.den.at(1))
                dve.reciprocal(pk[:, 2, :], pk[:, 2, :]).then_inc(self.p1.sem, 1)
                dve.wait_ge(*self.p1.at(1))
                dve.tensor_tensor(pk[:, 3, :], pk[:, 1, :], pk[:, 2, :], ALU.mult).then_inc(self.p2.sem, 1)
                dve.wait_ge(*self.p2.at(1))
                dve.wait_ge(*self.topi.at(NT + 1))
                for r in range(2):
                    dve.tensor_tensor(comb[:, r], bc(cst[:, C_IOTA:C_IOTA + 8], 1, NT), bc(topf[:, :, r], 2, 8),
                                      ALU.is_equal).then_inc(self.oh.sem, 1)
                dve.wait_ge(*self.oh.at(2))
                for r in range(2):
                    dve.tensor_tensor(comb[:, r], comb[:, r], bc(pk[:, 2 + r, :], 2, 8), ALU.mult).then_inc(self.oh.sem, 1)
                dve.wait_ge(*self.oh.at(4))
                dve.tensor_tensor(comb[:, 0], comb[:, 0], comb[:, 1], ALU.add).then_inc(self.comb.sem, 1)
                dve.wait_ge(*self.comb.at(1))

            def accumulate(self, dve, k):
                dve.wait_ge(*self.y_mm.at(k + 1))
                e, h = ROUNDS[k]
                if k >= 1:
                    dve.wait_ge(*self.acc.at(4 * k))
                for j in range(4):
                    t = 4 * h + j
                    dve.scalar_tensor_tensor(XR[:, t, :], PS[:, 4 + k % 2, P * j:P * (j + 1)], comb[:, 0, t, e:e + 1],
                                             (X if e == 0 else XR)[:, t, :], ALU.mult, ALU.add).then_inc(self.acc.sem, 1)

            def dve(self, dve):
                self.largest(dve)
                self.x_low(dve, 1)
                for n in range(EARLY, LAST):
                    self.step_dve(dve, n)
                self.statistics(dve, 1)

            def statistics(self, dve, h):
                norm = self.norm
                dve.wait_ge(*self.acc.at(4 * (len(ROUNDS) - 1 + h)))
                for i in range(4 * h, 4 * h + 4):
                    dve.bn_stats(st8[:, i, :], XR[:, i, :]).then_inc(norm.st.sem, 1)
                for i in range(4 * h, 4 * h + 4):
                    dve.wait_ge(*norm.st.at(i + 1))
                    dve.bn_aggr(mv8[:, i, :], st8[:, i, :]).then_inc(norm.mv.sem, 1)

            def apply(self, dve, h):
                norm = self.norm
                dve.wait_ge(*norm.rstd.at(4 * h + 4))
                for i in range(4 * h, 4 * h + 4):
                    dve.tensor_scalar(X[:, i, :], XR[:, i, :], mv8[:, i, 0:1], rstd8[:, i, :],
                                      ALU.subtract, ALU.mult).then_inc(norm.ln.sem, 1)

            def pool(self, pool):
                pool.wait_ge(*self.w_mm.at(3 * EXPERTS))
                pool.memset(VW, 0.0).then_inc(s_wz, 1)
                norm = self.norm
                for h in range(2):
                    t = slice(4 * h, 4 * h + 4)
                    pool.wait_ge(*norm.mv.at(4 * h + 4))
                    pool.tensor_scalar(ve8[:, t, :], mv8[:, t, 1:2], LN_EPS, None, ALU.add).then_inc(norm.ve.sem, 4)
                    pool.wait_ge(*norm.ve.at(4 * h + 4))
                    pool.tensor_tensor(rstd8[:, t, :], ve8[:, t, :], bc(half[:, :], 1, 4), ALU.pow).then_inc(norm.rstd.sem, 4)

        a0 = Narrow("self0", 0, XT, rope=True, bias=0, row=0, next_row=1)
        a0.res, a0.input = Mark("first_residual_made"), None
        a1 = Narrow("cross0", 4, CT, bias=1, fill=0, row=1)
        a1.res, a1.input = a0.norm.xr, a0.norm
        moe = Experts(a1.norm)
        wide = Wide("wide")
        wide.input = moe.norm
        a2 = Narrow("cross1", 8, CT, fill=1, next_row=2)
        a2.input = wide.norm
        fc = Ternary("ternary")
        fc.res, fc.input = a2.norm.xr, a2.norm
        pre, post = stream_of(a0, a1), stream_of(wide, a2, fc)
        NB = 6

        DRAIN = len(pre)

        FIRST = {18: ([], [0]), 19: ([1], []), 20: ([2], []), 21: ([3], [4])}
        EARLY = 5

        def first_steps(j, late, prepare, step, eng):
            if j == 18 and not late:
                prepare(eng, 0)
            if j in FIRST:
                for n in FIRST[j][late]:
                    step(eng, n)

        def pre_pe(pe, j, late):
            if j == 1 and late:
                later.pe(pe)
            if j == 2 and not late:
                later.done(pe)
            if j in (2, 3) and late:
                weights.pe(pe, [j - 2])
            if j == 4 and late:
                weights.done(pe)
            if j == DRAIN and not late:
                for s in pre[-1].stage.qk_read(NT - 1):
                    pe.wait_ge(*s)
            if not late and j - DRAIN in (0, 1, 2):
                for g in (2 * (j - DRAIN), 2 * (j - DRAIN) + 1):
                    moe.weights_pe(pe, g)
            first_steps(j, late, lambda pe, h: None, moe.step_pe, pe)

        def pre_act(act, j, late):
            if j == 1 and late:
                later.copies(act, 0)
            if j in (2, 3) and late:
                weights.copies(act, 0, [j - 2])
            if not late and j - DRAIN in (0, 1, 2):
                for g in (2 * (j - DRAIN), 2 * (j - DRAIN) + 1):
                    moe.weights_act(act, g)
            first_steps(j, late, moe.x_high, moe.step_act, act)

        def masks(dve):
            dve.wait_ge(s_m, 16 * 5)
            dve.tensor_scalar(mk[:, :, :], mki[:, :, :], 0.0, 1.0, ALU.is_equal, ALU.subtract).then_inc(s_mk0, 1)
            dve.wait_ge(s_mk0, 1)
            dve.tensor_scalar(mk[:, :, :], mk[:, :, :], -1.0, None, ALU.mult).then_inc(s_mk0, 1)
            dve.tensor_scalar(mrb[:, :, :], mri[:, :, :], 0.0, None, ALU.is_equal).then_inc(s_mk, 1)
            dve.wait_ge(s_mk0, 2)

        def pre_dve(dve, j, late):
            if j == 1 and late:
                later.copies(dve, 1)
            if j in (2, 3) and late:
                weights.copies(dve, 1, [j - 2])
            if j == 2 and not late:
                masks(dve)
            if not late and j - DRAIN in (0, 1, 2):
                for g in (2 * (j - DRAIN), 2 * (j - DRAIN) + 1):
                    moe.weights_dve(dve, g)
            first_steps(j, late, moe.x_low, moe.step_dve, dve)

        def post_pe(pe, j, late):
            if j == 1 and late:
                moe.x_pe(pe, 1)

        def post_act(act, j, late):
            if j == 1 and late:
                moe.x_act(act, 1)

        def post_dve(dve, j, late):
            if j == 1 and late:
                moe.apply(dve, 1)

        def load_biases(eng, b):
            w, o = (("L0_attn_b", "p"), ("L0_xattn_b", "o"))[b]
            for n, x in enumerate("qk"):
                for r in range(2):
                    eng.dma_start(qkb[64 * r:64 * r + 64, b, n, :], A[w + x].rearrange("(g p) -> p g", g=2),
                                  allow_slow_non_contiguous=True).then_inc(s_b[b], 16)
            eng.dma_start(bvc[:, b:b + 1], A[w + "v"].rearrange("(p o) -> p o", o=1)).then_inc(s_b[b], 16)
            eng.dma_start(rowb[:, b, :], A[w + o].partition_broadcast(P)).then_inc(s_b[b], 16)

        @block.sync
        def _(sp):
            def load(dst, src, s, **k):
                sp.dma_start(dst, src, **k).then_inc(s, 16)

            x = A["x"].rearrange("(t b) s f -> (b s) t f", b=2)
            load(X[:, 0:4, :], x[:, 0:4], s_x[0])
            for n in range(4):
                load(RAWW[:, n, :], A[WNAMES[n]], s_w0)
            load_biases(sp, 0)
            load(X[:, 4:8, :], x[:, 4:8], s_x[1])
            load(CTXR[:, :, :], A["ctx_1024"].rearrange("(t b) s f -> (b s) t f", b=2), s_ctx)
            load(gw[:, :], A["L0_ffn_gate_w"], s_ctx)
            for n in range(4, 12):
                load(RAWW[:, n, :], A[WNAMES[n]], s_w)
            load_biases(sp, 1)
            mask = A["mask_Bx1x1xS2_ik0"].rearrange("(t b) x y k -> b (x y) t k", b=2)
            for b in range(2):
                load(mki[64 * b:64 * b + 64, :, :], mask[b].to_broadcast([64, NT, SEQ]), s_m)
            for j in range(3):
                load(mri[2 * j:2 * j + 2, :, :], mask[:, 0], s_m)

            def load_expert(e):
                for w, name in enumerate(("L0_ffn_wg", "L0_ffn_wu")):
                    load(RAW[:, e % 4, w].rearrange("p (c h) -> p c h", c=CH),
                         A[name][e].rearrange("(c i) h -> i c h", c=CH), s_raw[e % 4])
                load(RAW[:, e % 4, 2], A["L0_ffn_wd"][e], s_raw[e % 4])

            for e in range(4):
                load_expert(e)
            load(WQKV[:, :], A["L1_attn_W_qkv"], s_wide)
            load(WOUT[:, :, :], A["L1_attn_W_out"].rearrange("(u p) f -> p u f", p=P), s_wide)
            load(FCW[:, 0], A["L1_ffn_W_fc"].rearrange("(c i) f -> i c f", c=CH), s_fc)
            load(FCW[:, 1].rearrange("p c f -> p (c f)"), A["L1_ffn_W_proj"], s_fc)
            for n, name in enumerate(("L1_ffn_ln_w", "L1_ffn_ln_b")):
                load(lnwb[:, n, :], A[name].rearrange("(c p) -> p c", c=CH), s_fc, allow_slow_non_contiguous=True)
            for e in range(4, EXPERTS):
                sp.wait_ge(*moe.w_mm.at(3 * (e - 3)))
                load_expert(e)
            out_v = out.rearrange("(t b) s f -> (b s) t f", b=2)
            for i in range(NT):
                sp.wait_ge(*fc.norm.ln.at(i + 1))
                sp.dma_start(out_v[:, i, :], X[:, i, :]).then_inc(s_out, 16)
            sp.wait_ge(s_out, 16 * NT)

        @block.gpsimd
        def _(pool):
            pool.memset(half[:, :], -0.5).then_inc(s_half, 1)
            pool.memset(QS[:, :, :, :], 0.0).then_inc(s_z, 1)
            pool.memset(VB[:, :, :, :, :, :], 0.0).then_inc(s_z, 1)
            pool.wait_ge(s_cst, 16)
            pool.wait_ge(s_z, 2)
            for b in range(2):
                for a in range(2):
                    pool.tensor_copy(VB[:, :, :, b, a, DH], bc(cst[:, C_HALF + a:C_HALF + a + 1], 1, 3).to_broadcast([P, 3, PAIRS]))\
                        .then_inc(s_z, 1)
            pool.wait_ge(s_half, 1)
            for h in range(2):
                pool.wait_ge(s_x[h], 16)
            pool.wait_ge(s_b[0], 16 * NB)
            stream_pool(pool, pre)
            moe.pool(pool)
            stream_pool(pool, post)

        @block.scalar
        def _(act):
            act.dma_start(ident, table[:, C_ID:C_ID + P]).then_inc(s_id, 16)
            act.dma_start(cst[:, C_ID + P:], table[:, C_ID + P:]).then_inc(s_cst, 16)
            first.copies(act, 0)
            act.wait_ge(s_b[0], 16 * NB)
            stream_act(act, pre, pre_act)
            moe.act(act)
            act.wait_ge(s_fc, 64)
            stream_act(act, post, post_act)

        @block.vector
        def _(dve):
            dve.wait_ge(s_id, 16)
            dve.wait_ge(s_cst, 16)
            dve.tensor_copy(idb[:, :], ident).then_inc(s_bf, 1)
            dve.tensor_copy(caus[:, :], cst[:, C_CAUSAL:C_CAUSAL + SEQ]).then_inc(s_bf, 1)
            dve.wait_ge(s_bf, 2)
            dve.tensor_copy(fills[:, :, :], cst[0:6, C_FILL0:C_FILL0 + 2 * P].rearrange("p (l q) -> p l q", l=2))\
               .then_inc(s_bfc, 1)
            first.copies(dve, 1)
            stream_dve(dve, pre, pre_dve)
            moe.dve(dve)
            stream_dve(dve, post, post_dve)

        @block.tensor
        def _(pe):
            first.pe(pe)
            first.done(pe)
            pe.wait_ge(s_bfc, 1)
            stream_pe(pe, pre, pre_pe)
            moe.pe(pe)
            stream_pe(pe, post, post_pe)


def kernel(**inputs):
    import concourse.bacc as _bacc
    from concourse.bass_utils import run_bass_kernel_spmd as _run

    nc = _bacc.Bacc("TRN2", target_bir_lowering=False, num_devices=1)
    arrays, args = {}, {}
    for name in inputs:
        a = np.ascontiguousarray(inputs[name])
        arrays[f"in_{name}_dram"] = a
        args[name] = nc.dram_tensor(f"in_{name}_dram", a.shape, mybir.dt.from_np(a.dtype), kind="ExternalInput").ap()
    out = nc.dram_tensor("out_0_dram", (BATCH, SEQ, P), F32, kind="ExternalOutput").ap()
    decoder_kernel(nc, args, out)
    r = _run(nc, [arrays], core_ids=[0])
    return r.results[0]["out_0_dram"]
```
